# Optimizing a Trainium2 kernel written in Bass

```python
import numpy as np
import jax
import jax.numpy as jnp

def _softmax(x, axis=-1):
    return jax.nn.softmax(x, axis=axis)

def _gelu(x):
    return jax.nn.gelu(x, approximate=True)

def _silu(x):
    return jax.nn.silu(x)

def _sigmoid(x):
    return jax.nn.sigmoid(x)

def _layernorm(x, axis=-1, eps=1e-05):
    m = jnp.mean(x, axis=axis, keepdims=True)
    v = jnp.var(x, axis=axis, keepdims=True)
    return (x - m) / jnp.sqrt(v + eps)

def _scatter_add(tgt, idx, src, axis=0):
    return tgt.at[idx].add(src)

def _segment_sum(src, seg, n):
    return jax.ops.segment_sum(src, seg, n)
kernel_name = 'mk_xattn_ffn_d2_seqx_r8_4470fd'

def setup_inputs(seed: int=0):
    np.random.seed(seed)
    _w = jnp.asarray

    def _rec_inputs():
        import jax
        import jax.numpy as jnp
        _rk = jax.random.key(seed)
        x = 7.22e-05 + 1 * jax.random.normal(jax.random.fold_in(_rk, 1), (8, 100, 256), jnp.float32)
        _lenS = 100 - jax.random.randint(jax.random.fold_in(_rk, 7), (8,), 0, max(1, 100 // 4) + 1, jnp.int32)
        _lenS2 = 1444 - jax.random.randint(jax.random.fold_in(_rk, 8), (8,), 0, max(1, 1444 // 4) + 1, jnp.int32)
        _ctx_512P = jax.random.normal(jax.random.fold_in(_rk, 11), (8, 16, 64), jnp.float32)
        _ctx_512c = jax.random.dirichlet(jax.random.fold_in(_rk, 511), 0.3 * jnp.ones((16,), jnp.float32), (8, 1444))
        _ctx_512t = jnp.einsum('bsk,bkd->bsd', _ctx_512c, _ctx_512P)
        _ctx_512t = _ctx_512t * jax.lax.rsqrt(jnp.mean(jnp.square(_ctx_512t)) + 1e-12) * 0.953939
        ctx_512 = -0.000514642 + 1.00011 * (_ctx_512t + 0.3 * jax.random.normal(jax.random.fold_in(_rk, 611), (8, 1444, 64), jnp.float32))
        return (x, ctx_512)
    x, ctx_512 = _rec_inputs()

    def _L0_xattn_setup():
        import jax, jax.numpy as jnp
        import numpy as np
        B, S, H, NH, L = (2, 256, 256, 16, 64)
        HD = H // NH
        key = jax.random.key(seed)
        k1, k2, k3, k4, k5 = jax.random.split(key, 5)
        scale = 0.02
        return {'q': jax.random.normal(k1, (B, S, H), dtype=jnp.float32), 'latent_kv': jax.random.normal(k2, (B, S, L), dtype=jnp.float32), 'Wq': jax.random.normal(k3, (H, H), dtype=jnp.float32) * scale, 'Wkv_expand': jax.random.normal(k4, (2 * H, L), dtype=jnp.float32) * scale, 'Wout': jax.random.normal(k5, (H, H), dtype=jnp.float32) * scale}
    _L0_xattn_all = _L0_xattn_setup()
    _L0_xattn_in = {k: v for k, v in _L0_xattn_all.items() if k in ('Wq', 'Wkv_expand', 'Wout')}
    del _L0_xattn_all

    def _L0_ffn_setup():
        import jax, jax.numpy as jnp
        import numpy as np
        E, H, I = (8, 256, 512)
        TOP_K = 1
        B, S = (1, 256)
        key = jax.random.key(seed)
        ks = jax.random.split(key, 7)
        std = 0.02
        return {'hidden_states': jax.random.normal(ks[0], (B, S, H), dtype=jnp.float32), 'router_w': jax.random.normal(ks[1], (E, H), dtype=jnp.float32) * std, 'gate_up_proj': jax.random.normal(ks[2], (E, H, 2 * I), dtype=jnp.float32) * std, 'down_proj': jax.random.normal(ks[3], (E, I, H), dtype=jnp.float32) * std, 'shared_gate_w': jax.random.normal(ks[4], (H, I), dtype=jnp.float32) * std, 'shared_up_w': jax.random.normal(ks[5], (H, I), dtype=jnp.float32) * std, 'shared_down_w': jax.random.normal(ks[6], (I, H), dtype=jnp.float32) * std}
    _L0_ffn_all = _L0_ffn_setup()
    _L0_ffn_in = {k: v for k, v in _L0_ffn_all.items() if k in ('router_w', 'gate_up_proj', 'down_proj', 'shared_gate_w', 'shared_up_w', 'shared_down_w')}
    del _L0_ffn_all

    def _L1_xattn_setup():
        import jax, jax.numpy as jnp
        import numpy as np
        B, S, L = (2, 128, 128)
        DIM_Q, H, K, D_C, D_CQ, R = (256, 16, 128, 64, 192, 64)

        def _rope_tables(length, dim):
            inv = 1.0 / 10000.0 ** (jnp.arange(0, dim, 2, dtype=jnp.float32) / dim)
            f = jnp.arange(length, dtype=jnp.float32)[:, None] * inv[None, :]
            sin = jnp.repeat(jnp.sin(f), 2, axis=-1)
            cos = jnp.repeat(jnp.cos(f), 2, axis=-1)
            return (sin, cos)

        def _rotate_half(x):
            half = x.shape[-1] // 2
            return jnp.concatenate([-x[..., half:], x[..., :half]], axis=-1)

        def _apply_rope(x, sin, cos):
            return x * cos + _rotate_half(x) * sin
        key = jax.random.key(seed)
        ks = jax.random.split(key, 8)
        return {'hidden_q': jax.random.normal(ks[0], (B, S, DIM_Q), jnp.float32), 'kv_c': jax.random.normal(ks[1], (B, L, D_C), jnp.float32), 'Wq': jax.random.normal(ks[2], (H * K, DIM_Q), jnp.float32) / np.sqrt(DIM_Q).astype(np.float32), 'w_kc_q': jax.random.normal(ks[3], (H, K, D_CQ), jnp.float32) / np.sqrt(K).astype(np.float32), 'w_kc_kv': jax.random.normal(ks[4], (H, K, D_C), jnp.float32) / np.sqrt(K).astype(np.float32), 'W_qr': jax.random.normal(ks[5], (H, D_CQ, R), jnp.float32) / np.float32(np.sqrt(D_CQ) * np.sqrt(R)), 'W_kr': jax.random.normal(ks[6], (H, D_C, R), jnp.float32) / np.sqrt(D_C).astype(np.float32), 'Wo': jax.random.normal(ks[7], (DIM_Q, H * K), jnp.float32) / np.sqrt(H * K).astype(np.float32)}
    _L1_xattn_all = _L1_xattn_setup()
    _L1_xattn_in = {k: v for k, v in _L1_xattn_all.items() if k in ('Wq', 'w_kc_q', 'w_kc_kv', 'W_qr', 'W_kr', 'Wo')}
    del _L1_xattn_all

    def _L1_ffn_setup():
        import jax, jax.numpy as jnp
        import numpy as np
        EPS = 1e-05
        RMS_EPS = 1e-06

        def activation_quant(x, num_bits=8):
            qn = -2 ** (num_bits - 1)
            qp = 2 ** (num_bits - 1) - 1
            xf = x.astype(jnp.float32)
            s = qp / jnp.clip(jnp.max(jnp.abs(xf), axis=-1, keepdims=True), EPS, None)
            return (jnp.clip(jnp.round(xf * s), qn, qp) / s).astype(x.dtype)

        def weight_quant(w):
            wf = w.astype(jnp.float32)
            s = 1.0 / jnp.clip(jnp.mean(jnp.abs(wf)), EPS, None)
            return (jnp.clip(jnp.round(wf * s), -1.0, 1.0) / s).astype(w.dtype)

        def bit_linear(x, w):
            qx = x + jax.lax.stop_gradient(activation_quant(x) - x)
            qw = w + jax.lax.stop_gradient(weight_quant(w) - w)
            return jnp.einsum('bsh,oh->bso', qx, qw)

        def rms_norm(x, weight, eps=RMS_EPS):
            xf = x.astype(jnp.float32)
            var = jnp.mean(xf * xf, axis=-1, keepdims=True)
            return weight * (xf * jax.lax.rsqrt(var + eps)).astype(x.dtype)
        key = jax.random.key(seed)
        k1, k2, k3, k4 = jax.random.split(key, 4)
        B, S, H, I = (2, 256, 256, 1024)
        scale = 1.0 / np.sqrt(H)
        return {'x': jax.random.normal(k1, (B, S, H), dtype=jnp.float32), 'w_gate': jax.random.normal(k2, (I, H), dtype=jnp.float32) * scale, 'w_up': jax.random.normal(k3, (I, H), dtype=jnp.float32) * scale, 'w_down': jax.random.normal(k4, (H, I), dtype=jnp.float32) * (1.0 / np.sqrt(I)), 'ln_weight': jnp.ones((I,), dtype=jnp.float32)}
    _L1_ffn_all = _L1_ffn_setup()
    _L1_ffn_in = {k: v for k, v in _L1_ffn_all.items() if k in ('w_gate', 'w_up', 'w_down', 'ln_weight')}
    del _L1_ffn_all
    return {'x': x, 'ctx_512': ctx_512, 'L0_xattn_Wq': _L0_xattn_in['Wq'], 'L0_xattn_Wkv_expand': _L0_xattn_in['Wkv_expand'], 'L0_xattn_Wout': _L0_xattn_in['Wout'], 'L0_ffn_router_w': _L0_ffn_in['router_w'], 'L0_ffn_gate_up_proj': _L0_ffn_in['gate_up_proj'], 'L0_ffn_down_proj': _L0_ffn_in['down_proj'], 'L0_ffn_shared_gate_w': _L0_ffn_in['shared_gate_w'], 'L0_ffn_shared_up_w': _L0_ffn_in['shared_up_w'], 'L0_ffn_shared_down_w': _L0_ffn_in['shared_down_w'], 'L1_xattn_Wq': _L1_xattn_in['Wq'], 'L1_xattn_w_kc_q': _L1_xattn_in['w_kc_q'], 'L1_xattn_w_kc_kv': _L1_xattn_in['w_kc_kv'], 'L1_xattn_W_qr': _L1_xattn_in['W_qr'], 'L1_xattn_W_kr': _L1_xattn_in['W_kr'], 'L1_xattn_Wo': _L1_xattn_in['Wo'], 'L1_ffn_w_gate': _L1_ffn_in['w_gate'], 'L1_ffn_w_up': _L1_ffn_in['w_up'], 'L1_ffn_w_down': _L1_ffn_in['w_down'], 'L1_ffn_ln_weight': _L1_ffn_in['ln_weight']}

def reference(x, ctx_512, L0_xattn_Wq, L0_xattn_Wkv_expand, L0_xattn_Wout, L0_ffn_router_w, L0_ffn_gate_up_proj, L0_ffn_down_proj, L0_ffn_shared_gate_w, L0_ffn_shared_up_w, L0_ffn_shared_down_w, L1_xattn_Wq, L1_xattn_w_kc_q, L1_xattn_w_kc_kv, L1_xattn_W_qr, L1_xattn_W_kr, L1_xattn_Wo, L1_ffn_w_gate, L1_ffn_w_up, L1_ffn_w_down, L1_ffn_ln_weight):
    import jax
    import jax.numpy as jnp

    def _L0_xattn_ref(q, latent_kv, Wq, Wkv_expand, Wout):
        import jax, jax.numpy as jnp
        import numpy as np
        B, S, H, NH, L = (2, 256, 256, 16, 64)
        HD = H // NH
        b, sq, _ = q.shape
        sk = latent_kv.shape[1]
        qp = q @ Wq.T
        kv = latent_kv @ Wkv_expand.T
        k, v = jnp.split(kv, 2, axis=-1)
        qh = qp.reshape(b, sq, NH, HD).transpose(0, 2, 1, 3)
        kh = k.reshape(b, sk, NH, HD).transpose(0, 2, 1, 3)
        vh = v.reshape(b, sk, NH, HD).transpose(0, 2, 1, 3)
        inv_sqrt_d = 1.0 / jnp.sqrt(jnp.float32(HD))
        scores = jnp.einsum('bhqd,bhkd->bhqk', qh, kh) * inv_sqrt_d
        causal = jnp.tril(jnp.ones((sq, sk), dtype=bool))
        scores = jnp.where(causal, scores, jnp.finfo(scores.dtype).min)
        attn = jax.nn.softmax(scores, axis=-1)
        out = jnp.einsum('bhqk,bhkd->bhqd', attn, vh)
        out = out.transpose(0, 2, 1, 3).reshape(b, sq, H)
        return out @ Wout.T

    def _L0_ffn_ref(hidden_states, router_w, gate_up_proj, down_proj, shared_gate_w, shared_up_w, shared_down_w):
        import jax, jax.numpy as jnp
        import numpy as np
        E, H, I = (8, 256, 512)
        TOP_K = 1
        B, S = (1, 256)
        orig_shape = hidden_states.shape
        x = hidden_states.reshape(-1, H)
        T = x.shape[0]
        logits = x @ router_w.T
        top_vals, top_idx = jax.lax.top_k(logits, TOP_K)
        scores = jnp.full_like(logits, -jnp.inf)
        scores = scores.at[jnp.arange(T)[:, None], top_idx].set(top_vals)
        scores = jax.nn.sigmoid(scores.astype(jnp.float32)).astype(logits.dtype)
        xr = x[None, :, :] * scores.T[:, :, None]
        gate_up = jnp.einsum('eth,ehf->etf', xr, gate_up_proj)
        gate, up = jnp.split(gate_up, 2, axis=-1)
        routed = jnp.einsum('etf,efh->eth', up * jax.nn.silu(gate), down_proj)
        routed_sum = routed.sum(axis=0)
        shared = jax.nn.silu(x @ shared_gate_w) * (x @ shared_up_w) @ shared_down_w
        return (shared + routed_sum).reshape(orig_shape)

    def _L1_xattn_ref(hidden_q, kv_c, Wq, w_kc_q, w_kc_kv, W_qr, W_kr, Wo):
        import jax, jax.numpy as jnp
        import numpy as np
        B, S, L = (2, 128, 128)
        DIM_Q, H, K, D_C, D_CQ, R = (256, 16, 128, 64, 192, 64)

        def _rope_tables(length, dim):
            inv = 1.0 / 10000.0 ** (jnp.arange(0, dim, 2, dtype=jnp.float32) / dim)
            f = jnp.arange(length, dtype=jnp.float32)[:, None] * inv[None, :]
            sin = jnp.repeat(jnp.sin(f), 2, axis=-1)
            cos = jnp.repeat(jnp.cos(f), 2, axis=-1)
            return (sin, cos)

        def _rotate_half(x):
            half = x.shape[-1] // 2
            return jnp.concatenate([-x[..., half:], x[..., :half]], axis=-1)

        def _apply_rope(x, sin, cos):
            return x * cos + _rotate_half(x) * sin
        Bv, Sv, _ = hidden_q.shape
        _, Lv, _ = kv_c.shape
        q_hk = (hidden_q @ Wq.T).reshape(Bv, Sv, H, K)
        q_big = jnp.einsum('bshk,hkq->bshq', q_hk, w_kc_q)
        sin_q, cos_q = _rope_tables(Sv, D_CQ)
        q_big = _apply_rope(q_big, sin_q[None, :, None, :], cos_q[None, :, None, :])
        sin_k, cos_k = _rope_tables(Lv, D_C)
        kv_r = _apply_rope(kv_c, sin_k[None], cos_k[None])
        q_r = jnp.einsum('bshq,hqr->bhsr', q_big, W_qr)
        k_r = jnp.einsum('bld,hdr->bhlr', kv_r, W_kr)
        scores = jnp.einsum('bhsr,bhlr->bhsl', q_r, k_r)
        attn = jax.nn.softmax(scores, axis=-1)
        ctx_c = jnp.einsum('bhsl,bld->bhsd', attn, kv_r)
        ctx_lat = jnp.einsum('bhsd,hkd->bhsk', ctx_c, w_kc_kv)
        ctx = ctx_lat.transpose(0, 2, 1, 3).reshape(Bv, Sv, H * K)
        return ctx @ Wo.T

    def _L1_ffn_ref(x, w_gate, w_up, w_down, ln_weight):
        import jax, jax.numpy as jnp
        import numpy as np
        EPS = 1e-05
        RMS_EPS = 1e-06

        def activation_quant(x, num_bits=8):
            qn = -2 ** (num_bits - 1)
            qp = 2 ** (num_bits - 1) - 1
            xf = x.astype(jnp.float32)
            s = qp / jnp.clip(jnp.max(jnp.abs(xf), axis=-1, keepdims=True), EPS, None)
            return (jnp.clip(jnp.round(xf * s), qn, qp) / s).astype(x.dtype)

        def weight_quant(w):
            wf = w.astype(jnp.float32)
            s = 1.0 / jnp.clip(jnp.mean(jnp.abs(wf)), EPS, None)
            return (jnp.clip(jnp.round(wf * s), -1.0, 1.0) / s).astype(w.dtype)

        def bit_linear(x, w):
            qx = x + jax.lax.stop_gradient(activation_quant(x) - x)
            qw = w + jax.lax.stop_gradient(weight_quant(w) - w)
            return jnp.einsum('bsh,oh->bso', qx, qw)

        def rms_norm(x, weight, eps=RMS_EPS):
            xf = x.astype(jnp.float32)
            var = jnp.mean(xf * xf, axis=-1, keepdims=True)
            return weight * (xf * jax.lax.rsqrt(var + eps)).astype(x.dtype)
        h = jax.nn.silu(bit_linear(x, w_gate)) * bit_linear(x, w_up)
        h = rms_norm(h, ln_weight)
        return bit_linear(h, w_down)
    x = x + _L0_xattn_ref(_layernorm(x, axis=-1), ctx_512, L0_xattn_Wq, L0_xattn_Wkv_expand, L0_xattn_Wout)
    x = x + _L0_ffn_ref(_layernorm(x, axis=-1), L0_ffn_router_w, L0_ffn_gate_up_proj, L0_ffn_down_proj, L0_ffn_shared_gate_w, L0_ffn_shared_up_w, L0_ffn_shared_down_w)
    x = x + _L1_xattn_ref(_layernorm(x, axis=-1), ctx_512, L1_xattn_Wq, L1_xattn_w_kc_q, L1_xattn_w_kc_kv, L1_xattn_W_qr, L1_xattn_W_kr, L1_xattn_Wo)
    x = x + _L1_ffn_ref(_layernorm(x, axis=-1), L1_ffn_w_gate, L1_ffn_w_up, L1_ffn_w_down, L1_ffn_ln_weight)
    return x

_drawn_inputs = setup_inputs


def setup_inputs(seed=0):
    import zlib

    import numpy as np

    out = dict(_drawn_inputs(seed))
    spreads = {'L1_ffn_ln_weight': (1.0, 0.2)}
    factors = {'L0_xattn_Wq': 7.172,
     'L0_ffn_router_w': 3.408,
     'L0_ffn_gate_up_proj': 3.253,
     'L0_ffn_down_proj': 3.253}
    for name, (base, spread) in spreads.items():
        noise = np.random.default_rng([zlib.crc32(name.encode()), seed]).standard_normal(out[name].shape)
        drawn = base * np.exp(spread * noise) if base else spread * noise
        out[name] = jnp.asarray(drawn.astype(out[name].dtype))
    for name, factor in factors.items():
        out[name] = (out[name] * factor).astype(out[name].dtype)
    return out
```

```python
from contextlib import ExitStack

import concourse.bass as bass
from concourse import mybir

F32 = mybir.dt.float32
F32R = mybir.dt.float32r
BF16 = mybir.dt.bfloat16
ALU = mybir.AluOpType
ACT = mybir.ActivationFunctionType
AX = mybir.AxisListType

B, S, D = 8, 100, 256
T = B * S
HT = T // 2
DC = D // 128
LC, CD = 1444, 64
NH, HD = 16, 16
HS = 32
HG = 4
NG = NH // HG
NE, FI = 8, 512
FM = FI // 128
QK, QB, RD = 128, 192, 64
KT = 12
KP = -(-LC // KT)
KL = LC - (KP - 1) * KT
GH = NH // 2
GQ = GH * S
MT = -(-NH * S // 128)
MN = 482
MSTART = (0, 481, 962)
F1 = 1024
FC = F1 // 128
SLOTS = NG * KT
SPREAD_AT = 6
LAG = 2
LN_EPS, RMS_EPS, Q_EPS, Q_MAX = 1e-5, 1e-6, 1e-5, 127.0
ROUND = 12582912.0
MASKED = -1e30

ITEMS = (NE + 1) * FM * 2
EBUF = 3
M_SLOT = [(i * (SLOTS - 1)) // (MT - 1) for i in range(MT)]
HQ_SLOT, DOWN_SLOT = 22, 28
PT_BUF = 4
KV_BUF = 3


def key_rows(t):
    return KP if t < KL else KP - 1


def key_start(t):
    return t * KP if t <= KL else KL * KP + (t - KL) * (KP - 1)


def m_rows(i):
    return min(128, NH * S - 128 * i)


def build(nc, x, ctx_in, wq0, wkv0, wout0, router, gate_up, down, sh_gate, sh_up, sh_down,
          wq1, kcq, kckv, wqr, wkr, wo1, fg, fu, fd, lnw, rope_q, rope_kc, rope_ks, out):
    with ExitStack() as ctx:
        def sem(name):
            return ctx.enter_context(nc.semaphore(name))

        total = 212544
        slab_at = -(-nc.sbuf_base // 64) * 64
        ctx.enter_context(nc.sbuf_tensor("slab", [128, total // 4 + 16], F32))
        cursor = [0]

        def size_of(shape, dt):
            n = 2 if dt == BF16 else 4
            for d in shape[1:]:
                n *= d
            return -(-n // 32) * 32

        def place(name, shape, dt=F32):
            at = cursor[0]
            cursor[0] += size_of(shape, dt)
            assert cursor[0] <= total, (name, cursor[0])
            return nc.alloc_sbuf_tensor_at(name, shape, dt, offset=slab_at + at)

        x_sb = place("x_sb", [S, B, D])
        ident = place("ident", [128, 128])
        ident_bf = place("ident_bf", [128, 128], BF16)
        mhalf = place("mhalf", [128, B])
        wqb = place("wqb", [128, DC, NH, QB])
        amat = place("amat", [128, NH, 3, CD])
        bmat = place("bmat", [128, GH, D])
        ropeq = place("ropeq", [128, 4, S])
        wgT = place("wgT", [128, DC, F1], BF16)
        wuT = place("wuT", [128, DC, F1], BF16)
        wdT = place("wdT", [128, FC, D], BF16)
        wmean = place("wmean", [128, 3])
        wcol = place("wcol", [128, 3])
        wsum = place("wsum", [128, 3])
        winv = place("winv", [128, 3])
        stats = place("stats", [S, B, 6])
        mv = place("mv", [S, B, 2])
        veps = place("veps", [S, B])
        rstd = place("rstd", [S, B])
        top = place("top", [S, B])
        gatev = place("gatev", [S, B])
        pick = place("pick", [S, B])
        eq = place("eq", [S, B, NE])
        cand = place("cand", [S, B, NE])
        score = place("score", [S, B, NE])
        order = place("order", [S, NE])
        mx0 = [place(f"mx0_{i}", [S, NH]) for i in range(2)]
        rec0 = place("rec0", [S, NH])
        ones = place("ones", [128, CD])
        stats4 = place("stats4", [S, 6])
        mv4 = place("mv4", [S, 2])
        veps4 = place("veps4", [S, 1])
        rstd4 = place("rstd4", [S, 1])
        qsc = place("qsc", [S, 8])
        ssq = place("ssq", [S, 2])
        vh = place("vh", [S, 1])
        rstdh = place("rstdh", [S, 1])
        after_fixed = cursor[0]

        wkr_n = place("wkr_n", [CD, NH, RD])
        wqr_n = place("wqr_n", [QB // 2, 2 * NH, RD])
        lxyz = [place(f"lxyz{i}", [RD, 2, 3, 128]) for i in range(2)]
        wkrT = place("wkrT", [RD, NH, CD])
        kckv_n = place("kckv_n", [QK, NH, CD])
        wo_n = place("wo_n", [128, DC, NH * QK])
        woT = [place(f"woT{i}", [QK, 2, D]) for i in range(2)]
        end_1 = cursor[0]
        cursor[0] = after_fixed
        wq1_n = place("wq1_n", [QK, NH, D])
        kcq_n = place("kcq_n", [QK, NH, QB])
        fw = place("fw", [128, 2 * F1])
        fq = [place(f"fq{i}", [128, 2 * F1], BF16) for i in range(3)]
        end_2 = cursor[0]
        cursor[0] = after_fixed
        kv = [place(f"kv{i}", [KP, KT, CD + 1]) for i in range(KV_BUF)]
        craw = [place(f"craw{i}", [KP, KT, CD]) for i in range(2)]
        ropekc = place("ropekc", [KP, KT, CD])
        ropeks = place("ropeks", [KP, KT, CD])
        kcos = place("kcos", [KP, KT, CD])
        ksin = place("ksin", [KP, KT, CD])
        ctu = place("ctu", [128, GQ])
        ct = place("ct", [128, GQ])
        lnw_b = place("lnw_b", [S, F1])
        end_3 = cursor[0]
        after_stage = max(end_1, end_2, end_3)

        cursor[0] = after_stage
        xnT = place("xnT", [128, DC, T])
        xn = place("xn", [S, B, D])
        wqT = place("wqT", [128, DC, NG, 128])
        wkT = place("wkT", [CD, NG, 128])
        wvT = place("wvT", [CD, D])
        woutT = place("woutT", [128, DC, D])
        routerT = place("routerT", [128, DC, NE])
        ctx0T = place("ctx0T", [CD, T])
        qT = place("qT", [128, NG, T])
        kT = place("kT", [128, NG, T])
        vaug = place("vaug", [S, B, NH, HD + 1])
        sm = [place(f"sm{i}", [S, NH, S]) for i in range(2)]
        turned_once = cursor[0]
        wq_n = place("wq_n", [128, DC, D])
        wout_n = place("wout_n", [128, DC, D])
        router_n = place("router_n", [NE, D])
        cursor[0] = turned_once
        pT = place("pT", [S, NH, S])
        mask = place("mask", [S, S])
        turned_once = cursor[0]
        wkv_n = place("wkv_n", [128, 4, CD])
        ctx0 = place("ctx0", [S, B, CD])
        cursor[0] = turned_once
        oT = place("oT", [128, DC, S])
        ao = place("ao", [S, D])
        cursor[0] = after_stage + size_of([128, DC, T], F32)
        xr = [place(f"xr{i}", [128, DC, T]) for i in range(2)]
        scB = place("scB", [128, NE, T])
        scT = place("scT", [NE, T])
        egu = [place(f"egu{i}", [128, DC, 2 * FI]) for i in range(EBUF)]
        edn = [place(f"edn{i}", [128, FM, D]) for i in range(EBUF)]
        sg = [place(f"sg{i}", [128, HT]) for i in range(2)]
        hT = [place(f"hT{i}", [128, HT]) for i in range(3)]
        cursor[0] = after_stage + 3 * size_of([128, DC, T], F32)
        yT = place("yT", [128, DC, T])
        cursor[0] = after_stage
        khl = [place(f"khl{i}", [128, LC], F32R) for i in range(2)]
        kh1 = [place(f"kh1{i}", [CD + 1, LC], F32R) for i in range(2)]
        qh = [place(f"qh{i}", [128, NH * S], F32R) for i in range(2)]
        ql = [place(f"ql{i}", [CD + 1, NH * S], F32R) for i in range(2)]
        xyz = [place(f"xyz{i}", [128, 3, HG, S]) for i in range(2)]
        pt = [place(f"pt{i}", [KP, HT]) for i in range(PT_BUF)]
        xn3 = place("xn3", [S, D])
        x3T = place("x3T", [128, DC, S])
        nmx = [place(f"nmx{i}", [128, MT]) for i in range(2)]
        nmr = [place(f"nmr{i}", [MT, 128], F32R) for i in range(2)]
        xn4 = place("xn4", [S, D])
        xq = place("xq", [S, D], BF16)
        xqT = place("xqT", [128, DC, S], BF16)
        sg1 = place("sg1", [S, F1])
        h1 = place("h1", [S, F1])
        hq = place("hq", [S, F1], BF16)
        hqT = place("hqT", [128, FC, S], BF16)
        y = [place(f"y{i}", [S, D]) for i in range(2)]
        rec1 = [place(f"rec1{i}", [CD + 1, HT]) for i in range(2)]

        ps = ctx.enter_context(nc.psum_tensor("ps", [128, 8, 512], F32))

        ld_x, ld_ctx0, ld_w0, ld_router = sem("ld_x"), sem("ld_ctx0"), sem("ld_w0"), sem("ld_router")
        ld_st1, ld_st2, ld_wo, ld_const = sem("ld_st1"), sem("ld_st2"), sem("ld_wo"), sem("ld_const")
        ld_f = [sem(f"ld_f{i}") for i in range(3)]
        ld_e = [sem(f"ld_e{i}") for i in range(EBUF)]
        ld_craw = [sem(f"ld_craw{i}") for i in range(2)]
        tails_set = sem("tails_set")
        ld_rk, ld_lnw = sem("ld_rk"), sem("ld_lnw")
        set_up, pool_step = sem("set_up"), sem("pool_step")
        dve_step = sem("dve_step")
        var_ready, rstd_ready, xn_ready = sem("var_ready"), sem("rstd_ready"), sem("xn_ready")
        w_turned, w_kept = sem("w_turned"), sem("w_kept")
        proj_done, proj_kept_a, proj_kept_v = sem("proj_done"), sem("proj_kept_a"), sem("proj_kept_v")
        st_turned, st_kept, st_product, st_product_kept = (
            sem("st_turned"), sem("st_kept"), sem("st_product"), sem("st_product_kept"))
        qb_product, qb_kept_a, qb_kept_v = sem("qb_product"), sem("qb_kept_a"), sem("qb_kept_v")
        w_abs, w_mean, w_scaled, w_quant = sem("w_abs"), sem("w_mean"), sem("w_scaled"), sem("w_quant")
        fq_turned, fq_kept = sem("fq_turned"), sem("fq_kept")
        s0_done, s0_masked, s0_max, s0_shifted, s0_exp = (
            sem("s0_done"), sem("s0_masked"), sem("s0_max"), sem("s0_shifted"), sem("s0_exp"))
        p0_turned, p0_kept_a, p0_kept_v = sem("p0_turned"), sem("p0_kept_a"), sem("p0_kept_v")
        pv0_done, ao_ready, o0_turned, o0_kept, out0_done, x1_ready = (
            sem("pv0_done"), sem("ao_ready"), sem("o0_turned"), sem("o0_kept"), sem("out0_done"), sem("x1_ready"))
        var2_ready, rstd2_ready, xn2_ready, xn2_turned, xn2_kept = (
            sem("var2_ready"), sem("rstd2_ready"), sem("xn2_ready"), sem("xn2_turned"), sem("xn2_kept"))
        logits_done, top_ready, gate_ready, score_ready = (
            sem("logits_done"), sem("top_ready"), sem("gate_ready"), sem("score_ready"))
        sc_turned, sc_kept, sc_spread, sc_spread_kept = (
            sem("sc_turned"), sem("sc_kept"), sem("sc_spread"), sem("sc_spread_kept"))
        xr_ready, gu_done, silu_done, h_ready, down_done = (
            sem("xr_ready"), sem("gu_done"), sem("silu_done"), sem("h_ready"), sem("down_done"))
        y_kept_a, y_kept_v, y_turned, x2_ready = sem("y_kept_a"), sem("y_kept_v"), sem("y_turned"), sem("x2_ready")
        var3_ready, rstd3_ready, xn3_ready, x3_turned, x3_kept = (
            sem("var3_ready"), sem("rstd3_ready"), sem("xn3_ready"), sem("x3_turned"), sem("x3_kept"))
        craw_clear, kv_ready, k_turned, k_hi, k_lo = (
            sem("craw_clear"), sem("kv_ready"), sem("k_turned"), sem("k_hi"), sem("k_lo"))
        qbig_done, rope_done, q_done, q_hi, q_lo = (
            sem("qbig_done"), sem("rope_done"), sem("q_done"), sem("q_hi"), sem("q_lo"))
        m_done, m_reduced, m_turned, m_kept = sem("m_done"), sem("m_reduced"), sem("m_turned"), sem("m_kept")
        max_row = [sem(f"max_row{i}") for i in range(2)]
        s_done, p_ready, pv_done = sem("s_done"), sem("p_ready"), sem("pv_done")
        sum_inverted, c_kept, sum_spread, c_ready, o_done, x3_ready = (
            sem("sum_inverted"), sem("c_kept"), sem("sum_spread"), sem("c_ready"), sem("o_done"), sem("x3_ready"))
        var4_ready, rstd4_ready, xq_ready, xq_turned, xq_kept = (
            sem("var4_ready"), sem("rstd4_ready"), sem("xq_ready"), sem("xq_turned"), sem("xq_kept"))
        g_done, u_done, silu1_done, h1_part, h1_ready, h1_square = (
            sem("g_done"), sem("u_done"), sem("silu1_done"), sem("h1_part"), sem("h1_ready"), sem("h1_square"))
        varh_ready, rstdh_ready, hq_ready, hq_turned, hq_kept = (
            sem("varh_ready"), sem("rstdh_ready"), sem("hq_ready"), sem("hq_turned"), sem("hq_kept"))
        down1_done, y_ready = sem("down1_done"), sem("y_ready")
        y_stored = [sem(f"y_stored{i}") for i in range(2)]

        SET_UP = 7 + NE
        ST1 = 16
        block = ctx.enter_context(nc.Block())

        def load_expert(sp, e):
            g, d, s = egu[e % EBUF], edn[e % EBUF], ld_e[e % EBUF]
            if e == 0:
                sp.dma_start(g[:, :, 0:FI], sh_gate.rearrange("(c p) n -> p c n", p=128)).then_inc(s, 16)
                sp.dma_start(g[:, :, FI:2 * FI], sh_up.rearrange("(c p) n -> p c n", p=128)).then_inc(s, 16)
                sp.dma_start(d[:, :, :], sh_down.rearrange("(m p) n -> p m n", p=128)).then_inc(s, 16)
            else:
                sp.dma_start(g[:, :, :], gate_up[e - 1].rearrange("(c p) n -> p c n", p=128)).then_inc(s, 16)
                sp.dma_start(d[:, :, :], down[e - 1].rearrange("(m p) n -> p m n", p=128)).then_inc(s, 16)

        def load_ternary(sp, i):
            if i:
                sp.wait_ge(w_scaled, i)
            dst = fw[:, :].rearrange("p (r n) -> p r n", r=2 if i == 2 else FC)
            sp.dma_start(dst, (fg, fu, fd)[i].rearrange("(r p) n -> p r n", p=128)).then_inc(ld_f[i], 16)

        def expert_loaded(e):
            return 32 * (e // EBUF + 1) + (16 if e % EBUF == 0 else 0)

        def load_keys(sp, b):
            if b >= 2:
                sp.wait_ge(kv_ready, b - 1)
            c = craw[b % 2]
            sp.dma_start(c[0:KP - 1, :, :], ctx_in[b, 0:(KP - 1) * KT, :].rearrange("(p t) d -> p t d", t=KT)).then_inc(ld_craw[b % 2], 16)
            sp.dma_start(c[KP - 1:KP, 0:KL, :], ctx_in[b, (KP - 1) * KT:LC, :].rearrange("(p t) d -> p t d", t=KL)).then_inc(ld_craw[b % 2], 16)

        def store_y(sp, b):
            sp.wait_ge(y_ready, b + 1)
            sp.dma_start(out[b], y[b % 2][:, :]).then_inc(y_stored[b % 2], 16)

        @block.sync
        def _(sp):
            sp.dma_start(x_sb[:, :, :], x.rearrange("b s d -> s b d")).then_inc(ld_x, 16)
            sp.dma_start(wq_n[:, :, :], wq0.rearrange("(r p) d -> p r d", p=128)).then_inc(ld_w0, 16)
            sp.dma_start(wkv_n[:, :, :], wkv0.rearrange("(r p) d -> p r d", p=128)).then_inc(ld_w0, 16)
            sp.dma_start(wout_n[:, :, :], wout0.rearrange("(r p) d -> p r d", p=128)).then_inc(ld_w0, 16)
            sp.dma_start(ctx0[:, :, :], ctx_in[:, 0:S, :].rearrange("b s d -> s b d")).then_inc(ld_ctx0, 16)
            sp.dma_start(router_n[:, :], router).then_inc(ld_router, 16)
            sp.dma_start(wkr_n[:, :, :], wkr.rearrange("h d r -> d h r")).then_inc(ld_st1, 16)
            sp.dma_start(wqr_n[:, :, :], wqr.rearrange("h (a q) r -> q (h a) r", a=2)).then_inc(ld_st1, 16)
            sp.dma_start(kckv_n[:, :, :], kckv.rearrange("h k d -> k h d")).then_inc(ld_wo, 16)
            sp.dma_start(wo_n[:, :, :], wo1.rearrange("(r p) k -> p r k", p=128)).then_inc(ld_wo, 16)
            sp.dma_start(ropeq[:, :, :], rope_q).then_inc(ld_const, 16)
            sp.wait_ge(st_product, ST1)
            sp.wait_ge(st_kept, ST1)
            sp.dma_start(wq1_n[:, :, :], wq1.rearrange("(h k) d -> k h d", k=QK)).then_inc(ld_st2, 16)
            sp.dma_start(kcq_n[:, :, :], kcq.rearrange("h k q -> k h q")).then_inc(ld_st2, 16)
            load_ternary(sp, 0)
            sp.wait_ge(out0_done, B)
            sp.wait_ge(o0_kept, B)
            sp.wait_ge(x1_ready, B)
            sp.wait_ge(xn2_turned, B)
            for e in range(EBUF):
                load_expert(sp, e)
            load_ternary(sp, 1)
            for e in range(EBUF, NE + 1):
                sp.wait_ge(down_done, 2 * FM * (e - EBUF + 1))
                load_expert(sp, e)
                if e == 5:
                    load_ternary(sp, 2)
            sp.wait_ge(qb_product, NH)
            sp.wait_ge(fq_turned, 6)
            sp.dma_start(ropekc[0:KP - 1, :, :], rope_kc[0:(KP - 1) * KT, :].rearrange("(p t) d -> p t d", t=KT)).then_inc(ld_rk, 16)
            sp.dma_start(ropeks[0:KP - 1, :, :], rope_ks[0:(KP - 1) * KT, :].rearrange("(p t) d -> p t d", t=KT)).then_inc(ld_rk, 16)
            sp.dma_start(lnw_b[:, :], lnw.rearrange("(a n) -> a n", a=1).to_broadcast([S, F1])).then_inc(ld_lnw, 16)
            sp.wait_ge(craw_clear, 2)
            sp.dma_start(ropekc[KP - 1:KP, 0:KL, :], rope_kc[(KP - 1) * KT:LC, :].rearrange("(p t) d -> p t d", t=KL)).then_inc(ld_rk, 16)
            sp.dma_start(ropeks[KP - 1:KP, 0:KL, :], rope_ks[(KP - 1) * KT:LC, :].rearrange("(p t) d -> p t d", t=KL)).then_inc(ld_rk, 16)
            load_keys(sp, 0)
            load_keys(sp, 1)
            for b in range(B):
                sp.wait_ge(m_kept, b + 1)
                if b >= 2:
                    sp.wait_ge(s_done, SLOTS * (b - 1))
                row = ql[b % 2][CD:CD + 1, :].bitcast(F32)
                for i0, n in ((0, MT - 1), (MT - 1, 1)):
                    w = m_rows(i0)
                    sp.dma_start(row[:, 128 * i0:128 * i0 + n * w].rearrange("a (i q) -> a i q", q=w),
                                 nmr[b % 2][i0:i0 + n, 0:w].bitcast(F32)).then_inc(max_row[b % 2], 16)
                if b + 2 < B:
                    load_keys(sp, b + 2)
                if b >= 2:
                    store_y(sp, b - 2)
            store_y(sp, B - 2)
            store_y(sp, B - 1)
            for i in range(2):
                sp.wait_ge(y_stored[i], 16 * B // 2)

        def rotate_keys(pool, step, b):
            c, k = craw[b % 2], kv[b % KV_BUF]
            h = CD // 2
            pool.wait_ge(ld_craw[b % 2], 32 * (b // 2 + 1))
            if b:
                pool.wait_ge(kv_ready, b)
            if b >= KV_BUF:
                pool.wait_ge(pv_done, SLOTS * (b - KV_BUF + 1))
            for rows, t0, t1 in ((KP, 0, KL), (KP - 1, KL, KT)):
                r, t = slice(0, rows), slice(t0, t1)
                nc.gpsimd.tensor_tensor(kcos[r, t, :], c[r, t, :], ropekc[r, t, :], ALU.mult)
                nc.gpsimd.tensor_tensor(ksin[r, t, 0:h], c[r, t, h:CD], ropeks[r, t, 0:h], ALU.mult)
                last = nc.gpsimd.tensor_tensor(ksin[r, t, h:CD], c[r, t, 0:h], ropeks[r, t, h:CD], ALU.mult)
            step(last)
            for rows, t0, t1 in ((KP, 0, KL), (KP - 1, KL, KT)):
                r, t = slice(0, rows), slice(t0, t1)
                last = nc.gpsimd.tensor_tensor(k[r, t, 0:CD], kcos[r, t, :], ksin[r, t, :], ALU.add)
            last.then_inc(kv_ready, 1)

        def norm_x4(pool, power, b):
            pool.wait_ge(var4_ready, b + 1)
            power(rstd4[:, :], veps4[:, :], S).then_inc(rstd4_ready, 1)

        def norm_h(pool, power, b):
            pool.wait_ge(varh_ready, b + 1)
            power(rstdh[:, :], vh[:, :], S).then_inc(rstdh_ready, 1)

        @block.gpsimd
        def _(pool):
            steps = [0]

            def step(ins):
                steps[0] += 1
                ins.then_inc(pool_step, 1)
                pool.wait_ge(pool_step, steps[0])

            def power(dst, src, rows):
                return nc.gpsimd.tensor_tensor(dst, src, mhalf[0:rows, 0:src.shape[1]], ALU.pow)

            step(nc.gpsimd.memset(ident[:, :], 0.0))
            step(nc.gpsimd.affine_select(out=ident[:, :], in_=ident[:, :], compare_op=ALU.not_equal, fill=1.0,
                                         base=0, pattern=[[-1, 128]], channel_multiplier=1))
            nc.gpsimd.tensor_copy(ident_bf[:, :], ident[:, :]).then_inc(set_up, 1)
            nc.gpsimd.memset(mhalf[:, :], -0.5).then_inc(set_up, 1)
            nc.gpsimd.memset(ones[:, :], 1.0).then_inc(set_up, 1)
            nc.gpsimd.memset(wqT[:, :, :, :], 0.0).then_inc(set_up, 1)
            nc.gpsimd.memset(wkT[:, :, :], 0.0).then_inc(set_up, 1)
            nc.gpsimd.memset(vaug[:, :, :, HD:HD + 1], 1.0).then_inc(set_up, 1)
            for e in range(NE):
                nc.gpsimd.memset(order[:, e:e + 1], float(NE - e)).then_inc(set_up, 1)
            step(nc.gpsimd.memset(mask[:, :], 0.0))
            nc.gpsimd.affine_select(out=mask[:, :], in_=mask[:, :], compare_op=ALU.is_ge, fill=MASKED,
                                    base=0, pattern=[[-1, S]], channel_multiplier=1).then_inc(set_up, 1)
            pool.wait_ge(set_up, SET_UP)
            pool.wait_ge(var_ready, 1)
            power(rstd[:, :], veps[:, :], S).then_inc(rstd_ready, 1)
            for i in range(B + 2):
                if i < B:
                    pool.wait_ge(s0_max, i + 1)
                    nc.gpsimd.tensor_tensor(sm[i % 2][:, :, :], sm[i % 2][:, :, :],
                                            mx0[i % 2][:, :].unsqueeze(2).to_broadcast([S, NH, S]),
                                            ALU.subtract).then_inc(s0_shifted, 1)
                if i >= 2:
                    b = i - 2
                    pool.wait_ge(var2_ready, b + 1)
                    power(rstd[:, b:b + 1], veps[:, b:b + 1], S).then_inc(rstd2_ready, 1)
            for i in range(3):
                pool.wait_ge(w_abs, i + 1)
                nc.gpsimd.partition_all_reduce(wsum[:, i:i + 1], wcol[:, i:i + 1], 128,
                                               bass.bass_isa.ReduceOp.add).then_inc(w_mean, 1)
                pool.wait_ge(w_quant, 2 * i + 1)
                step(nc.gpsimd.tensor_scalar(fw[:, :], fw[:, :], winv[:, i:i + 1], 1.0, ALU.mult, ALU.min))
                step(nc.gpsimd.tensor_scalar(fw[:, :], fw[:, :], -1.0, ROUND, ALU.max, ALU.add))
                nc.gpsimd.tensor_scalar(fq[i][:, :], fw[:, :], ROUND, None, ALU.subtract).then_inc(w_scaled, 1)
                pool.wait_ge(w_scaled, i + 1)
                pool.wait_ge(w_quant, 2 * i + 2)
            pool.wait_ge(var3_ready, 1)
            power(rstd[:, :], veps[:, :], S).then_inc(rstd3_ready, 1)
            pool.wait_ge(qb_product, NH)
            pool.wait_ge(fq_turned, 6)
            pool.wait_ge(ld_rk, 32)
            for i in range(KV_BUF):
                step(nc.gpsimd.memset(kv[i][:, :, CD:CD + 1], 1.0))
            for i in range(2):
                nc.gpsimd.memset(craw[i][:, :, :], 0.0).then_inc(craw_clear, 1)
                step(nc.gpsimd.memset(nmx[i][:, :], 0.0))
                nc.gpsimd.memset(kh1[i][CD:CD + 1, :].bitcast(F32), 1.0).then_inc(tails_set, 1)
                pool.wait_ge(tails_set, i + 1)
            pool.wait_ge(ld_rk, 64)
            rotate_keys(pool, step, 0)
            rotate_keys(pool, step, 1)
            for b in range(B + 1):
                if b:
                    norm_x4(pool, power, b - 1)
                if b + 2 < B:
                    rotate_keys(pool, step, b + 2)
                if b:
                    norm_h(pool, power, b - 1)

        @block.tensor
        def _(pe):
            mm, turn = nc.tensor.matmul, nc.tensor.transpose

            def job_bank(n):
                if n >= 4:
                    pe.wait_ge(w_kept, n - 3)
                return ps[:, 4 + n % 4, :]

            pe.wait_ge(set_up, SET_UP)
            pe.wait_ge(ld_w0, 48)
            for n, src in ((0, wq_n), (2, wout_n)):
                if n == 2:
                    o = job_bank(1)
                    for r in range(4):
                        last = turn(o[0:CD, 128 * r:128 * r + 128], wkv_n[:, r, :], ident[:, :])
                    last.then_inc(w_turned, 1)
                o = job_bank(n)
                for c in range(DC):
                    for r in range(DC):
                        last = turn(o[:, (DC * c + r) * 128:(DC * c + r + 1) * 128],
                                    src[:, r, 128 * c:128 * c + 128], ident[:, :])
                last.then_inc(w_turned, 1)
            pe.wait_ge(ld_ctx0, 16)
            for n in (3, 4):
                o = job_bank(n)
                for j in range(4):
                    last = turn(o[0:CD, S * j:S * j + S], ctx0[:, 4 * (n - 3) + j, :], ident[0:S, 0:S])
                last.then_inc(w_turned, 1)
            pe.wait_ge(ld_router, 16)
            o = job_bank(5)
            for c in range(DC):
                last = turn(o[:, NE * c:NE * c + NE], router_n[:, 128 * c:128 * c + 128], ident[0:NE, 0:NE])
            last.then_inc(w_turned, 1)
            for j in range(4):
                pe.wait_ge(xn_ready, 2 * j + 2)
                o = job_bank(6 + j)
                for c in range(DC):
                    for i in range(2):
                        last = turn(o[:, (2 * c + i) * S:(2 * c + i + 1) * S],
                                    xn[:, 2 * j + i, 128 * c:128 * c + 128], ident[0:S, 0:S])
                last.then_inc(w_turned, 1)

            job = 0

            def proj_bank():
                if job >= 4:
                    pe.wait_ge(proj_kept_v if job % 2 else proj_kept_a, (job - 4) // 2 + 1)
                return ps[:, job % 4, :]

            for n in range(2):
                pe.wait_ge(w_kept, 8 + 2 * n)
                for g in range(NG):
                    o = proj_bank()
                    for c in range(DC):
                        last = mm(o[:, 0:HT], wqT[:, c, g, :], xnT[:, c, HT * n:HT * n + HT], start=c == 0, stop=c == DC - 1)
                    last.then_inc(proj_done, 1)
                    job += 1
                    o = proj_bank()
                    mm(o[:, 0:HT], wkT[:, g, :], ctx0T[:, HT * n:HT * n + HT], start=True, stop=True).then_inc(proj_done, 1)
                    job += 1
            for b in range(B):
                o = proj_bank()
                mm(o[0:S, 0:D], ctx0T[:, S * b:S * b + S], wvT[:, :], start=True, stop=True).then_inc(proj_done, 1)
                job += 1

            pe.wait_ge(ld_st1, 32)
            pe.wait_ge(w_kept, 10)
            for j in range(2):
                for i in range(8):
                    last = turn(ps[0:RD, 4 + j, CD * i:CD * i + CD], wkr_n[:, 8 * j + i, :], ident[0:CD, 0:CD])
                last.then_inc(st_turned, 1)

            def stage_turn(i):
                pe.wait_ge(st_kept, i + 1 if i < 2 else i - 1 + 2)
                o = ps[:, 4 + i % 2, :]
                if i < 8:
                    for j in range(4):
                        last = turn(o[0:RD, 96 * j:96 * j + 96], wqr_n[:, 4 * i + j, :], ident[0:96, 0:96])
                else:
                    if i == 8:
                        pe.wait_ge(ld_wo, 32)
                    for a in range(2):
                        h = i - 8 + GH * a
                        for r in range(DC):
                            last = turn(o[:, (DC * a + r) * 128:(DC * a + r + 1) * 128],
                                        wo_n[:, r, QK * h:QK * h + QK], ident[:, :])
                last.then_inc(st_turned, 1)

            def stage_product(i):
                pe.wait_ge(st_kept, i + 3)
                if i >= 2:
                    pe.wait_ge(st_product_kept, i - 1)
                o = ps[:, 6 + i % 2, :]
                if i < 8:
                    for a in range(2):
                        for k in range(3):
                            last = mm(o[:, (3 * a + k) * CD:(3 * a + k + 1) * CD], lxyz[i % 2][:, a, k, :],
                                      wkrT[:, 2 * i + a, :], start=True, stop=True)
                else:
                    for a in range(2):
                        h = i - 8 + GH * a
                        last = mm(o[CD * a:CD * a + CD, 0:D], kckv_n[:, h, :], woT[i % 2][:, a, :], start=True, stop=True)
                last.then_inc(st_product, 1)

            stage_turn(0)
            for i in range(ST1):
                if i + 1 < ST1:
                    stage_turn(i + 1)
                stage_product(i)

            pe.wait_ge(proj_kept_a, 12)
            pe.wait_ge(proj_kept_v, 12)
            pe.wait_ge(st_product_kept, ST1)
            for step in range(B + 3):
                if step < B:
                    b = step
                    if b:
                        pe.wait_ge(s0_masked, b)
                    tok = slice(S * b, S * b + S)
                    for g in range(NG):
                        for i in range(HG):
                            p = slice(HS * i, HS * i + HS)
                            last = mm(ps[0:S, i, S * g:S * g + S], qT[p, g, tok], kT[p, g, tok], start=True, stop=True)
                    last.then_inc(s0_done, 1)
                if 1 <= step <= B:
                    b = step - 1
                    pe.wait_ge(s0_exp, b + 1)
                    for half in range(2):
                        if half == 1:
                            pe.wait_ge(p0_kept_a, b + 1)
                        elif b:
                            pe.wait_ge(p0_kept_v, b)
                        for j in range(8):
                            last = turn(ps[0:S, 4 + j // 4, S * (j % 4):S * (j % 4) + S],
                                        sm[b % 2][:, 8 * half + j, :], ident[0:S, 0:S])
                        last.then_inc(p0_turned, 1)
                    pe.wait_ge(p0_kept_v, b + 1)
                    if b:
                        pe.wait_ge(ao_ready, b)
                    for i in range(HG):
                        for g in range(NG):
                            h = HG * g + i
                            last = mm(ps[0:S, 6, (HD + 1) * h:(HD + 1) * (h + 1)], pT[:, NG * i + g, :],
                                      vaug[:, b, h, :], start=True, stop=True)
                    last.then_inc(pv0_done, 1)
                if 2 <= step <= B + 1:
                    b = step - 2
                    pe.wait_ge(ao_ready, b + 1)
                    if b:
                        pe.wait_ge(xn2_kept, b - 1) if b > 1 else None
                        pe.wait_ge(x1_ready, b)
                    for c in range(DC):
                        last = turn(ps[:, 7, S * c:S * c + S], ao[:, 128 * c:128 * c + 128], ident[0:S, 0:S])
                    last.then_inc(o0_turned, 1)
                    pe.wait_ge(o0_kept, b + 1)
                    for c in range(DC):
                        last = mm(ps[0:S, 7, D:2 * D], oT[:, c, :], woutT[:, c, :], start=c == 0, stop=c == DC - 1)
                    last.then_inc(out0_done, 1)
                if step >= 3:
                    b = step - 3
                    pe.wait_ge(xn2_ready, b + 1)
                    pe.wait_ge(x1_ready, min(b + 2, B))
                    for c in range(DC):
                        last = turn(ps[:, 7, S * c:S * c + S], xn[:, b, 128 * c:128 * c + 128], ident[0:S, 0:S])
                    last.then_inc(xn2_turned, 1)
                    if step < B + 2:
                        pe.wait_ge(xn2_kept, b + 1)

            pe.wait_ge(xn2_kept, B)
            for b in range(B):
                for c in range(DC):
                    last = mm(ps[0:S, 6, NE * b:NE * b + NE], xnT[:, c, S * b:S * b + S], routerT[:, c, :],
                              start=c == 0, stop=c == DC - 1)
            last.then_inc(logits_done, 1)
            pe.wait_ge(ld_st2, 32)
            for h in range(NH):
                if h >= 4:
                    pe.wait_ge(qb_kept_v if h % 2 else qb_kept_a, (h - 4) // 2 + 1)
                for c in range(DC):
                    last = mm(ps[:, h % 4, QB * c:QB * c + QB], wq1_n[:, h, 128 * c:128 * c + 128], kcq_n[:, h, :],
                              start=True, stop=True)
                last.then_inc(qb_product, 1)
            pe.wait_ge(score_ready, 1)
            for b in range(B):
                last = turn(ps[0:NE, 4 + b // 4, S * (b % 4):S * (b % 4) + S], score[:, b, :], ident[0:S, 0:S])
            last.then_inc(sc_turned, 1)
            pe.wait_ge(sc_kept, 1)
            for e in range(NE):
                if e >= 2:
                    pe.wait_ge(sc_spread_kept, e - 1)
                for n in range(2):
                    last = mm(ps[:, 4 + 2 * (e % 2) + n, 0:HT], ident[0:NE, e:e + 1].to_broadcast([NE, 128]),
                              scT[:, HT * n:HT * n + HT], start=True, stop=True)
                last.then_inc(sc_spread, 1)
            pe.wait_ge(sc_spread_kept, NE)
            pe.wait_ge(qb_kept_a, NH // 2)
            pe.wait_ge(qb_kept_v, NH // 2)

            for k in range(ITEMS + 1):
                if k < ITEMS:
                    e, m, n = k // (2 * FM), k // 2 % FM, k % 2
                    w, src = egu[e % EBUF], (xnT if e == 0 else xr[e % 2])
                    if k % (2 * FM) == 0:
                        pe.wait_ge(ld_e[e % EBUF], expert_loaded(e))
                        if e:
                            pe.wait_ge(xr_ready, e)
                    if k >= 2:
                        pe.wait_ge(h_ready, k - 1)
                    for a in range(2):
                        for c in range(DC):
                            last = mm(ps[:, 4 + 2 * a + n, 0:HT], w[:, c, FI * a + 128 * m:FI * a + 128 * m + 128],
                                      src[:, c, HT * n:HT * n + HT], start=c == 0, stop=c == DC - 1)
                    last.then_inc(gu_done, 1)
                if k:
                    j = k - 1
                    e, m, n = j // (2 * FM), j // 2 % FM, j % 2
                    pe.wait_ge(h_ready, j + 1)
                    for c in range(DC):
                        last = mm(ps[:, 2 * c + n, 0:HT], edn[e % EBUF][:, m, 128 * c:128 * c + 128], hT[j % 3][:, :],
                                  start=j < 2, stop=j >= ITEMS - 2)
                    last.then_inc(down_done, 1)
            pe.wait_ge(y_kept_a, 2)
            pe.wait_ge(y_kept_v, 2)
            for b in range(B):
                if b >= 4:
                    pe.wait_ge(x2_ready, b - 3)
                for c in range(DC):
                    last = turn(ps[0:S, 4 + b % 4, 128 * c:128 * c + 128], yT[:, c, S * b:S * b + S], ident[:, :])
                last.then_inc(y_turned, 1)
            for n in range(6):
                i, half = n // 2, n % 2
                pe.wait_ge(w_scaled, i + 1)
                if n >= 4:
                    pe.wait_ge(fq_kept, n - 3)
                o = ps[:, n % 4, :].bitcast(BF16)
                src = fq[i][:, :].rearrange("p (r n) -> p r n", r=2 if i == 2 else FC)
                for j in range(8):
                    if i < 2:
                        part = src[:, j, 128 * half:128 * half + 128]
                    else:
                        part = src[:, j % 2, 128 * (4 * half + j // 2):128 * (4 * half + j // 2) + 128]
                    last = turn(o[:, 128 * j:128 * j + 128], part, ident_bf[:, :])
                last.then_inc(fq_turned, 1)
            pe.wait_ge(fq_kept, 6)

            def turn_x3(b):
                pe.wait_ge(xn3_ready, b + 1)
                for c in range(DC):
                    last = turn(ps[:, 4, S * c:S * c + S], xn3[:, 128 * c:128 * c + 128], ident[0:S, 0:S])
                last.then_inc(x3_turned, 1)
                pe.wait_ge(x3_kept, b + 1)

            def q_big(b, g):
                if NG * b + g:
                    pe.wait_ge(rope_done, NG * b + g)
                for i in range(HG):
                    h = HG * g + i
                    for c in range(DC):
                        mm(ps[:, 4, S * i:S * i + S], wqb[:, c, h, 0:128], x3T[:, c, :], start=c == 0, stop=c == DC - 1)
                for i in range(HG):
                    h = HG * g + i
                    for c in range(DC):
                        last = mm(ps[0:CD, 5, S * i:S * i + S], wqb[:, c, h, 128:QB],
                                  x3T[:, c, :], start=c == 0, stop=c == DC - 1)
                last.then_inc(qbig_done, 1)

            def q_latent(b, g):
                k = NG * b + g
                pe.wait_ge(rope_done, k + 1)
                if k:
                    pe.wait_ge(q_lo, k)
                for i in range(HG):
                    h = HG * g + i
                    for j in range(3):
                        last = mm(ps[0:CD, 6, S * i:S * i + S], amat[:, h, j, :],
                                  xyz[k % 2][:, j, i, :], start=j == 0, stop=j == 2)
                last.then_inc(q_done, 1)

            def turn_keys(b, j):
                pe.wait_ge(kv_ready, b + 1)
                if 3 * b + j:
                    pe.wait_ge(k_lo, 3 * b + j)
                if j == 0 and b >= 2:
                    pe.wait_ge(c_ready, NG * (b - 1))
                for t in range(4 * j, 4 * j + 4):
                    at = key_start(t) - key_start(4 * j)
                    last = turn(ps[0:CD, 7, at:at + key_rows(t)], kv[b % KV_BUF][0:key_rows(t), t, 0:CD],
                                ident[0:key_rows(t), 0:key_rows(t)])
                last.then_inc(k_turned, 1)

            def q_and_keys(b, last_out):
                turn_x3(b)
                q_big(b, 0)
                if last_out:
                    spread_sums(NG * (b - 1) - 1)
                turn_keys(b, 0)
                if last_out:
                    attention_out(b - 2)
                for g in range(1, NG):
                    q_big(b, g)
                    q_latent(b, g - 1)
                    if g < 3:
                        turn_keys(b, g)
                q_latent(b, NG - 1)

            def max_tile(b, i):
                k = MT * b + i
                if i == 0:
                    pe.wait_ge(q_lo, NG * (b + 1))
                    pe.wait_ge(k_lo, 3 * (b + 1))
                if k:
                    pe.wait_ge(m_reduced, k)
                w = m_rows(i)
                for n in range(3):
                    last = mm(ps[0:w, 4 + n, 0:MN], qh[b % 2][:, 128 * i:128 * i + w],
                              khl[b % 2][:, MSTART[n]:MSTART[n] + MN], start=True, stop=True)
                last.then_inc(m_done, 1)

            def turn_max(b):
                pe.wait_ge(tails_set, 2)
                pe.wait_ge(m_reduced, MT * (b + 1))
                turn(ps[0:MT, 6, 0:128], nmx[b % 2][:, :], ident[:, :]).then_inc(m_turned, 1)
                pe.wait_ge(m_kept, b + 1)

            def scores(k):
                b, c, t = k // SLOTS, k // KT % NG, k % KT
                if k % SLOTS == 0:
                    pe.wait_ge(max_row[b % 2], 32 * (b // 2 + 1))
                if k >= 2:
                    pe.wait_ge(p_ready, k - 1)
                keys = slice(key_start(t), key_start(t) + key_rows(t))
                for lhs, rhs, first in ((khl[b % 2], qh[b % 2], True), (kh1[b % 2], ql[b % 2], False)):
                    last = mm(ps[0:key_rows(t), k % 2, 0:HT], lhs[:, keys], rhs[:, HT * c:HT * c + HT],
                              start=first, stop=not first)
                last.then_inc(s_done, 1)

            def values(k):
                b, t, q = k // SLOTS, k % KT, k // KT
                pe.wait_ge(p_ready, k + 1)
                if t == 0 and q >= 2:
                    pe.wait_ge(c_kept, q - 1)
                    pe.wait_ge(sum_inverted, q - 1)
                mm(ps[0:CD + 1, 2 + q % 2, 0:HT], kv[b % KV_BUF][0:key_rows(t), t, :],
                   pt[k % PT_BUF][0:key_rows(t), :], start=t == 0, stop=t == KT - 1).then_inc(pv_done, 1)

            def spread_sums(q):
                a = q % NG // 2
                pe.wait_ge(sum_inverted, q + 1)
                if q:
                    pe.wait_ge(c_ready, q)
                if q % NG == 0 and q // NG + 1 < B:
                    pe.wait_ge(k_lo, 3 * (q // NG + 2))
                mm(ps[CD * a:CD * a + CD, 7, 0:HT], ones[CD:CD + 1, :], rec1[q % 2][CD:CD + 1, :],
                   start=True, stop=True).then_inc(sum_spread, 1)

            def attention_out(b):
                pe.wait_ge(c_ready, NG * (b + 1))
                if b + 2 < B:
                    pe.wait_ge(q_lo, NG * (b + 2))
                for h in range(GH):
                    last = mm(ps[0:S, 6, 0:D], ct[:, S * h:S * h + S], bmat[:, h, :], start=h == 0, stop=h == GH - 1)
                last.then_inc(o_done, 1)
                pe.wait_ge(x3_ready, b + 1)

            def ffn_first(b):
                pe.wait_ge(xq_ready, b + 1)
                o = ps[:, 4, :].bitcast(BF16)
                for c in range(DC):
                    last = turn(o[:, S * c:S * c + S], xq[:, 128 * c:128 * c + 128], ident_bf[0:S, 0:S])
                last.then_inc(xq_turned, 1)
                pe.wait_ge(xq_kept, b + 1)
                for half in range(2):
                    for w, bank, s in ((wgT, 5 + half, g_done), (wuT, 4, u_done)):
                        if half and w is wuT:
                            pe.wait_ge(h1_part, 2 * b + 1)
                        for c in range(DC):
                            last = mm(ps[0:S, bank, :], xqT[:, c, :], w[:, c, 512 * half:512 * half + 512],
                                      start=c == 0, stop=c == DC - 1)
                        last.then_inc(s, 1)

            def turn_hq(b):
                pe.wait_ge(hq_ready, b + 1)
                o = ps[:, 4, :].bitcast(BF16)
                for f in range(FC):
                    last = turn(o[:, S * f:S * f + S], hq[:, 128 * f:128 * f + 128], ident_bf[0:S, 0:S])
                last.then_inc(hq_turned, 1)
                pe.wait_ge(hq_kept, b + 1)

            def ffn_down(b):
                for f in range(FC):
                    last = mm(ps[0:S, 5, 0:D], hqT[:, f, :], wdT[:, f, :], start=f == 0, stop=f == FC - 1)
                last.then_inc(down1_done, 1)
                pe.wait_ge(y_ready, b + 1)

            q_and_keys(0, False)
            pe.wait_ge(tails_set, 2)
            for i in range(MT):
                max_tile(0, i)
            turn_max(0)
            for b in range(B):
                if b + 1 < B:
                    q_and_keys(b + 1, b > 0)
                elif b:
                    spread_sums(NG * b - 1)
                    attention_out(b - 1)
                if b:
                    ffn_first(b - 1)
                for s in range(SLOTS + LAG):
                    k = SLOTS * b + s
                    if s < SLOTS:
                        scores(k)
                    if s >= LAG:
                        values(k - LAG)
                    if s > KT and s % KT == SPREAD_AT:
                        spread_sums(NG * b + s // KT - 1)
                    if b and s == HQ_SLOT:
                        if b + 1 < B:
                            pe.wait_ge(m_reduced, MT * (b + 1) + sum(x < s for x in M_SLOT))
                        turn_hq(b - 1)
                    if b and s == DOWN_SLOT:
                        if b + 1 < B:
                            pe.wait_ge(m_reduced, MT * (b + 1) + sum(x < s for x in M_SLOT))
                        ffn_down(b - 1)
                    if b + 1 < B and s in M_SLOT:
                        if s == 0 and b:
                            pe.wait_ge(h1_part, 2 * b)
                            pe.wait_ge(silu1_done, 2 * b)
                        max_tile(b + 1, M_SLOT.index(s))
                if b + 1 < B:
                    turn_max(b + 1)
            spread_sums(NG * B - 1)
            attention_out(B - 1)
            ffn_first(B - 1)
            turn_hq(B - 1)
            ffn_down(B - 1)

        @block.scalar
        def _(act):
            def keep(dst, src, **more):
                return nc.scalar.activation(dst, src, ACT.Copy, **more)

            act.wait_ge(set_up, SET_UP)
            for n in range(10):
                act.wait_ge(w_turned, n + 1)
                o = ps[:, 4 + n % 4, :]
                if n == 0:
                    last = keep(wqT[:, :, :, :].rearrange("p c g (i s) -> p (c g i) s", s=HS)[:, :, 0:HD],
                                o.rearrange("p (j d) -> p j d", d=HD))
                elif n == 1:
                    keep(wkT[:, :, :].rearrange("p g (i s) -> p (g i) s", s=HS)[:, :, 0:HD],
                         o[0:CD, 0:D].rearrange("p (j d) -> p j d", d=HD))
                    last = keep(wvT[:, :], o[0:CD, D:2 * D])
                elif n == 2:
                    last = keep(woutT[:, :, :].rearrange("p c n -> p (c n)"), o)
                elif n in (3, 4):
                    last = keep(ctx0T[:, HT * (n - 3):HT * (n - 2)], o[0:CD, 0:HT])
                elif n == 5:
                    last = keep(routerT[:, :, :].rearrange("p c e -> p (c e)"), o[:, 0:DC * NE])
                else:
                    j = n - 6
                    last = keep(xnT[:, :, 2 * S * j:2 * S * (j + 1)], o[:, 0:2 * DC * S].rearrange("p (c q) -> p c q", c=DC))
                last.then_inc(w_kept, 1)
            for job in range(0, 24, 2):
                act.wait_ge(proj_done, job + 1)
                o = ps[:, job % 4, :]
                if job < 16:
                    last = keep(qT[:, job // 2 % NG, HT * (job // 8):HT * (job // 8 + 1)], o[:, 0:HT])
                else:
                    last = keep(vaug[:, job - 16, :, 0:HD], o[0:S, 0:D].rearrange("p (h d) -> p h d", d=HD))
                last.then_inc(proj_kept_a, 1)
            for j in range(2):
                act.wait_ge(st_turned, j + 1)
                keep(wkrT[:, 8 * j:8 * j + 8, :].rearrange("p h d -> p (h d)"), ps[0:RD, 4 + j, :]).then_inc(st_kept, 1)
            for i in range(ST1):
                act.wait_ge(st_turned, i + 3)
                if i >= 2:
                    act.wait_ge(st_product, i - 1)
                o = ps[:, 4 + i % 2, :]
                if i < 8:
                    t = o[0:RD, 0:2 * QB].rearrange("p (a q) -> p a q", a=2)
                    l, h = lxyz[i % 2], QB // 2
                    keep(l[:, :, 0, :], t[:, :, 0:128])
                    keep(l[:, :, 1, 0:h], t[:, :, h:QB])
                    keep(l[:, :, 1, h:128], t[:, :, 0:128 - h])
                    keep(l[:, :, 2, 0:RD], t[:, :, 128:QB])
                    last = keep(l[:, :, 2, RD:128], t[:, :, 128 - h:QB - h])
                else:
                    last = keep(woT[i % 2][:, :, :].rearrange("p a n -> p (a n)"), o)
                last.then_inc(st_kept, 1)
            for step in range(B + 3):
                if 1 <= step <= B:
                    b = step - 1
                    act.wait_ge(p0_turned, 2 * b + 1)
                    if b:
                        act.wait_ge(pv0_done, b)
                    keep(pT[:, 0:8, :].rearrange("p (a j) q -> p a (j q)", a=2), ps[0:S, 4:6, 0:HT]).then_inc(p0_kept_a, 1)
                if step < B:
                    act.wait_ge(s0_shifted, step + 1)
                    nc.scalar.activation(sm[step % 2][:, :, :], sm[step % 2][:, :, :], ACT.Exp, scale=HD ** -0.5)\
                      .then_inc(s0_exp, 1)
                if 2 <= step <= B + 1:
                    act.wait_ge(o0_turned, step - 1)
                    keep(oT[:, :, :].rearrange("p c q -> p (c q)"), ps[:, 7, 0:DC * S]).then_inc(o0_kept, 1)
                if step >= 3:
                    b = step - 3
                    act.wait_ge(xn2_turned, b + 1)
                    keep(xnT[:, :, S * b:S * b + S], ps[:, 7, 0:DC * S].rearrange("p (c q) -> p c q", c=DC)).then_inc(xn2_kept, 1)
            act.wait_ge(top_ready, 1)
            nc.scalar.activation(gatev[:, :], top[:, :], ACT.Sigmoid).then_inc(gate_ready, 1)
            for h in range(0, NH, 2):
                act.wait_ge(qb_product, h + 1)
                keep(wqb[:, :, h, :], ps[:, h % 4, 0:DC * QB].rearrange("p (c q) -> p c q", c=DC)).then_inc(qb_kept_a, 1)
            for e in range(NE):
                act.wait_ge(sc_spread, e + 1)
                keep(scB[:, e, :].rearrange("p (n q) -> p n q", n=2), ps[:, 4 + 2 * (e % 2):6 + 2 * (e % 2), 0:HT])\
                    .then_inc(sc_spread_kept, 1)
            for k in range(ITEMS):
                act.wait_ge(gu_done, k + 1)
                if k >= 2:
                    act.wait_ge(h_ready, k - 1)
                nc.scalar.activation(sg[k % 2][:, :], ps[:, 4 + k % 2, 0:HT], ACT.Silu).then_inc(silu_done, 1)
            for n in range(2):
                act.wait_ge(down_done, ITEMS - 1 + n)
                keep(yT[:, 0, HT * n:HT * n + HT], ps[:, n, 0:HT]).then_inc(y_kept_a, 1)
            for n in range(6):
                i, half = n // 2, n % 2
                act.wait_ge(fq_turned, n + 1)
                o = ps[:, n % 4, :].bitcast(BF16)
                if i < 2:
                    last = keep((wgT, wuT)[i][:, half, :], o)
                else:
                    last = keep(wdT[:, 4 * half:4 * half + 4, :].rearrange("p f n -> p (f n)"), o)
                last.then_inc(fq_kept, 1)

            def keep_x3(b):
                act.wait_ge(x3_turned, b + 1)
                keep(x3T[:, :, :].rearrange("p c q -> p (c q)"), ps[:, 4, 0:DC * S]).then_inc(x3_kept, 1)

            def keep_q(b, g):
                k = NG * b + g
                act.wait_ge(q_done, k + 1)
                if g == 0 and b >= 2:
                    act.wait_ge(s_done, SLOTS * (b - 1))
                for p in (0, CD):
                    last = nc.scalar.activation(qh[b % 2][p:p + CD, HT * g:HT * g + HT], ps[0:CD, 6, 0:HT], ACT.Copy)
                last.then_inc(q_hi, 1)

            def keep_keys(b, j):
                act.wait_ge(k_turned, 3 * b + j + 1)
                if j == 0 and b >= 2:
                    act.wait_ge(s_done, SLOTS * (b - 1))
                k0 = key_start(4 * j)
                n = key_start(4 * j + 4) - k0
                keep(khl[b % 2][0:CD, k0:k0 + n], ps[0:CD, 7, 0:n])
                keep(kh1[b % 2][0:CD, k0:k0 + n], ps[0:CD, 7, 0:n]).then_inc(k_hi, 1)

            def q_and_keys(b, last_out):
                keep_x3(b)
                if last_out:
                    keep_context(NG * (b - 1) - 1)
                keep_keys(b, 0)
                for g in range(1, NG):
                    keep_q(b, g - 1)
                    if g < 3:
                        keep_keys(b, g)
                keep_q(b, NG - 1)

            def keep_max(b):
                act.wait_ge(m_turned, b + 1)
                if b >= 2:
                    act.wait_ge(max_row[b % 2], 32 * (b // 2))
                nc.scalar.activation(nmr[b % 2][:, :], ps[0:MT, 6, 0:128], ACT.Copy).then_inc(m_kept, 1)

            def keep_context(q):
                act.wait_ge(pv_done, KT * (q + 1))
                if q >= NG:
                    act.wait_ge(c_ready, q - NG + 1)
                a = q % NG // 2
                keep(ctu[CD * a:CD * a + CD, HT * (q % 2):HT * (q % 2) + HT], ps[0:CD, 2 + q % 2, 0:HT]).then_inc(c_kept, 1)

            def ffn_first(b):
                act.wait_ge(xq_turned, b + 1)
                o = ps[:, 4, :].bitcast(BF16)
                keep(xqT[:, :, :].rearrange("p c q -> p (c q)"), o[:, 0:DC * S]).then_inc(xq_kept, 1)
                for half in range(2):
                    act.wait_ge(g_done, 2 * b + half + 1)
                    if b and half == 0:
                        act.wait_ge(hq_ready, b)
                    nc.scalar.activation(sg1[:, 512 * half:512 * half + 512], ps[0:S, 5 + half, :], ACT.Silu,
                                         scale=qsc[:, 2:3]).then_inc(silu1_done, 1)
                act.wait_ge(h1_part, 2 * b + 2)
                nc.scalar.activation(sg1[:, :], h1[:, :], ACT.Square, accum_out=ssq[:, 0:1]).then_inc(h1_square, 1)

            def turn_hq(b):
                act.wait_ge(hq_turned, b + 1)
                o = ps[:, 4, :].bitcast(BF16)
                keep(hqT[:, :, :].rearrange("p f q -> p (f q)"), o[:, 0:FC * S]).then_inc(hq_kept, 1)

            q_and_keys(0, False)
            keep_max(0)
            for b in range(B):
                if b + 1 < B:
                    q_and_keys(b + 1, b > 0)
                elif b:
                    keep_context(NG * b - 1)
                if b:
                    ffn_first(b - 1)
                for s in range(SLOTS):
                    k = SLOTS * b + s
                    act.wait_ge(s_done, k + 1)
                    if k >= PT_BUF:
                        act.wait_ge(pv_done, k - PT_BUF + 1)
                    rows = key_rows(k % KT)
                    nc.scalar.activation(pt[k % PT_BUF][0:rows, :], ps[0:rows, k % 2, 0:HT], ACT.Exp).then_inc(p_ready, 1)
                    if s > KT and s % KT == LAG + 1:
                        keep_context(NG * b + s // KT - 1)
                    if b and s == HQ_SLOT:
                        turn_hq(b - 1)
                if b + 1 < B:
                    keep_max(b + 1)
            keep_context(NG * B - 1)
            ffn_first(B - 1)
            turn_hq(B - 1)

        @block.vector
        def _(dve):
            steps = [0]
            tt, ts, stt = nc.vector.tensor_tensor, nc.vector.tensor_scalar, nc.vector.scalar_tensor_tensor

            def step(ins):
                steps[0] += 1
                ins.then_inc(dve_step, 1)
                dve.wait_ge(dve_step, steps[0])

            dve.wait_ge(ld_x, 16)
            for b in range(B):
                last = nc.vector.bn_stats(stats[:, b, :], x_sb[:, b, :])
            step(last)
            for b in range(B):
                last = nc.vector.bn_aggr(mv[:, b, :], stats[:, b, :])
            step(last)
            dve.wait_ge(set_up, SET_UP)
            ts(veps[:, :], mv[:, :, 1], LN_EPS, None, ALU.add).then_inc(var_ready, 1)
            dve.wait_ge(rstd_ready, 1)
            for b in range(B):
                ts(xn[:, b, :], x_sb[:, b, :], mv[:, b, 0:1], rstd[:, b:b + 1], ALU.subtract, ALU.mult).then_inc(xn_ready, 1)
            for job in range(1, 24, 2):
                dve.wait_ge(proj_done, job + 1)
                o = ps[:, job % 4, :]
                if job < 16:
                    last = nc.vector.tensor_copy(kT[:, job // 2 % NG, HT * (job // 8):HT * (job // 8 + 1)], o[:, 0:HT])
                else:
                    last = nc.vector.tensor_copy(vaug[:, job - 16, :, 0:HD], o[0:S, 0:D].rearrange("p (h d) -> p h d", d=HD))
                last.then_inc(proj_kept_v, 1)
            for i in range(ST1):
                dve.wait_ge(st_product, i + 1)
                o = ps[:, 6 + i % 2, :]
                if i < 8:
                    last = nc.vector.tensor_copy(amat[:, 2 * i:2 * i + 2, :, :].rearrange("p a j d -> p (a j d)"), o[:, 0:6 * CD])
                else:
                    last = nc.vector.tensor_copy(bmat[:, i - 8, :], o[:, 0:D])
                last.then_inc(st_product_kept, 1)

            for s in range(B + 3):
                if s < B:
                    dve.wait_ge(s0_done, s + 1)
                    if s >= 2:
                        dve.wait_ge(p0_turned, 2 * (s - 1))
                    m = sm[s % 2]
                    tt(m[:, :, :].rearrange("p (i g) k -> p i g k", i=HG),
                       ps[0:S, 0:HG, 0:HT].rearrange("p i (g k) -> p i g k", g=NG),
                       mask[:, :].unsqueeze(1).unsqueeze(1).to_broadcast([S, HG, NG, S]), ALU.add).then_inc(s0_masked, 1)
                    dve.wait_ge(s0_masked, s + 1)
                    nc.vector.tensor_reduce(mx0[s % 2][:, :], m[:, :, :], AX.X, ALU.max).then_inc(s0_max, 1)
                if 1 <= s <= B:
                    b = s - 1
                    dve.wait_ge(p0_turned, 2 * b + 2)
                    if b:
                        dve.wait_ge(pv0_done, b)
                    nc.vector.tensor_copy(pT[:, 8:16, :].rearrange("p (a j) q -> p a (j q)", a=2), ps[0:S, 4:6, 0:HT])\
                      .then_inc(p0_kept_v, 1)
                    dve.wait_ge(pv0_done, b + 1)
                    if b:
                        dve.wait_ge(o0_turned, b)
                    o = ps[0:S, 6, 0:NH * (HD + 1)].rearrange("p (h d) -> p h d", d=HD + 1)
                    step(nc.vector.reciprocal(rec0[:, :], o[:, :, HD]))
                    tt(ao[:, :].rearrange("p (h d) -> p h d", d=HD), o[:, :, 0:HD],
                       rec0[:, :].unsqueeze(2).to_broadcast([S, NH, HD]), ALU.mult).then_inc(ao_ready, 1)
                if 2 <= s <= B + 1:
                    b = s - 2
                    dve.wait_ge(out0_done, b + 1)
                    tt(x_sb[:, b, :], x_sb[:, b, :], ps[0:S, 7, D:2 * D], ALU.add).then_inc(x1_ready, 1)
                    dve.wait_ge(x1_ready, b + 1)
                    step(nc.vector.bn_stats(stats[:, b, :], x_sb[:, b, :]))
                    step(nc.vector.bn_aggr(mv[:, b, :], stats[:, b, :]))
                    ts(veps[:, b:b + 1], mv[:, b, 1:2], LN_EPS, None, ALU.add).then_inc(var2_ready, 1)
                    dve.wait_ge(rstd2_ready, b + 1)
                    ts(xn[:, b, :], x_sb[:, b, :], mv[:, b, 0:1], rstd[:, b:b + 1], ALU.subtract, ALU.mult).then_inc(xn2_ready, 1)

            dve.wait_ge(logits_done, 1)
            lg = ps[0:S, 6, 0:B * NE].rearrange("p (b e) -> p b e", e=NE)

            def over(v):
                return v.unsqueeze(2).to_broadcast([S, B, NE])

            nc.vector.tensor_reduce(top[:, :], lg, AX.X, ALU.max).then_inc(top_ready, 1)
            dve.wait_ge(top_ready, 1)
            step(tt(eq[:, :, :], lg, over(top[:, :]), ALU.is_equal))
            step(tt(cand[:, :, :], eq[:, :, :], order[:, :].unsqueeze(1).to_broadcast([S, B, NE]), ALU.mult))
            step(nc.vector.tensor_reduce(pick[:, :], cand[:, :, :], AX.X, ALU.max))
            step(tt(eq[:, :, :], cand[:, :, :], over(pick[:, :]), ALU.is_equal))
            dve.wait_ge(gate_ready, 1)
            tt(score[:, :, :], eq[:, :, :], over(gatev[:, :]), ALU.mult).then_inc(score_ready, 1)
            for h in range(1, NH, 2):
                dve.wait_ge(qb_product, h + 1)
                nc.vector.tensor_copy(wqb[:, :, h, :], ps[:, h % 4, 0:DC * QB].rearrange("p (c q) -> p c q", c=DC))\
                  .then_inc(qb_kept_v, 1)
            dve.wait_ge(sc_turned, 1)
            nc.vector.tensor_copy(scT[:, :].rearrange("p (n q) -> p n q", n=2), ps[0:NE, 4:6, 0:HT]).then_inc(sc_kept, 1)

            def scaled_x(e):
                dve.wait_ge(sc_spread_kept, e)
                if e >= 3:
                    dve.wait_ge(gu_done, 2 * FM * (e - 1))
                tt(xr[e % 2][:, :, :], xnT[:, :, :], scB[:, e - 1, :].unsqueeze(1).to_broadcast([128, DC, T]),
                   ALU.mult).then_inc(xr_ready, 1)

            def weight_mean(i):
                dve.wait_ge(ld_f[i], 16)
                nc.vector.tensor_reduce(wcol[:, i:i + 1], fw[:, :], AX.X, ALU.add, apply_absolute_value=True)\
                  .then_inc(w_abs, 1)
                dve.wait_ge(w_mean, i + 1)
                step(ts(wmean[:, i:i + 1], wsum[:, i:i + 1], 1.0 / (F1 * D), Q_EPS, ALU.mult, ALU.max))
                nc.vector.reciprocal(winv[:, i:i + 1], wmean[:, i:i + 1]).then_inc(w_quant, 2)

            scaled_x(1)
            scaled_x(2)
            for k in range(ITEMS):
                e = k // (2 * FM)
                if k % (2 * FM) == 4 and 2 <= e < NE:
                    scaled_x(e + 1)
                if k in (3, 27, 51):
                    weight_mean(k // 24)
                dve.wait_ge(silu_done, k + 1)
                if k >= 3:
                    dve.wait_ge(down_done, k - 2)
                tt(hT[k % 3][:, :], sg[k % 2][:, :], ps[:, 6 + k % 2, 0:HT], ALU.mult).then_inc(h_ready, 1)
            for n in range(2):
                dve.wait_ge(down_done, ITEMS - 1 + n)
                nc.vector.tensor_copy(yT[:, 1, HT * n:HT * n + HT], ps[:, 2 + n, 0:HT]).then_inc(y_kept_v, 1)
            for b in range(B):
                dve.wait_ge(y_turned, b + 1)
                tt(x_sb[:, b, :], x_sb[:, b, :], ps[0:S, 4 + b % 4, 0:D], ALU.add).then_inc(x2_ready, 1)
            dve.wait_ge(x2_ready, B)
            for b in range(B):
                last = nc.vector.bn_stats(stats[:, b, :], x_sb[:, b, :])
            step(last)
            for b in range(B):
                last = nc.vector.bn_aggr(mv[:, b, :], stats[:, b, :])
            step(last)
            ts(veps[:, :], mv[:, :, 1], LN_EPS, None, ALU.add).then_inc(var3_ready, 1)
            dve.wait_ge(rstd3_ready, 1)

            def norm_x3(b):
                if b:
                    dve.wait_ge(x3_turned, b)
                ts(xn3[:, :], x_sb[:, b, :], mv[:, b, 0:1], rstd[:, b:b + 1], ALU.subtract, ALU.mult).then_inc(xn3_ready, 1)

            def rope(b, g):
                k = NG * b + g
                dve.wait_ge(qbig_done, k + 1)
                if k >= 2:
                    dve.wait_ge(q_done, k - 1)
                for j, (src, dst, bank) in enumerate((((0, 128), 0, 4), ((0, 128), 0, 4), ((0, CD), 0, 5), ((0, CD), CD, 5))):
                    n = src[1]
                    last = tt(xyz[k % 2][dst:dst + n, min(j, 2), :, :], ps[0:n, bank, 0:HT].rearrange("p (i q) -> p i q", i=HG),
                              ropeq[0:n, j, :].unsqueeze(1).to_broadcast([n, HG, S]), ALU.mult)
                last.then_inc(rope_done, 1)

            def low_q(b, g):
                k = NG * b + g
                cols = slice(HT * g, HT * g + HT)
                dve.wait_ge(q_hi, k + 1)
                tt(ql[b % 2][0:CD, cols], ps[0:CD, 6, 0:HT], qh[b % 2][0:CD, cols].bitcast(F32), ALU.subtract).then_inc(q_lo, 1)

            def low_keys(b, j):
                dve.wait_ge(k_hi, 3 * b + j + 1)
                k0 = key_start(4 * j)
                n = key_start(4 * j + 4) - k0
                tt(khl[b % 2][CD:128, k0:k0 + n], ps[0:CD, 7, 0:n], kh1[b % 2][0:CD, k0:k0 + n].bitcast(F32),
                   ALU.subtract).then_inc(k_lo, 1)

            def q_and_keys(b, last_out):
                if last_out:
                    invert_sums(NG * (b - 1) - 1)
                rope(b, 0)
                if last_out:
                    divide(NG * (b - 1) - 1)
                low_keys(b, 0)
                if last_out:
                    residual(b - 2)
                for g in range(1, NG):
                    rope(b, g)
                    low_q(b, g - 1)
                    if g < 3:
                        low_keys(b, g)
                low_q(b, NG - 1)

            def reduce_max(b, i):
                dve.wait_ge(m_done, MT * b + i + 1)
                w = m_rows(i)
                if i == 0 and b >= 2:
                    dve.wait_ge(m_turned, b - 1)
                nc.vector.tensor_reduce(nmx[b % 2][0:w, i:i + 1], ps[0:w, 4:7, 0:MN], AX.XY, ALU.max, negate=True)\
                  .then_inc(m_reduced, 1)

            def invert_sums(q):
                dve.wait_ge(pv_done, KT * (q + 1))
                if q >= 2:
                    dve.wait_ge(sum_spread, q - 1)
                nc.vector.reciprocal(rec1[q % 2][CD:CD + 1, :], ps[CD:CD + 1, 2 + q % 2, 0:HT]).then_inc(sum_inverted, 1)

            def divide(q):
                dve.wait_ge(sum_spread, q + 1)
                dve.wait_ge(c_kept, q + 1)
                if q >= NG and q % NG == 0:
                    dve.wait_ge(o_done, q // NG)
                a = q % NG // 2
                p, cols = slice(CD * a, CD * a + CD), slice(HT * (q % 2), HT * (q % 2) + HT)
                tt(ct[p, cols], ctu[p, cols], ps[p, 7, 0:HT], ALU.mult).then_inc(c_ready, 1)

            def residual(b):
                dve.wait_ge(o_done, b + 1)
                tt(x_sb[:, b, :], x_sb[:, b, :], ps[0:S, 6, 0:D], ALU.add).then_inc(x3_ready, 1)
                dve.wait_ge(x3_ready, b + 1)
                step(nc.vector.bn_stats(stats4[:, :], x_sb[:, b, :]))
                step(nc.vector.bn_aggr(mv4[:, :], stats4[:, :]))
                ts(veps4[:, :], mv4[:, 1:2], LN_EPS, None, ALU.add).then_inc(var4_ready, 1)

            def quantise(dst, src, high, ready):
                step(nc.vector.tensor_reduce(qsc[:, 4:5], src, AX.X, ALU.max, apply_absolute_value=True))
                step(ts(qsc[:, 4:5], qsc[:, 4:5], Q_EPS, None, ALU.max))
                step(nc.vector.reciprocal(qsc[:, 5:6], qsc[:, 4:5]))
                step(ts(qsc[:, 5:6], qsc[:, 5:6], Q_MAX, None, ALU.mult))
                ts(qsc[:, high:high + 1], qsc[:, 4:5], 1.0 / Q_MAX, None, ALU.mult)
                step(ts(src, src, qsc[:, 5:6], ROUND, ALU.mult, ALU.add))
                ts(dst, src, ROUND, Q_MAX, ALU.subtract, ALU.min).then_inc(ready, 1)

            def quantise_x(b):
                dve.wait_ge(rstd4_ready, b + 1)
                if b:
                    dve.wait_ge(xq_turned, b)
                    dve.wait_ge(silu1_done, 2 * b)
                step(ts(xn4[:, :], x_sb[:, b, :], mv4[:, 0:1], rstd4[:, 0:1], ALU.subtract, ALU.mult))
                step(nc.vector.tensor_reduce(qsc[:, 4:5], xn4[:, :], AX.X, ALU.max, apply_absolute_value=True))
                step(ts(qsc[:, 4:5], qsc[:, 4:5], Q_EPS, None, ALU.max))
                step(nc.vector.reciprocal(qsc[:, 5:6], qsc[:, 4:5]))
                step(ts(qsc[:, 5:6], qsc[:, 5:6], Q_MAX, None, ALU.mult))
                step(ts(xn4[:, :], xn4[:, :], qsc[:, 5:6], ROUND, ALU.mult, ALU.add))
                ts(qsc[:, 2:3], qsc[:, 4:5], 1.0 / Q_MAX, wmean[0:S, 0:1], ALU.mult, ALU.mult)
                ts(qsc[:, 3:4], qsc[:, 4:5], 1.0 / Q_MAX, wmean[0:S, 1:2], ALU.mult, ALU.mult)
                ts(xq[:, :], xn4[:, :], ROUND, Q_MAX, ALU.subtract, ALU.min).then_inc(xq_ready, 1)

            def hidden(b, half):
                dve.wait_ge(silu1_done, 2 * b + half + 1)
                dve.wait_ge(u_done, 2 * b + half + 1)
                cols = slice(512 * half, 512 * half + 512)
                stt(h1[:, cols], ps[0:S, 4, :], qsc[:, 3:4], sg1[:, cols], ALU.mult, ALU.mult).then_inc(h1_part, 1)

            def hidden_norm(b):
                dve.wait_ge(h1_square, b + 1)
                ts(vh[:, :], ssq[:, 0:1], 1.0 / F1, RMS_EPS, ALU.mult, ALU.add).then_inc(varh_ready, 1)

            def quantise_h(b):
                dve.wait_ge(rstdh_ready, b + 1)
                step(stt(h1[:, :], h1[:, :], rstdh[:, 0:1], lnw_b[:, :], ALU.mult, ALU.mult))
                step(nc.vector.tensor_reduce(qsc[:, 6:7], h1[:, :], AX.X, ALU.max, apply_absolute_value=True))
                step(ts(qsc[:, 6:7], qsc[:, 6:7], Q_EPS, None, ALU.max))
                step(nc.vector.reciprocal(qsc[:, 7:8], qsc[:, 6:7]))
                step(ts(qsc[:, 7:8], qsc[:, 7:8], Q_MAX, None, ALU.mult))
                step(ts(h1[:, :], h1[:, :], qsc[:, 7:8], ROUND, ALU.mult, ALU.add))
                step(ts(qsc[:, 0:1], qsc[:, 6:7], 1.0 / Q_MAX, wmean[0:S, 2:3], ALU.mult, ALU.mult))
                if b:
                    dve.wait_ge(hq_turned, b)
                ts(hq[:, :], h1[:, :], ROUND, Q_MAX, ALU.subtract, ALU.min).then_inc(hq_ready, 1)

            def result(b):
                dve.wait_ge(down1_done, b + 1)
                if b >= 2:
                    dve.wait_ge(y_stored[b % 2], 16 * (b // 2))
                stt(y[b % 2][:, :], ps[0:S, 5, 0:D], qsc[:, 0:1], x_sb[:, b, :], ALU.mult, ALU.add).then_inc(y_ready, 1)

            norm_x3(0)
            dve.wait_ge(ld_const, 16)
            dve.wait_ge(ld_lnw, 16)
            q_and_keys(0, False)
            norm_x3(1)
            dve.wait_ge(tails_set, 2)
            for i in range(MT):
                reduce_max(0, i)
            for b in range(B):
                if b + 1 < B:
                    q_and_keys(b + 1, b > 0)
                elif b:
                    invert_sums(NG * b - 1)
                    divide(NG * b - 1)
                    residual(b - 1)
                if b:
                    quantise_x(b - 1)
                    hidden(b - 1, 0)
                    hidden(b - 1, 1)
                    hidden_norm(b - 1)
                for s in range(SLOTS):
                    if s > KT and s % KT == LAG + 1:
                        invert_sums(NG * b + s // KT - 1)
                    if s > KT and s % KT == SPREAD_AT:
                        divide(NG * b + s // KT - 1)
                    if b + 1 < B and s in M_SLOT:
                        reduce_max(b + 1, M_SLOT.index(s))
                    if b and s == 5:
                        quantise_h(b - 1)
                    if b and s == DOWN_SLOT:
                        result(b - 1)
                    if s == DOWN_SLOT + 2 and b + 2 < B:
                        norm_x3(b + 2)
            invert_sums(NG * B - 1)
            divide(NG * B - 1)
            residual(B - 1)
            quantise_x(B - 1)
            hidden(B - 1, 0)
            hidden(B - 1, 1)
            hidden_norm(B - 1)
            quantise_h(B - 1)
            result(B - 1)


def rope_tables():
    import numpy as np

    def table(length, dim):
        inv = (np.float32(1.0) / np.power(np.float32(10000.0), np.arange(0, dim, 2, dtype=np.float32) / np.float32(dim))).astype(np.float32)
        f = np.arange(length, dtype=np.float32)[:, None] * inv[None, :]
        return np.repeat(np.sin(f), 2, axis=-1), np.repeat(np.cos(f), 2, axis=-1)

    half = QB // 2
    sin_q, cos_q = table(S, QB)
    turned = np.concatenate([sin_q[:, half:], -sin_q[:, :half]], axis=1)
    rope_q = np.zeros((128, 4, S), np.float32)
    rope_q[:, 0] = cos_q[:, 0:128].T
    rope_q[:, 1] = turned[:, 0:128].T
    rope_q[0:CD, 2] = cos_q[:, 128:QB].T
    rope_q[0:CD, 3] = turned[:, 128:QB].T
    sin_k, cos_k = table(LC, CD)
    sin_k = np.concatenate([-sin_k[:, :CD // 2], sin_k[:, CD // 2:]], axis=1)
    return rope_q, np.ascontiguousarray(cos_k), np.ascontiguousarray(sin_k)


_INS = ['x', 'ctx_512', 'L0_xattn_Wq', 'L0_xattn_Wkv_expand', 'L0_xattn_Wout', 'L0_ffn_router_w',
        'L0_ffn_gate_up_proj', 'L0_ffn_down_proj', 'L0_ffn_shared_gate_w', 'L0_ffn_shared_up_w',
        'L0_ffn_shared_down_w', 'L1_xattn_Wq', 'L1_xattn_w_kc_q', 'L1_xattn_w_kc_kv', 'L1_xattn_W_qr',
        'L1_xattn_W_kr', 'L1_xattn_Wo', 'L1_ffn_w_gate', 'L1_ffn_w_up', 'L1_ffn_w_down', 'L1_ffn_ln_weight']


def kernel(**inputs):
    import numpy as _np
    import concourse.bacc as _bacc
    from concourse import mybir as _mybir
    from concourse.bass_utils import run_bass_kernel_spmd as _run

    nc = _bacc.Bacc("TRN2", target_bir_lowering=False, num_devices=1)
    arrays, args = {}, []
    tables = dict(zip(("rope_q", "rope_kc", "rope_ks"), rope_tables()))
    for name in _INS + list(tables):
        a = _np.ascontiguousarray(tables[name] if name in tables else inputs[name])
        arrays[f"in_{name}_dram"] = a
        args.append(nc.dram_tensor(f"in_{name}_dram", a.shape, _mybir.dt.from_np(a.dtype), kind="ExternalInput").ap())
    args.append(nc.dram_tensor("out_0_dram", (B, S, D), F32, kind="ExternalOutput").ap())
    build(nc, *args)
    r = _run(nc, [arrays], core_ids=[0])
    return r.results[0]["out_0_dram"]
```

```python
from contextlib import ExitStack

import concourse.bass as bass
from concourse import mybir

F32 = mybir.dt.float32
F32R = mybir.dt.float32r
BF16 = mybir.dt.bfloat16
ALU = mybir.AluOpType
ACT = mybir.ActivationFunctionType
AX = mybir.AxisListType

B, S, D = 8, 100, 256
T = B * S
HT = T // 2
DC = D // 128
LC, CD = 1444, 64
NH, HD = 16, 16
HS = 32
HG = 4
NG = NH // HG
NE, FI = 8, 512
FM = FI // 128
QK, QB, RD = 128, 192, 64
KT = 12
KP = -(-LC // KT)
KL = LC - (KP - 1) * KT
GH = NH // 2
GQ = GH * S
MT = -(-NH * S // 128)
MN = 482
MSTART = (0, 481, 962)
F1 = 1024
FC = F1 // 128
SLOTS = NG * KT
LAG = 3
KEEP_AT, TURN_AT, SPREAD_AT = 3, 4, 5
X_SLOT = 0
KEY_SLOT = (7, 9, 11)
BIG_SLOT = (1, 4, 7, 10)
LAT_SLOT = (4, 7, 10, 12)
M_SLOT = (14, 18, 22, 24, 26, 28, 30, 32, 34, 36, 37, 39, 40)
MX_SLOT = 42
OUT_SLOT = 8
XQ_SLOT, GU_SLOT = 17, (19, 21)
SQ_SLOT, QH_SLOT = 22, (25, 27, 29, 31)
HQ_SLOT, DOWN_SLOT = 35, 38
X4_SLOT, H_NORM_SLOT = 12, 24
ROTATE_SLOT = (4, 5, 7, 8, 10, 11)
LN_EPS, RMS_EPS, Q_EPS, Q_MAX = 1e-5, 1e-6, 1e-5, 127.0
ROUND = 12582912.0
MASKED = -1e30

ITEMS = (NE + 1) * FM * 2
EBUF = 3
PT_BUF, PS_BUF = 3, 4
KV_BUF = 3


def key_rows(t):
    return KP if t < KL else KP - 1


def key_start(t):
    return t * KP if t <= KL else KL * KP + (t - KL) * (KP - 1)


def m_rows(i):
    return min(128, NH * S - 128 * i)


EARLY = 4


def max_bank(b, i):
    return 4 if b or (i > EARLY and i % 2) else 0


def groups_for(i):
    return (min(128 * (i + 1), NH * S) - 1) // HT + 1


def build(nc, x, ctx_in, wq0, wkv0, wout0, router, gate_up, down, sh_gate, sh_up, sh_down,
          wq1, kcq, kckv, wqr, wkr, wo1, fg, fu, fd, lnw, rope_q, rope_kc, rope_ks, out):
    with ExitStack() as ctx:
        def sem(name):
            return ctx.enter_context(nc.semaphore(name))

        total = 212544
        slab_at = -(-nc.sbuf_base // 64) * 64
        ctx.enter_context(nc.sbuf_tensor("slab", [128, total // 4 + 16], F32))
        cursor = [0]

        def size_of(shape, dt):
            n = 2 if dt == BF16 else 4
            for d in shape[1:]:
                n *= d
            return -(-n // 32) * 32

        def place(name, shape, dt=F32):
            at = cursor[0]
            cursor[0] += size_of(shape, dt)
            assert cursor[0] <= total, (name, cursor[0])
            return nc.alloc_sbuf_tensor_at(name, shape, dt, offset=slab_at + at)

        x_sb = place("x_sb", [S, B, D])
        ident = place("ident", [128, 128])
        ident_bf = place("ident_bf", [128, 128], BF16)
        mhalf = place("mhalf", [128, B])
        wqb = place("wqb", [128, DC, NH, 128])
        wqt = place("wqt", [128, DC, NH, QB - 128])
        amat = place("amat", [128, NH, 3, CD])
        bmat = place("bmat", [128, GH, D])
        ropeq = place("ropeq", [128, 4, S])
        wgT = place("wgT", [128, DC, F1], BF16)
        wuT = place("wuT", [128, DC, F1], BF16)
        wdT = place("wdT", [128, FC, D], BF16)
        wmean = place("wmean", [128, 3])
        wcol = place("wcol", [128, 3])
        wsum = place("wsum", [128, 3])
        winv = place("winv", [128, 3])
        stats = place("stats", [S, B, 6])
        mv = place("mv", [S, B, 2])
        veps = place("veps", [S, B])
        rstd = place("rstd", [S, B])
        top = place("top", [S, B])
        gatev = place("gatev", [S, B])
        pick = place("pick", [S, B])
        eq = place("eq", [S, B, NE])
        cand = place("cand", [S, B, NE])
        score = place("score", [S, B, NE])
        order = place("order", [S, NE])
        mx0 = [place(f"mx0_{i}", [S, NH]) for i in range(2)]
        rec0 = place("rec0", [S, NH])
        ones = place("ones", [128, CD])
        stats4 = place("stats4", [S, 6])
        mv4 = place("mv4", [S, 2])
        veps4 = place("veps4", [S, 1])
        rstd4 = place("rstd4", [S, 1])
        qsc = place("qsc", [S, 8])
        ssq = place("ssq", [S, 2])
        vh = place("vh", [S, 1])
        rstdh = place("rstdh", [S, 1])
        after_fixed = cursor[0]

        wkr_n = place("wkr_n", [CD, NH, RD])
        wqr_n = place("wqr_n", [QB // 2, 2 * NH, RD])
        lxyz = [place(f"lxyz{i}", [RD, 2, 3, 128]) for i in range(2)]
        wkrT = place("wkrT", [RD, NH, CD])
        kckv_n = place("kckv_n", [QK, NH, CD])
        wo_n = place("wo_n", [128, DC, NH * QK])
        woT = [place(f"woT{i}", [QK, 2, D]) for i in range(2)]
        end_1 = cursor[0]
        cursor[0] = after_fixed
        wq1_n = place("wq1_n", [QK, NH, D])
        kcq_n = place("kcq_n", [QK, NH, QB])
        after_qb = cursor[0]
        fw = place("fw", [128, 2 * F1])
        fq = [place(f"fq{i}", [128, 2 * F1], BF16) for i in range(3)]
        end_2 = cursor[0]
        cursor[0] = after_fixed
        kv = [place(f"kv{i}", [KP, KT, 2 * CD + 1], F32R) for i in range(2)]
        craw = [place(f"craw{i}", [KP, KT, CD]) for i in range(2)]
        ropekc = place("ropekc", [KP, KT, CD])
        ropeks = place("ropeks", [KP, KT, CD])
        kcos = place("kcos", [KP, 2, CD])
        ksin = place("ksin", [KP, 2, CD])
        kraw = place("kraw", [KP, 2, CD])
        y = [place(f"y{i}", [S, D]) for i in range(2)]
        assert cursor[0] <= after_qb
        cursor[0] = after_qb
        kv += [place(f"kv{i}", [KP, KT, 2 * CD + 1], F32R) for i in range(2, KV_BUF)]
        ctu = place("ctu", [128, GQ])
        ct = place("ct", [128, GQ])
        lnw_b = place("lnw_b", [S, F1])
        sums = [place(f"sums{i}", [CD + 1, HT]) for i in range(2)]
        end_3 = cursor[0]
        after_stage = max(end_1, end_2, end_3)

        cursor[0] = after_stage
        xnT = place("xnT", [128, DC, T])
        xn = place("xn", [S, B, D])
        wqT = place("wqT", [128, DC, NG, 128])
        wkT = place("wkT", [CD, NG, 128])
        wvT = place("wvT", [CD, D])
        woutT = place("woutT", [128, DC, D])
        routerT = place("routerT", [128, DC, NE])
        ctx0T = place("ctx0T", [CD, T])
        qT = place("qT", [128, NG, T])
        kT = place("kT", [128, NG, T])
        vaug = place("vaug", [S, B, NH, HD + 1])
        sm = [place(f"sm{i}", [S, NH, S]) for i in range(2)]
        turned_once = cursor[0]
        wq_n = place("wq_n", [128, DC, D])
        wout_n = place("wout_n", [128, DC, D])
        router_n = place("router_n", [NE, D])
        cursor[0] = turned_once
        pT = place("pT", [S, NH, S])
        mask = place("mask", [S, S])
        turned_once = cursor[0]
        wkv_n = place("wkv_n", [128, 4, CD])
        ctx0 = place("ctx0", [S, B, CD])
        cursor[0] = turned_once
        oT = place("oT", [128, DC, S])
        ao = place("ao", [S, D])
        cursor[0] = after_stage + size_of([128, DC, T], F32)
        xr = [place(f"xr{i}", [128, DC, T]) for i in range(2)]
        scB = place("scB", [128, NE, T])
        scT = place("scT", [NE, T])
        egu = [place(f"egu{i}", [128, DC, 2 * FI]) for i in range(EBUF)]
        edn = [place(f"edn{i}", [128, FM, D]) for i in range(EBUF)]
        sg = [place(f"sg{i}", [128, HT]) for i in range(2)]
        hT = [place(f"hT{i}", [128, HT]) for i in range(3)]
        cursor[0] = after_stage + 3 * size_of([128, DC, T], F32)
        yT = place("yT", [128, DC, T])
        cursor[0] = after_stage
        khl = [place(f"khl{i}", [128, LC], F32R) for i in range(2)]
        kh1 = [place(f"kh1{i}", [CD + 1, LC], F32R) for i in range(2)]
        qh = [place(f"qh{i}", [128, NH * S], F32R) for i in range(2)]
        ql = [place(f"ql{i}", [CD + 1, NH * S], F32R) for i in range(2)]
        xyz = [place(f"xyz{i}", [128, 3, HG, S]) for i in range(2)]
        pt = [place(f"pt{i}", [KP, HT]) for i in range(PT_BUF)]
        ph = [place(f"ph{i}", [KP, HT], F32R) for i in range(PS_BUF)]
        pl = [place(f"pl{i}", [KP, HT], F32R) for i in range(PS_BUF)]
        xn3 = place("xn3", [S, D])
        x3T = place("x3T", [128, DC, S])
        nmx = [place(f"nmx{i}", [128, MT]) for i in range(2)]
        nmr = [place(f"nmr{i}", [MT, 128], F32R) for i in range(2)]
        xn4 = place("xn4", [S, D])
        xq = place("xq", [S, D], BF16)
        xqT = place("xqT", [128, DC, S], BF16)
        sg1 = place("sg1", [S, F1])
        h1 = place("h1", [S, F1])
        hq = place("hq", [S, F1], BF16)
        hqT = place("hqT", [128, FC, S], BF16)
        inv = [place(f"inv{i}", [S, HG]) for i in range(2)]

        ps = ctx.enter_context(nc.psum_tensor("ps", [128, 8, 512], F32))

        ld_x, ld_ctx0, ld_w0, ld_router = sem("ld_x"), sem("ld_ctx0"), sem("ld_w0"), sem("ld_router")
        ld_st1, ld_st2, ld_wo, ld_const = sem("ld_st1"), sem("ld_st2"), sem("ld_wo"), sem("ld_const")
        ld_f = [sem(f"ld_f{i}") for i in range(3)]
        ld_e = [sem(f"ld_e{i}") for i in range(EBUF)]
        ld_craw = [sem(f"ld_craw{i}") for i in range(2)]
        tails_set = sem("tails_set")
        ld_rk, ld_lnw = sem("ld_rk"), sem("ld_lnw")
        set_up, pool_step = sem("set_up"), sem("pool_step")
        dve_step = sem("dve_step")
        var_ready, rstd_ready, xn_ready = sem("var_ready"), sem("rstd_ready"), sem("xn_ready")
        w_turned, w_kept = sem("w_turned"), sem("w_kept")
        proj_done, proj_kept_a, proj_kept_v = sem("proj_done"), sem("proj_kept_a"), sem("proj_kept_v")
        st_turned, st_kept, st_product, st_product_kept = (
            sem("st_turned"), sem("st_kept"), sem("st_product"), sem("st_product_kept"))
        qb_product, qb_kept_a, qb_kept_v = sem("qb_product"), sem("qb_kept_a"), sem("qb_kept_v")
        w_abs, w_mean, w_scaled, w_quant = sem("w_abs"), sem("w_mean"), sem("w_scaled"), sem("w_quant")
        fq_turned, fq_kept = sem("fq_turned"), sem("fq_kept")
        s0_done, s0_masked, s0_max, s0_shifted, s0_exp = (
            sem("s0_done"), sem("s0_masked"), sem("s0_max"), sem("s0_shifted"), sem("s0_exp"))
        p0_turned, p0_kept_a, p0_kept_v = sem("p0_turned"), sem("p0_kept_a"), sem("p0_kept_v")
        pv0_done, ao_ready, o0_turned, o0_kept, out0_done, x1_ready = (
            sem("pv0_done"), sem("ao_ready"), sem("o0_turned"), sem("o0_kept"), sem("out0_done"), sem("x1_ready"))
        var2_ready, rstd2_ready, xn2_ready, xn2_turned, xn2_kept = (
            sem("var2_ready"), sem("rstd2_ready"), sem("xn2_ready"), sem("xn2_turned"), sem("xn2_kept"))
        logits_done, top_ready, gate_ready, score_ready = (
            sem("logits_done"), sem("top_ready"), sem("gate_ready"), sem("score_ready"))
        sc_turned, sc_kept, sc_spread, sc_spread_kept = (
            sem("sc_turned"), sem("sc_kept"), sem("sc_spread"), sem("sc_spread_kept"))
        xr_ready, gu_done, silu_done, h_ready, down_done = (
            sem("xr_ready"), sem("gu_done"), sem("silu_done"), sem("h_ready"), sem("down_done"))
        y_kept_a, y_kept_v, y_turned, x2_ready = sem("y_kept_a"), sem("y_kept_v"), sem("y_turned"), sem("x2_ready")
        var3_ready, rstd3_ready, xn3_ready, x3_turned, x3_kept = (
            sem("var3_ready"), sem("rstd3_ready"), sem("xn3_ready"), sem("x3_turned"), sem("x3_kept"))
        kv_ready, k_turned, k_kept = (
            sem("kv_ready"), sem("k_turned"), sem("k_kept"))
        qbig_done, rope_done, q_done, q_hi, q_lo = (
            sem("qbig_done"), sem("rope_done"), sem("q_done"), sem("q_hi"), sem("q_lo"))
        m_done, m_reduced, m_turned, m_kept = sem("m_done"), sem("m_reduced"), sem("m_turned"), sem("m_kept")
        max_row = [sem(f"max_row{i}") for i in range(2)]
        s_done, ph_ready, pl_ready, pv_done = (
            sem("s_done"), sem("ph_ready"), sem("pl_ready"), sem("pv_done"))
        sums_kept, sums_turned, sums_inverted, c_kept, sum_spread, c_ready, o_done, x3_ready = (
            sem("sums_kept"), sem("sums_turned"), sem("sums_inverted"), sem("c_kept"), sem("sum_spread"), sem("c_ready"), sem("o_done"), sem("x3_ready"))
        var4_ready, rstd4_ready, xq_ready, xq_turned, xq_kept = (
            sem("var4_ready"), sem("rstd4_ready"), sem("xq_ready"), sem("xq_turned"), sem("xq_kept"))
        g_done, u_done, silu1_done, h1_part, h1_ready, h1_square = (
            sem("g_done"), sem("u_done"), sem("silu1_done"), sem("h1_part"), sem("h1_ready"), sem("h1_square"))
        varh_ready, rstdh_ready, hq_ready, hq_turned, hq_kept = (
            sem("varh_ready"), sem("rstdh_ready"), sem("hq_ready"), sem("hq_turned"), sem("hq_kept"))
        down1_done, y_ready = sem("down1_done"), sem("y_ready")
        y_stored = [sem(f"y_stored{i}") for i in range(2)]

        SET_UP = 7 + NE
        ST1 = 16
        block = ctx.enter_context(nc.Block())

        def load_expert(sp, e):
            g, d, s = egu[e % EBUF], edn[e % EBUF], ld_e[e % EBUF]
            if e == 0:
                sp.dma_start(g[:, :, 0:FI], sh_gate.rearrange("(c p) n -> p c n", p=128)).then_inc(s, 16)
                sp.dma_start(g[:, :, FI:2 * FI], sh_up.rearrange("(c p) n -> p c n", p=128)).then_inc(s, 16)
                sp.dma_start(d[:, :, :], sh_down.rearrange("(m p) n -> p m n", p=128)).then_inc(s, 16)
            else:
                sp.dma_start(g[:, :, :], gate_up[e - 1].rearrange("(c p) n -> p c n", p=128)).then_inc(s, 16)
                sp.dma_start(d[:, :, :], down[e - 1].rearrange("(m p) n -> p m n", p=128)).then_inc(s, 16)

        def load_ternary(sp, i):
            if i:
                sp.wait_ge(w_scaled, i)
            dst = fw[:, :].rearrange("p (r n) -> p r n", r=2 if i == 2 else FC)
            sp.dma_start(dst, (fg, fu, fd)[i].rearrange("(r p) n -> p r n", p=128)).then_inc(ld_f[i], 16)

        def expert_loaded(e):
            return 32 * (e // EBUF + 1) + (16 if e % EBUF == 0 else 0)

        def load_keys(sp, b):
            if b >= 2:
                sp.wait_ge(kv_ready, KT // 2 * (b - 1))
            c = craw[b % 2]
            sp.dma_start(c[0:KP - 1, :, :], ctx_in[b, 0:(KP - 1) * KT, :].rearrange("(p t) d -> p t d", t=KT)).then_inc(ld_craw[b % 2], 16)
            sp.dma_start(c[KP - 1:KP, 0:KL, :], ctx_in[b, (KP - 1) * KT:LC, :].rearrange("(p t) d -> p t d", t=KL)).then_inc(ld_craw[b % 2], 16)

        def store_y(sp, b):
            sp.wait_ge(y_ready, b + 1)
            sp.dma_start(out[b], y[b % 2][:, :]).then_inc(y_stored[b % 2], 16)

        @block.sync
        def _(sp):
            sp.dma_start(x_sb[:, :, :], x.rearrange("b s d -> s b d")).then_inc(ld_x, 16)
            sp.dma_start(wq_n[:, :, :], wq0.rearrange("(r p) d -> p r d", p=128)).then_inc(ld_w0, 16)
            sp.dma_start(wkv_n[:, :, :], wkv0.rearrange("(r p) d -> p r d", p=128)).then_inc(ld_w0, 16)
            sp.dma_start(wout_n[:, :, :], wout0.rearrange("(r p) d -> p r d", p=128)).then_inc(ld_w0, 16)
            sp.dma_start(ctx0[:, :, :], ctx_in[:, 0:S, :].rearrange("b s d -> s b d")).then_inc(ld_ctx0, 16)
            sp.dma_start(router_n[:, :], router).then_inc(ld_router, 16)
            sp.dma_start(wkr_n[:, :, :], wkr.rearrange("h d r -> d h r")).then_inc(ld_st1, 16)
            sp.dma_start(wqr_n[:, :, :], wqr.rearrange("h (a q) r -> q (h a) r", a=2)).then_inc(ld_st1, 16)
            sp.dma_start(kckv_n[:, :, :], kckv.rearrange("h k d -> k h d")).then_inc(ld_wo, 16)
            sp.dma_start(wo_n[:, :, :], wo1.rearrange("(r p) k -> p r k", p=128)).then_inc(ld_wo, 16)
            sp.dma_start(ropeq[:, :, :], rope_q).then_inc(ld_const, 16)
            sp.wait_ge(st_product, ST1)
            sp.wait_ge(st_kept, ST1)
            sp.dma_start(wq1_n[:, :, :], wq1.rearrange("(h k) d -> k h d", k=QK)).then_inc(ld_st2, 16)
            sp.dma_start(kcq_n[:, :, :], kcq.rearrange("h k q -> k h q")).then_inc(ld_st2, 16)
            load_ternary(sp, 0)
            sp.wait_ge(out0_done, B)
            sp.wait_ge(o0_kept, B)
            sp.wait_ge(x1_ready, B)
            sp.wait_ge(xn2_turned, B)
            for e in range(EBUF):
                load_expert(sp, e)
            sp.wait_ge(qb_product, NH)
            for dst, src in ((ropekc, rope_kc), (ropeks, rope_ks)):
                sp.dma_start(dst[0:KP - 1, :, :], src[0:(KP - 1) * KT, :].rearrange("(p t) d -> p t d", t=KT)).then_inc(ld_rk, 16)
                sp.dma_start(dst[KP - 1:KP, 0:KL, :], src[(KP - 1) * KT:LC, :].rearrange("(p t) d -> p t d", t=KL)).then_inc(ld_rk, 16)
            load_keys(sp, 0)
            load_keys(sp, 1)
            load_ternary(sp, 1)
            for e in range(EBUF, NE + 1):
                sp.wait_ge(down_done, 2 * FM * (e - EBUF + 1))
                load_expert(sp, e)
                if e == 5:
                    load_ternary(sp, 2)
            sp.wait_ge(fq_turned, 6)
            sp.dma_start(lnw_b[:, :], lnw.rearrange("(a n) -> a n", a=1).to_broadcast([S, F1])).then_inc(ld_lnw, 16)
            for b in range(B):
                sp.wait_ge(m_kept, b + 1)
                if b >= 2:
                    sp.wait_ge(s_done, SLOTS * (b - 1))
                row = ql[b % 2][CD:CD + 1, :].bitcast(F32)
                for i0, n in ((0, MT - 1), (MT - 1, 1)):
                    w = m_rows(i0)
                    sp.dma_start(row[:, 128 * i0:128 * i0 + n * w].rearrange("a (i q) -> a i q", q=w),
                                 nmr[b % 2][i0:i0 + n, 0:w].bitcast(F32)).then_inc(max_row[b % 2], 16)
                if b + 2 < B:
                    load_keys(sp, b + 2)
                if b >= 2:
                    store_y(sp, b - 2)
            store_y(sp, B - 2)
            store_y(sp, B - 1)
            for i in range(2):
                sp.wait_ge(y_stored[i], 16 * B // 2)

        def rotate_keys(pool, step, b, j):
            c, k = craw[b % 2], kv[b % KV_BUF]
            h = CD // 2
            r, t = slice(0, key_rows(2 * j)), slice(2 * j, 2 * j + 2)
            if j == 0:
                pool.wait_ge(ld_craw[b % 2], 32 * (b // 2 + 1))
                if b >= KV_BUF:
                    pool.wait_ge(pv_done, SLOTS * (b - KV_BUF + 1))
            nc.gpsimd.tensor_tensor(kcos[r, :, :], c[r, t, :], ropekc[r, t, :], ALU.mult)
            nc.gpsimd.tensor_tensor(ksin[r, :, 0:h], c[r, t, h:CD], ropeks[r, t, 0:h], ALU.mult)
            step(nc.gpsimd.tensor_tensor(ksin[r, :, h:CD], c[r, t, 0:h], ropeks[r, t, h:CD], ALU.mult))
            step(nc.gpsimd.tensor_tensor(kraw[r, :, :], kcos[r, :, :], ksin[r, :, :], ALU.add))
            step(nc.gpsimd.tensor_copy(k[r, t, CD:2 * CD], kraw[r, :, :]))
            nc.gpsimd.tensor_tensor(k[r, t, 0:CD], kraw[r, :, :], k[r, t, CD:2 * CD].bitcast(F32), ALU.subtract)\
                .then_inc(kv_ready, 1)
            pool.wait_ge(kv_ready, KT // 2 * b + j + 1)

        def norm_x4(pool, power, b):
            pool.wait_ge(var4_ready, b + 1)
            power(rstd4[:, :], veps4[:, :], S).then_inc(rstd4_ready, 1)

        def norm_h(pool, power, b):
            pool.wait_ge(varh_ready, b + 1)
            power(rstdh[:, :], vh[:, :], S).then_inc(rstdh_ready, 1)

        @block.gpsimd
        def _(pool):
            steps = [0]

            def step(ins):
                steps[0] += 1
                ins.then_inc(pool_step, 1)
                pool.wait_ge(pool_step, steps[0])

            def power(dst, src, rows):
                return nc.gpsimd.tensor_tensor(dst, src, mhalf[0:rows, 0:src.shape[1]], ALU.pow)

            step(nc.gpsimd.memset(ident[:, :], 0.0))
            step(nc.gpsimd.affine_select(out=ident[:, :], in_=ident[:, :], compare_op=ALU.not_equal, fill=1.0,
                                         base=0, pattern=[[-1, 128]], channel_multiplier=1))
            nc.gpsimd.tensor_copy(ident_bf[:, :], ident[:, :]).then_inc(set_up, 1)
            nc.gpsimd.memset(mhalf[:, :], -0.5).then_inc(set_up, 1)
            nc.gpsimd.memset(ones[:, :], 1.0).then_inc(set_up, 1)
            nc.gpsimd.memset(wqT[:, :, :, :], 0.0).then_inc(set_up, 1)
            nc.gpsimd.memset(wkT[:, :, :], 0.0).then_inc(set_up, 1)
            nc.gpsimd.memset(vaug[:, :, :, HD:HD + 1], 1.0).then_inc(set_up, 1)
            for e in range(NE):
                nc.gpsimd.memset(order[:, e:e + 1], float(NE - e)).then_inc(set_up, 1)
            step(nc.gpsimd.memset(mask[:, :], 0.0))
            nc.gpsimd.affine_select(out=mask[:, :], in_=mask[:, :], compare_op=ALU.is_ge, fill=MASKED,
                                    base=0, pattern=[[-1, S]], channel_multiplier=1).then_inc(set_up, 1)
            pool.wait_ge(set_up, SET_UP)
            pool.wait_ge(var_ready, 1)
            power(rstd[:, :], veps[:, :], S).then_inc(rstd_ready, 1)
            for i in range(B + 2):
                if i < B:
                    pool.wait_ge(s0_max, i + 1)
                    nc.gpsimd.tensor_tensor(sm[i % 2][:, :, :], sm[i % 2][:, :, :],
                                            mx0[i % 2][:, :].unsqueeze(2).to_broadcast([S, NH, S]),
                                            ALU.subtract).then_inc(s0_shifted, 1)
                if i >= 2:
                    b = i - 2
                    pool.wait_ge(var2_ready, b + 1)
                    power(rstd[:, b:b + 1], veps[:, b:b + 1], S).then_inc(rstd2_ready, 1)
            pool.wait_ge(qb_product, NH)
            for i in range(2):
                step(nc.gpsimd.memset(kv[i][:, :, 2 * CD:2 * CD + 1].bitcast(F32), 1.0))
            pool.wait_ge(ld_rk, 64)
            for b in range(2):
                for j in range(KT // 2):
                    rotate_keys(pool, step, b, j)
            for i in range(3):
                pool.wait_ge(w_abs, i + 1)
                nc.gpsimd.partition_all_reduce(wsum[:, i:i + 1], wcol[:, i:i + 1], 128,
                                               bass.bass_isa.ReduceOp.add).then_inc(w_mean, 1)
                pool.wait_ge(w_quant, 2 * i + 1)
                step(nc.gpsimd.tensor_scalar(fw[:, :], fw[:, :], winv[:, i:i + 1], 1.0, ALU.mult, ALU.min))
                step(nc.gpsimd.tensor_scalar(fw[:, :], fw[:, :], -1.0, ROUND, ALU.max, ALU.add))
                nc.gpsimd.tensor_scalar(fq[i][:, :], fw[:, :], ROUND, None, ALU.subtract).then_inc(w_scaled, 1)
                pool.wait_ge(w_scaled, i + 1)
                pool.wait_ge(w_quant, 2 * i + 2)
            pool.wait_ge(var3_ready, 1)
            power(rstd[:, :], veps[:, :], S).then_inc(rstd3_ready, 1)
            pool.wait_ge(fq_turned, 6)
            for i in range(2, KV_BUF):
                step(nc.gpsimd.memset(kv[i][:, :, 2 * CD:2 * CD + 1].bitcast(F32), 1.0))
            for i in range(2):
                step(nc.gpsimd.memset(nmx[i][:, :], 0.0))
                nc.gpsimd.memset(kh1[i][CD:CD + 1, :].bitcast(F32), 1.0).then_inc(tails_set, 1)
                pool.wait_ge(tails_set, i + 1)
            for b in range(B):
                for s in range(SLOTS):
                    k = SLOTS * b + s
                    pool.wait_ge(ph_ready, k + 1)
                    if k >= PS_BUF:
                        pool.wait_ge(pv_done, k - PS_BUF + 1)
                    r = slice(0, key_rows(k % KT))
                    nc.gpsimd.tensor_tensor(pl[k % PS_BUF][r, :], pt[k % PT_BUF][r, :], ph[k % PS_BUF][r, :].bitcast(F32),
                                            ALU.subtract).then_inc(pl_ready, 1)
                    if b and s == X4_SLOT:
                        pool.wait_ge(pl_ready, k + 1)
                        norm_x4(pool, power, b - 1)
                    if b and s == H_NORM_SLOT:
                        pool.wait_ge(pl_ready, k + 1)
                        norm_h(pool, power, b - 1)
                    if b + 2 < B and s in ROTATE_SLOT:
                        rotate_keys(pool, step, b + 2, ROTATE_SLOT.index(s))
            pool.wait_ge(pl_ready, SLOTS * B)
            norm_x4(pool, power, B - 1)
            norm_h(pool, power, B - 1)

        @block.tensor
        def _(pe):
            mm, turn = nc.tensor.matmul, nc.tensor.transpose

            def job_bank(n):
                if n >= 4:
                    pe.wait_ge(w_kept, n - 3)
                return ps[:, 4 + n % 4, :]

            pe.wait_ge(set_up, SET_UP)
            pe.wait_ge(ld_w0, 48)
            for n, src in ((0, wq_n), (2, wout_n)):
                if n == 2:
                    o = job_bank(1)
                    for r in range(4):
                        last = turn(o[0:CD, 128 * r:128 * r + 128], wkv_n[:, r, :], ident[:, :])
                    last.then_inc(w_turned, 1)
                o = job_bank(n)
                for c in range(DC):
                    for r in range(DC):
                        last = turn(o[:, (DC * c + r) * 128:(DC * c + r + 1) * 128],
                                    src[:, r, 128 * c:128 * c + 128], ident[:, :])
                last.then_inc(w_turned, 1)
            pe.wait_ge(ld_ctx0, 16)
            for n in (3, 4):
                o = job_bank(n)
                for j in range(4):
                    last = turn(o[0:CD, S * j:S * j + S], ctx0[:, 4 * (n - 3) + j, :], ident[0:S, 0:S])
                last.then_inc(w_turned, 1)
            pe.wait_ge(ld_router, 16)
            o = job_bank(5)
            for c in range(DC):
                last = turn(o[:, NE * c:NE * c + NE], router_n[:, 128 * c:128 * c + 128], ident[0:NE, 0:NE])
            last.then_inc(w_turned, 1)
            for j in range(4):
                pe.wait_ge(xn_ready, 2 * j + 2)
                o = job_bank(6 + j)
                for c in range(DC):
                    for i in range(2):
                        last = turn(o[:, (2 * c + i) * S:(2 * c + i + 1) * S],
                                    xn[:, 2 * j + i, 128 * c:128 * c + 128], ident[0:S, 0:S])
                last.then_inc(w_turned, 1)

            job = 0

            def proj_bank():
                if job >= 4:
                    pe.wait_ge(proj_kept_v if job % 2 else proj_kept_a, (job - 4) // 2 + 1)
                return ps[:, job % 4, :]

            for n in range(2):
                pe.wait_ge(w_kept, 8 + 2 * n)
                for g in range(NG):
                    o = proj_bank()
                    for c in range(DC):
                        last = mm(o[:, 0:HT], wqT[:, c, g, :], xnT[:, c, HT * n:HT * n + HT], start=c == 0, stop=c == DC - 1)
                    last.then_inc(proj_done, 1)
                    job += 1
                    o = proj_bank()
                    mm(o[:, 0:HT], wkT[:, g, :], ctx0T[:, HT * n:HT * n + HT], start=True, stop=True).then_inc(proj_done, 1)
                    job += 1
            for b in range(B):
                o = proj_bank()
                mm(o[0:S, 0:D], ctx0T[:, S * b:S * b + S], wvT[:, :], start=True, stop=True).then_inc(proj_done, 1)
                job += 1

            pe.wait_ge(ld_st1, 32)
            pe.wait_ge(w_kept, 10)
            for j in range(2):
                for i in range(8):
                    last = turn(ps[0:RD, 4 + j, CD * i:CD * i + CD], wkr_n[:, 8 * j + i, :], ident[0:CD, 0:CD])
                last.then_inc(st_turned, 1)

            def stage_turn(i):
                pe.wait_ge(st_kept, i + 1 if i < 2 else i - 1 + 2)
                o = ps[:, 4 + i % 2, :]
                if i < 8:
                    for j in range(4):
                        last = turn(o[0:RD, 96 * j:96 * j + 96], wqr_n[:, 4 * i + j, :], ident[0:96, 0:96])
                else:
                    if i == 8:
                        pe.wait_ge(ld_wo, 32)
                    for a in range(2):
                        h = i - 8 + GH * a
                        for r in range(DC):
                            last = turn(o[:, (DC * a + r) * 128:(DC * a + r + 1) * 128],
                                        wo_n[:, r, QK * h:QK * h + QK], ident[:, :])
                last.then_inc(st_turned, 1)

            def stage_product(i):
                pe.wait_ge(st_kept, i + 3)
                if i >= 2:
                    pe.wait_ge(st_product_kept, i - 1)
                o = ps[:, 6 + i % 2, :]
                if i < 8:
                    for a in range(2):
                        for k in range(3):
                            last = mm(o[:, (3 * a + k) * CD:(3 * a + k + 1) * CD], lxyz[i % 2][:, a, k, :],
                                      wkrT[:, 2 * i + a, :], start=True, stop=True)
                else:
                    for a in range(2):
                        h = i - 8 + GH * a
                        last = mm(o[CD * a:CD * a + CD, 0:D], kckv_n[:, h, :], woT[i % 2][:, a, :], start=True, stop=True)
                last.then_inc(st_product, 1)

            stage_turn(0)
            for i in range(ST1):
                if i + 1 < ST1:
                    stage_turn(i + 1)
                stage_product(i)

            pe.wait_ge(proj_kept_a, 12)
            pe.wait_ge(proj_kept_v, 12)
            pe.wait_ge(st_product_kept, ST1)
            for step in range(B + 3):
                if step < B:
                    b = step
                    if b:
                        pe.wait_ge(s0_masked, b)
                    tok = slice(S * b, S * b + S)
                    for g in range(NG):
                        for i in range(HG):
                            p = slice(HS * i, HS * i + HS)
                            last = mm(ps[0:S, i, S * g:S * g + S], qT[p, g, tok], kT[p, g, tok], start=True, stop=True)
                    last.then_inc(s0_done, 1)
                if 1 <= step <= B:
                    b = step - 1
                    pe.wait_ge(s0_exp, b + 1)
                    for half in range(2):
                        if half == 1:
                            pe.wait_ge(p0_kept_a, b + 1)
                        elif b:
                            pe.wait_ge(p0_kept_v, b)
                        for j in range(8):
                            last = turn(ps[0:S, 4 + j // 4, S * (j % 4):S * (j % 4) + S],
                                        sm[b % 2][:, 8 * half + j, :], ident[0:S, 0:S])
                        last.then_inc(p0_turned, 1)
                    pe.wait_ge(p0_kept_v, b + 1)
                    if b:
                        pe.wait_ge(ao_ready, b)
                    for i in range(HG):
                        for g in range(NG):
                            h = HG * g + i
                            last = mm(ps[0:S, 6, (HD + 1) * h:(HD + 1) * (h + 1)], pT[:, NG * i + g, :],
                                      vaug[:, b, h, :], start=True, stop=True)
                    last.then_inc(pv0_done, 1)
                if 2 <= step <= B + 1:
                    b = step - 2
                    pe.wait_ge(ao_ready, b + 1)
                    if b:
                        pe.wait_ge(xn2_kept, b - 1) if b > 1 else None
                        pe.wait_ge(x1_ready, b)
                    for c in range(DC):
                        last = turn(ps[:, 7, S * c:S * c + S], ao[:, 128 * c:128 * c + 128], ident[0:S, 0:S])
                    last.then_inc(o0_turned, 1)
                    pe.wait_ge(o0_kept, b + 1)
                    for c in range(DC):
                        last = mm(ps[0:S, 7, D:2 * D], oT[:, c, :], woutT[:, c, :], start=c == 0, stop=c == DC - 1)
                    last.then_inc(out0_done, 1)
                if step >= 3:
                    b = step - 3
                    pe.wait_ge(xn2_ready, b + 1)
                    pe.wait_ge(x1_ready, min(b + 2, B))
                    for c in range(DC):
                        last = turn(ps[:, 7, S * c:S * c + S], xn[:, b, 128 * c:128 * c + 128], ident[0:S, 0:S])
                    last.then_inc(xn2_turned, 1)
                    if step < B + 2:
                        pe.wait_ge(xn2_kept, b + 1)

            pe.wait_ge(xn2_kept, B)
            for b in range(B):
                for c in range(DC):
                    last = mm(ps[0:S, 6, NE * b:NE * b + NE], xnT[:, c, S * b:S * b + S], routerT[:, c, :],
                              start=c == 0, stop=c == DC - 1)
            last.then_inc(logits_done, 1)
            pe.wait_ge(ld_st2, 32)
            for h in range(NH):
                if h >= 4:
                    pe.wait_ge(qb_kept_v if h % 2 else qb_kept_a, (h - 4) // 2 + 1)
                for c in range(DC):
                    last = mm(ps[:, h % 4, QB * c:QB * c + QB], wq1_n[:, h, 128 * c:128 * c + 128], kcq_n[:, h, :],
                              start=True, stop=True)
                last.then_inc(qb_product, 1)
            pe.wait_ge(score_ready, 1)
            for b in range(B):
                last = turn(ps[0:NE, 4 + b // 4, S * (b % 4):S * (b % 4) + S], score[:, b, :], ident[0:S, 0:S])
            last.then_inc(sc_turned, 1)
            pe.wait_ge(sc_kept, 1)
            for e in range(NE):
                if e >= 2:
                    pe.wait_ge(sc_spread_kept, e - 1)
                for n in range(2):
                    last = mm(ps[:, 4 + 2 * (e % 2) + n, 0:HT], ident[0:NE, e:e + 1].to_broadcast([NE, 128]),
                              scT[:, HT * n:HT * n + HT], start=True, stop=True)
                last.then_inc(sc_spread, 1)
            pe.wait_ge(sc_spread_kept, NE)
            pe.wait_ge(qb_kept_a, NH // 2)
            pe.wait_ge(qb_kept_v, NH // 2)

            for k in range(ITEMS + 1):
                if k < ITEMS:
                    e, m, n = k // (2 * FM), k // 2 % FM, k % 2
                    w, src = egu[e % EBUF], (xnT if e == 0 else xr[e % 2])
                    if k % (2 * FM) == 0:
                        pe.wait_ge(ld_e[e % EBUF], expert_loaded(e))
                        if e:
                            pe.wait_ge(xr_ready, e)
                    if k >= 2:
                        pe.wait_ge(h_ready, k - 1)
                    for a in range(2):
                        for c in range(DC):
                            last = mm(ps[:, 4 + 2 * a + n, 0:HT], w[:, c, FI * a + 128 * m:FI * a + 128 * m + 128],
                                      src[:, c, HT * n:HT * n + HT], start=c == 0, stop=c == DC - 1)
                    last.then_inc(gu_done, 1)
                if k:
                    j = k - 1
                    e, m, n = j // (2 * FM), j // 2 % FM, j % 2
                    pe.wait_ge(h_ready, j + 1)
                    for c in range(DC):
                        last = mm(ps[:, 2 * c + n, 0:HT], edn[e % EBUF][:, m, 128 * c:128 * c + 128], hT[j % 3][:, :],
                                  start=j < 2, stop=j >= ITEMS - 2)
                    last.then_inc(down_done, 1)
            pe.wait_ge(y_kept_a, 2)
            pe.wait_ge(y_kept_v, 2)
            for b in range(B):
                if b >= 4:
                    pe.wait_ge(x2_ready, b - 3)
                for c in range(DC):
                    last = turn(ps[0:S, 4 + b % 4, 128 * c:128 * c + 128], yT[:, c, S * b:S * b + S], ident[:, :])
                last.then_inc(y_turned, 1)
            for n in range(6):
                i, half = n // 2, n % 2
                pe.wait_ge(w_scaled, i + 1)
                if n >= 4:
                    pe.wait_ge(fq_kept, n - 3)
                o = ps[:, n % 4, :].bitcast(BF16)
                src = fq[i][:, :].rearrange("p (r n) -> p r n", r=2 if i == 2 else FC)
                for j in range(8):
                    if i < 2:
                        part = src[:, j, 128 * half:128 * half + 128]
                    else:
                        part = src[:, j % 2, 128 * (4 * half + j // 2):128 * (4 * half + j // 2) + 128]
                    last = turn(o[:, 128 * j:128 * j + 128], part, ident_bf[:, :])
                last.then_inc(fq_turned, 1)
            pe.wait_ge(fq_kept, 6)

            def turn_x3(b):
                pe.wait_ge(xn3_ready, b + 1)
                for c in range(DC):
                    last = turn(ps[:, 4, S * c:S * c + S], xn3[:, 128 * c:128 * c + 128], ident[0:S, 0:S])
                last.then_inc(x3_turned, 1)

            def q_big(b, g):
                if g == 0:
                    pe.wait_ge(x3_kept, b + 1)
                if NG * b + g:
                    pe.wait_ge(rope_done, NG * b + g)
                for i in range(HG):
                    h = HG * g + i
                    for c in range(DC):
                        mm(ps[:, 4, S * i:S * i + S], wqb[:, c, h, 0:128], x3T[:, c, :], start=c == 0, stop=c == DC - 1)
                for i in range(HG // 2):
                    h = HG * g + 2 * i
                    for c in range(DC):
                        last = mm(ps[:, 5, S * i:S * i + S], wqt[:, c, h:h + 2, :].rearrange("p h q -> p (h q)"),
                                  x3T[:, c, :], start=c == 0, stop=c == DC - 1)
                last.then_inc(qbig_done, 1)

            def q_latent(b, g):
                k = NG * b + g
                pe.wait_ge(rope_done, k + 1)
                if k:
                    pe.wait_ge(q_lo, k)
                if g == 2 and b >= 2:
                    pe.wait_ge(x3_ready, b - 1)
                for i in range(HG):
                    h = HG * g + i
                    for j in range(3):
                        last = mm(ps[0:CD, 6, S * i:S * i + S], amat[:, h, j, :],
                                  xyz[k % 2][:, j, i, :], start=j == 0, stop=j == 2)
                last.then_inc(q_done, 1)

            def turn_keys(b, j):
                pe.wait_ge(kv_ready, KT // 2 * b + 2 * j + 2)
                if 3 * b + j:
                    pe.wait_ge(k_kept, 3 * b + j)
                if j == 0 and b >= 2:
                    pe.wait_ge(c_ready, NG * (b - 1))
                for t in range(4 * j, 4 * j + 4):
                    at = key_start(t) - key_start(4 * j)
                    last = turn(ps[:, 7, at:at + key_rows(t)], kv[b % KV_BUF][0:key_rows(t), t, 0:2 * CD].bitcast(F32),
                                ident[0:key_rows(t), 0:key_rows(t)])
                last.then_inc(k_turned, 1)

            def max_tile(b, i):
                k = MT * b + i
                if i == 0:
                    pe.wait_ge(k_kept, 3 * (b + 1))
                if i == 0 or b == 0:
                    pe.wait_ge(q_lo, NG * b + (groups_for(i) if b == 0 and i < EARLY else NG))
                if k:
                    pe.wait_ge(m_reduced, k - 1 if b == 0 and i > EARLY else k)
                w = m_rows(i)
                for n in range(3):
                    last = mm(ps[0:w, max_bank(b, i) + n, 0:MN], qh[b % 2][:, 128 * i:128 * i + w],
                              khl[b % 2][:, MSTART[n]:MSTART[n] + MN], start=True, stop=True)
                last.then_inc(m_done, 1)

            def turn_max(b):
                pe.wait_ge(tails_set, 2)
                pe.wait_ge(m_reduced, MT * (b + 1))
                turn(ps[0:MT, 6, 0:128], nmx[b % 2][:, :], ident[:, :]).then_inc(m_turned, 1)

            def scores(k):
                b, c, t = k // SLOTS, k // KT % NG, k % KT
                if k % SLOTS == 0:
                    pe.wait_ge(max_row[b % 2], 32 * (b // 2 + 1))
                if k >= 2:
                    pe.wait_ge(ph_ready, k - 1)
                keys = slice(key_start(t), key_start(t) + key_rows(t))
                for lhs, rhs, first in ((khl[b % 2], qh[b % 2], True), (kh1[b % 2], ql[b % 2], False)):
                    last = mm(ps[0:key_rows(t), k % 2, 0:HT], lhs[:, keys], rhs[:, HT * c:HT * c + HT],
                              start=first, stop=not first)
                last.then_inc(s_done, 1)

            def values(k):
                b, t, q = k // SLOTS, k % KT, k // KT
                pe.wait_ge(ph_ready, k + 1)
                if t == 0 and q >= 2:
                    pe.wait_ge(c_kept, q - 1)
                r, bank = slice(0, key_rows(t)), ps[:, 2 + q % 2, 0:HT]
                w, hi, lo = kv[b % KV_BUF], ph[k % PS_BUF], pl[k % PS_BUF]
                mm(bank[0:CD + 1, :], w[r, t, CD:2 * CD + 1], hi[r, :], start=t == 0, stop=False)
                mm(bank[0:CD, :], w[r, t, 0:CD], hi[r, :], start=False, stop=False)
                pe.wait_ge(pl_ready, k + 1)
                mm(bank[0:CD + 1, :], w[r, t, CD:2 * CD + 1], lo[r, :], start=False, stop=t == KT - 1).then_inc(pv_done, 1)

            def turn_sums(q):
                pe.wait_ge(sums_kept, q + 1)
                if q:
                    pe.wait_ge(c_ready, q)
                if q % NG == 0 and q // NG + 1 < B:
                    pe.wait_ge(k_kept, 3 * (q // NG + 2))
                for i in range(HG):
                    last = mm(ps[0:S, 7, i:i + 1], sums[q % 2][CD:CD + 1, S * i:S * i + S], ones[CD:CD + 1, 0:1],
                              start=True, stop=True)
                last.then_inc(sums_turned, 1)

            def spread_sums(q):
                a = q % NG // 2
                pe.wait_ge(sums_inverted, q + 1)
                for i in range(HG):
                    last = mm(ps[CD * a:CD * a + CD, 7, S * i:S * i + S], inv[q % 2][:, i:i + 1].to_broadcast([S, CD]),
                              ident[0:S, 0:S], start=True, stop=True)
                last.then_inc(sum_spread, 1)

            def attention_out(b):
                pe.wait_ge(c_ready, NG * (b + 1))
                if b + 2 < B:
                    pe.wait_ge(q_lo, NG * (b + 2) + 2)
                for h in range(GH):
                    last = mm(ps[0:S, 6, 0:D], ct[:, S * h:S * h + S], bmat[:, h, :], start=h == 0, stop=h == GH - 1)
                last.then_inc(o_done, 1)

            def maxima_read(b, s):
                if b + 2 < B:
                    pe.wait_ge(m_reduced, MT * (b + 2) + sum(x < s for x in M_SLOT))

            def turn_xq(b):
                pe.wait_ge(xq_ready, b + 1)
                maxima_read(b, XQ_SLOT)
                o = ps[:, 4, :].bitcast(BF16)
                for c in range(DC):
                    last = turn(o[:, S * c:S * c + S], xq[:, 128 * c:128 * c + 128], ident_bf[0:S, 0:S])
                last.then_inc(xq_turned, 1)

            def gate_and_up(b, half):
                maxima_read(b, GU_SLOT[half])
                if half:
                    pe.wait_ge(h1_part, 2 * b + 1)
                else:
                    pe.wait_ge(xq_kept, b + 1)
                    pe.wait_ge(x3_ready, b + 1)
                    for n in range(2):
                        for c in range(DC):
                            last = mm(ps[0:S, 5 + n, :], xqT[:, c, :], wgT[:, c, 512 * n:512 * n + 512],
                                      start=c == 0, stop=c == DC - 1)
                    last.then_inc(g_done, 1)
                for c in range(DC):
                    last = mm(ps[0:S, 4, :], xqT[:, c, :], wuT[:, c, 512 * half:512 * half + 512],
                              start=c == 0, stop=c == DC - 1)
                last.then_inc(u_done, 1)

            def turn_hq(b):
                pe.wait_ge(hq_ready, b + 1)
                maxima_read(b, HQ_SLOT)
                o = ps[:, 4, :].bitcast(BF16)
                for f in range(FC):
                    last = turn(o[:, S * f:S * f + S], hq[:, 128 * f:128 * f + 128], ident_bf[0:S, 0:S])
                last.then_inc(hq_turned, 1)

            def ffn_down(b):
                pe.wait_ge(hq_kept, b + 1)
                maxima_read(b, DOWN_SLOT)
                for f in range(FC):
                    last = mm(ps[0:S, 5, 0:D], hqT[:, f, :], wdT[:, f, :], start=f == 0, stop=f == FC - 1)
                last.then_inc(down1_done, 1)

            def feed_forward_read(b, s):
                if s > XQ_SLOT:
                    pe.wait_ge(xq_kept, b + 1)
                if s > GU_SLOT[1]:
                    pe.wait_ge(h1_part, 2 * b + 2)
                if s > HQ_SLOT:
                    pe.wait_ge(hq_kept, b + 1)
                if s > DOWN_SLOT:
                    pe.wait_ge(y_ready, b + 1)

            pe.wait_ge(x2_ready, B)
            turn_keys(0, 0)
            turn_x3(0)
            q_big(0, 0)
            turn_keys(0, 1)
            q_big(0, 1)
            q_latent(0, 0)
            turn_keys(0, 2)
            pe.wait_ge(tails_set, 2)
            q_big(0, 2)
            max_tile(0, 0)
            q_latent(0, 1)
            max_tile(0, 1)
            q_big(0, 3)
            max_tile(0, 2)
            q_latent(0, 2)
            max_tile(0, 3)
            q_latent(0, 3)
            for i in range(EARLY, MT):
                max_tile(0, i)
            turn_max(0)
            for b in range(B):
                pe.wait_ge(m_kept, b + 1)
                if b >= 2:
                    pe.wait_ge(y_ready, b - 1)
                for s in range(SLOTS):
                    k = SLOTS * b + s
                    scores(k)
                    if k >= LAG:
                        values(k - LAG)
                    if (b or s >= KT) and s % KT == TURN_AT:
                        turn_sums(NG * b + s // KT - 1)
                    if (b or s >= KT) and s % KT == SPREAD_AT:
                        spread_sums(NG * b + s // KT - 1)
                    if b + 1 < B:
                        if s == X_SLOT:
                            turn_x3(b + 1)
                        if s in BIG_SLOT:
                            q_big(b + 1, BIG_SLOT.index(s))
                        if s in LAT_SLOT:
                            q_latent(b + 1, LAT_SLOT.index(s))
                    if b + 1 < B and s in KEY_SLOT:
                        turn_keys(b + 1, KEY_SLOT.index(s))
                    if b:
                        if s == OUT_SLOT:
                            attention_out(b - 1)
                        if s == XQ_SLOT:
                            turn_xq(b - 1)
                        if s in GU_SLOT:
                            gate_and_up(b - 1, GU_SLOT.index(s))
                        if s == HQ_SLOT:
                            turn_hq(b - 1)
                        if s == DOWN_SLOT:
                            ffn_down(b - 1)
                    if b + 1 < B:
                        if s in M_SLOT:
                            if b:
                                feed_forward_read(b - 1, s)
                            max_tile(b + 1, M_SLOT.index(s))
                        if s == MX_SLOT:
                            turn_max(b + 1)
            for k in range(SLOTS * B - LAG, SLOTS * B):
                values(k)
            turn_sums(NG * B - 1)
            spread_sums(NG * B - 1)
            attention_out(B - 1)
            turn_xq(B - 1)
            gate_and_up(B - 1, 0)
            gate_and_up(B - 1, 1)
            pe.wait_ge(h1_part, 2 * B)
            turn_hq(B - 1)
            ffn_down(B - 1)

        @block.scalar
        def _(act):
            def keep(dst, src, **more):
                return nc.scalar.activation(dst, src, ACT.Copy, **more)

            act.wait_ge(set_up, SET_UP)
            for n in range(10):
                act.wait_ge(w_turned, n + 1)
                o = ps[:, 4 + n % 4, :]
                if n == 0:
                    last = keep(wqT[:, :, :, :].rearrange("p c g (i s) -> p (c g i) s", s=HS)[:, :, 0:HD],
                                o.rearrange("p (j d) -> p j d", d=HD))
                elif n == 1:
                    keep(wkT[:, :, :].rearrange("p g (i s) -> p (g i) s", s=HS)[:, :, 0:HD],
                         o[0:CD, 0:D].rearrange("p (j d) -> p j d", d=HD))
                    last = keep(wvT[:, :], o[0:CD, D:2 * D])
                elif n == 2:
                    last = keep(woutT[:, :, :].rearrange("p c n -> p (c n)"), o)
                elif n in (3, 4):
                    last = keep(ctx0T[:, HT * (n - 3):HT * (n - 2)], o[0:CD, 0:HT])
                elif n == 5:
                    last = keep(routerT[:, :, :].rearrange("p c e -> p (c e)"), o[:, 0:DC * NE])
                else:
                    j = n - 6
                    last = keep(xnT[:, :, 2 * S * j:2 * S * (j + 1)], o[:, 0:2 * DC * S].rearrange("p (c q) -> p c q", c=DC))
                last.then_inc(w_kept, 1)
            for job in range(0, 24, 2):
                act.wait_ge(proj_done, job + 1)
                o = ps[:, job % 4, :]
                if job < 16:
                    last = keep(qT[:, job // 2 % NG, HT * (job // 8):HT * (job // 8 + 1)], o[:, 0:HT])
                else:
                    last = keep(vaug[:, job - 16, :, 0:HD], o[0:S, 0:D].rearrange("p (h d) -> p h d", d=HD))
                last.then_inc(proj_kept_a, 1)
            for j in range(2):
                act.wait_ge(st_turned, j + 1)
                keep(wkrT[:, 8 * j:8 * j + 8, :].rearrange("p h d -> p (h d)"), ps[0:RD, 4 + j, :]).then_inc(st_kept, 1)
            for i in range(ST1):
                act.wait_ge(st_turned, i + 3)
                if i >= 2:
                    act.wait_ge(st_product, i - 1)
                o = ps[:, 4 + i % 2, :]
                if i < 8:
                    t = o[0:RD, 0:2 * QB].rearrange("p (a q) -> p a q", a=2)
                    l, h = lxyz[i % 2], QB // 2
                    keep(l[:, :, 0, :], t[:, :, 0:128])
                    keep(l[:, :, 1, 0:h], t[:, :, h:QB])
                    keep(l[:, :, 1, h:128], t[:, :, 0:128 - h])
                    keep(l[:, :, 2, 0:RD], t[:, :, 128:QB])
                    last = keep(l[:, :, 2, RD:128], t[:, :, 128 - h:QB - h])
                else:
                    last = keep(woT[i % 2][:, :, :].rearrange("p a n -> p (a n)"), o)
                last.then_inc(st_kept, 1)
            for step in range(B + 3):
                if 1 <= step <= B:
                    b = step - 1
                    act.wait_ge(p0_turned, 2 * b + 1)
                    if b:
                        act.wait_ge(pv0_done, b)
                    keep(pT[:, 0:8, :].rearrange("p (a j) q -> p a (j q)", a=2), ps[0:S, 4:6, 0:HT]).then_inc(p0_kept_a, 1)
                if step < B:
                    act.wait_ge(s0_shifted, step + 1)
                    nc.scalar.activation(sm[step % 2][:, :, :], sm[step % 2][:, :, :], ACT.Exp, scale=HD ** -0.5)\
                      .then_inc(s0_exp, 1)
                if 2 <= step <= B + 1:
                    act.wait_ge(o0_turned, step - 1)
                    keep(oT[:, :, :].rearrange("p c q -> p (c q)"), ps[:, 7, 0:DC * S]).then_inc(o0_kept, 1)
                if step >= 3:
                    b = step - 3
                    act.wait_ge(xn2_turned, b + 1)
                    keep(xnT[:, :, S * b:S * b + S], ps[:, 7, 0:DC * S].rearrange("p (c q) -> p c q", c=DC)).then_inc(xn2_kept, 1)
            act.wait_ge(top_ready, 1)
            nc.scalar.activation(gatev[:, :], top[:, :], ACT.Sigmoid).then_inc(gate_ready, 1)
            for h in range(0, NH, 2):
                act.wait_ge(qb_product, h + 1)
                o = ps[:, h % 4, 0:DC * QB].rearrange("p (c q) -> p c q", c=DC)
                keep(wqb[:, :, h, :], o[:, :, 0:128])
                keep(wqt[:, :, h, :], o[:, :, 128:QB]).then_inc(qb_kept_a, 1)
            for e in range(NE):
                act.wait_ge(sc_spread, e + 1)
                keep(scB[:, e, :].rearrange("p (n q) -> p n q", n=2), ps[:, 4 + 2 * (e % 2):6 + 2 * (e % 2), 0:HT])\
                    .then_inc(sc_spread_kept, 1)
            for k in range(ITEMS):
                act.wait_ge(gu_done, k + 1)
                if k >= 2:
                    act.wait_ge(h_ready, k - 1)
                nc.scalar.activation(sg[k % 2][:, :], ps[:, 4 + k % 2, 0:HT], ACT.Silu).then_inc(silu_done, 1)
            for n in range(2):
                act.wait_ge(down_done, ITEMS - 1 + n)
                keep(yT[:, 0, HT * n:HT * n + HT], ps[:, n, 0:HT]).then_inc(y_kept_a, 1)
            for n in range(6):
                i, half = n // 2, n % 2
                act.wait_ge(fq_turned, n + 1)
                o = ps[:, n % 4, :].bitcast(BF16)
                if i < 2:
                    last = keep((wgT, wuT)[i][:, half, :], o)
                else:
                    last = keep(wdT[:, 4 * half:4 * half + 4, :].rearrange("p f n -> p (f n)"), o)
                last.then_inc(fq_kept, 1)

            def keep_x3(b):
                act.wait_ge(x3_turned, b + 1)
                keep(x3T[:, :, :].rearrange("p c q -> p (c q)"), ps[:, 4, 0:DC * S]).then_inc(x3_kept, 1)

            def keep_q(b, g):
                k = NG * b + g
                act.wait_ge(q_done, k + 1)
                if g == 0 and b >= 2:
                    act.wait_ge(s_done, SLOTS * (b - 1))
                for p in (0, CD):
                    last = nc.scalar.activation(qh[b % 2][p:p + CD, HT * g:HT * g + HT], ps[0:CD, 6, 0:HT], ACT.Copy)
                last.then_inc(q_hi, 1)

            def keep_keys(b, j):
                act.wait_ge(k_turned, 3 * b + j + 1)
                if j == 0 and b >= 2:
                    act.wait_ge(s_done, SLOTS * (b - 1))
                k0 = key_start(4 * j)
                n = key_start(4 * j + 4) - k0
                keep(khl[b % 2][:, k0:k0 + n], ps[:, 7, 0:n])
                keep(kh1[b % 2][0:CD, k0:k0 + n], ps[CD:128, 7, 0:n]).then_inc(k_kept, 1)

            def keep_max(b):
                act.wait_ge(m_turned, b + 1)
                if b >= 2:
                    act.wait_ge(max_row[b % 2], 32 * (b // 2))
                nc.scalar.activation(nmr[b % 2][:, :], ps[0:MT, 6, 0:128], ACT.Copy).then_inc(m_kept, 1)

            def keep_context(q):
                act.wait_ge(pv_done, KT * (q + 1))
                if q >= 2:
                    act.wait_ge(sums_turned, q - 1)
                if q >= NG:
                    act.wait_ge(c_ready, q - NG + 1)
                keep(sums[q % 2][CD:CD + 1, :], ps[CD:CD + 1, 2 + q % 2, 0:HT]).then_inc(sums_kept, 1)
                a = q % NG // 2
                keep(ctu[CD * a:CD * a + CD, HT * (q % 2):HT * (q % 2) + HT], ps[0:CD, 2 + q % 2, 0:HT]).then_inc(c_kept, 1)

            def keep_xq(b):
                act.wait_ge(xq_turned, b + 1)
                o = ps[:, 4, :].bitcast(BF16)
                keep(xqT[:, :, :].rearrange("p c q -> p (c q)"), o[:, 0:DC * S]).then_inc(xq_kept, 1)

            def silu_gate(b):
                act.wait_ge(g_done, b + 1)
                if b:
                    act.wait_ge(hq_ready, b)
                nc.scalar.activation(sg1[:, :].rearrange("p (n q) -> p n q", n=2), ps[0:S, 5:7, :], ACT.Silu,
                                     scale=qsc[:, 2:3]).then_inc(silu1_done, 1)

            def square_h(b):
                act.wait_ge(h1_part, 2 * b + 2)
                nc.scalar.activation(sg1[:, :], h1[:, :], ACT.Square, accum_out=ssq[:, 0:1]).then_inc(h1_square, 1)

            def turn_hq(b):
                act.wait_ge(hq_turned, b + 1)
                o = ps[:, 4, :].bitcast(BF16)
                keep(hqT[:, :, :].rearrange("p f q -> p (f q)"), o[:, 0:FC * S]).then_inc(hq_kept, 1)

            keep_keys(0, 0)
            keep_x3(0)
            keep_keys(0, 1)
            keep_q(0, 0)
            keep_keys(0, 2)
            for g in range(1, NG):
                keep_q(0, g)
            keep_max(0)
            for b in range(B):
                for s in range(SLOTS):
                    k = SLOTS * b + s
                    act.wait_ge(s_done, k + 1)
                    if k >= PT_BUF:
                        act.wait_ge(pl_ready, k - PT_BUF + 1)
                    if k >= PS_BUF:
                        act.wait_ge(pv_done, k - PS_BUF + 1)
                    rows = key_rows(k % KT)
                    nc.scalar.activation(pt[k % PT_BUF][0:rows, :], ps[0:rows, k % 2, 0:HT], ACT.Exp)
                    nc.scalar.activation(ph[k % PS_BUF][0:rows, :], ps[0:rows, k % 2, 0:HT], ACT.Exp).then_inc(ph_ready, 1)
                    if b + 1 < B:
                        if s == X_SLOT:
                            keep_x3(b + 1)
                        if s in KEY_SLOT:
                            keep_keys(b + 1, KEY_SLOT.index(s))
                        if s in LAT_SLOT:
                            keep_q(b + 1, LAT_SLOT.index(s))
                    if (b or s >= KT) and s % KT == KEEP_AT:
                        keep_context(NG * b + s // KT - 1)
                    if b:
                        if s == XQ_SLOT:
                            keep_xq(b - 1)
                        if s == GU_SLOT[0]:
                            silu_gate(b - 1)
                        if s == SQ_SLOT:
                            square_h(b - 1)
                        if s == HQ_SLOT:
                            turn_hq(b - 1)
                    if b + 1 < B and s == MX_SLOT:
                        keep_max(b + 1)
            keep_context(NG * B - 1)
            keep_xq(B - 1)
            silu_gate(B - 1)
            square_h(B - 1)
            turn_hq(B - 1)

        @block.vector
        def _(dve):
            steps = [0]
            tt, ts, stt = nc.vector.tensor_tensor, nc.vector.tensor_scalar, nc.vector.scalar_tensor_tensor

            def step(ins):
                steps[0] += 1
                ins.then_inc(dve_step, 1)
                dve.wait_ge(dve_step, steps[0])

            dve.wait_ge(ld_x, 16)
            for b in range(B):
                last = nc.vector.bn_stats(stats[:, b, :], x_sb[:, b, :])
            step(last)
            for b in range(B):
                last = nc.vector.bn_aggr(mv[:, b, :], stats[:, b, :])
            step(last)
            dve.wait_ge(set_up, SET_UP)
            ts(veps[:, :], mv[:, :, 1], LN_EPS, None, ALU.add).then_inc(var_ready, 1)
            dve.wait_ge(rstd_ready, 1)
            for b in range(B):
                ts(xn[:, b, :], x_sb[:, b, :], mv[:, b, 0:1], rstd[:, b:b + 1], ALU.subtract, ALU.mult).then_inc(xn_ready, 1)
            for job in range(1, 24, 2):
                dve.wait_ge(proj_done, job + 1)
                o = ps[:, job % 4, :]
                if job < 16:
                    last = nc.vector.tensor_copy(kT[:, job // 2 % NG, HT * (job // 8):HT * (job // 8 + 1)], o[:, 0:HT])
                else:
                    last = nc.vector.tensor_copy(vaug[:, job - 16, :, 0:HD], o[0:S, 0:D].rearrange("p (h d) -> p h d", d=HD))
                last.then_inc(proj_kept_v, 1)
            for i in range(ST1):
                dve.wait_ge(st_product, i + 1)
                o = ps[:, 6 + i % 2, :]
                if i < 8:
                    last = nc.vector.tensor_copy(amat[:, 2 * i:2 * i + 2, :, :].rearrange("p a j d -> p (a j d)"), o[:, 0:6 * CD])
                else:
                    last = nc.vector.tensor_copy(bmat[:, i - 8, :], o[:, 0:D])
                last.then_inc(st_product_kept, 1)

            for s in range(B + 3):
                if s < B:
                    dve.wait_ge(s0_done, s + 1)
                    if s >= 2:
                        dve.wait_ge(p0_turned, 2 * (s - 1))
                    m = sm[s % 2]
                    tt(m[:, :, :].rearrange("p (i g) k -> p i g k", i=HG),
                       ps[0:S, 0:HG, 0:HT].rearrange("p i (g k) -> p i g k", g=NG),
                       mask[:, :].unsqueeze(1).unsqueeze(1).to_broadcast([S, HG, NG, S]), ALU.add).then_inc(s0_masked, 1)
                    dve.wait_ge(s0_masked, s + 1)
                    nc.vector.tensor_reduce(mx0[s % 2][:, :], m[:, :, :], AX.X, ALU.max).then_inc(s0_max, 1)
                if 1 <= s <= B:
                    b = s - 1
                    dve.wait_ge(p0_turned, 2 * b + 2)
                    if b:
                        dve.wait_ge(pv0_done, b)
                    nc.vector.tensor_copy(pT[:, 8:16, :].rearrange("p (a j) q -> p a (j q)", a=2), ps[0:S, 4:6, 0:HT])\
                      .then_inc(p0_kept_v, 1)
                    dve.wait_ge(pv0_done, b + 1)
                    if b:
                        dve.wait_ge(o0_turned, b)
                    o = ps[0:S, 6, 0:NH * (HD + 1)].rearrange("p (h d) -> p h d", d=HD + 1)
                    step(nc.vector.reciprocal(rec0[:, :], o[:, :, HD]))
                    tt(ao[:, :].rearrange("p (h d) -> p h d", d=HD), o[:, :, 0:HD],
                       rec0[:, :].unsqueeze(2).to_broadcast([S, NH, HD]), ALU.mult).then_inc(ao_ready, 1)
                if 2 <= s <= B + 1:
                    b = s - 2
                    dve.wait_ge(out0_done, b + 1)
                    tt(x_sb[:, b, :], x_sb[:, b, :], ps[0:S, 7, D:2 * D], ALU.add).then_inc(x1_ready, 1)
                    dve.wait_ge(x1_ready, b + 1)
                    step(nc.vector.bn_stats(stats[:, b, :], x_sb[:, b, :]))
                    step(nc.vector.bn_aggr(mv[:, b, :], stats[:, b, :]))
                    ts(veps[:, b:b + 1], mv[:, b, 1:2], LN_EPS, None, ALU.add).then_inc(var2_ready, 1)
                    dve.wait_ge(rstd2_ready, b + 1)
                    ts(xn[:, b, :], x_sb[:, b, :], mv[:, b, 0:1], rstd[:, b:b + 1], ALU.subtract, ALU.mult).then_inc(xn2_ready, 1)

            dve.wait_ge(logits_done, 1)
            lg = ps[0:S, 6, 0:B * NE].rearrange("p (b e) -> p b e", e=NE)

            def over(v):
                return v.unsqueeze(2).to_broadcast([S, B, NE])

            nc.vector.tensor_reduce(top[:, :], lg, AX.X, ALU.max).then_inc(top_ready, 1)
            dve.wait_ge(top_ready, 1)
            step(tt(eq[:, :, :], lg, over(top[:, :]), ALU.is_equal))
            step(tt(cand[:, :, :], eq[:, :, :], order[:, :].unsqueeze(1).to_broadcast([S, B, NE]), ALU.mult))
            step(nc.vector.tensor_reduce(pick[:, :], cand[:, :, :], AX.X, ALU.max))
            step(tt(eq[:, :, :], cand[:, :, :], over(pick[:, :]), ALU.is_equal))
            dve.wait_ge(gate_ready, 1)
            tt(score[:, :, :], eq[:, :, :], over(gatev[:, :]), ALU.mult).then_inc(score_ready, 1)
            for h in range(1, NH, 2):
                dve.wait_ge(qb_product, h + 1)
                o = ps[:, h % 4, 0:DC * QB].rearrange("p (c q) -> p c q", c=DC)
                nc.vector.tensor_copy(wqb[:, :, h, :], o[:, :, 0:128])
                nc.vector.tensor_copy(wqt[:, :, h, :], o[:, :, 128:QB]).then_inc(qb_kept_v, 1)
            dve.wait_ge(sc_turned, 1)
            nc.vector.tensor_copy(scT[:, :].rearrange("p (n q) -> p n q", n=2), ps[0:NE, 4:6, 0:HT]).then_inc(sc_kept, 1)

            def scaled_x(e):
                dve.wait_ge(sc_spread_kept, e)
                if e >= 3:
                    dve.wait_ge(gu_done, 2 * FM * (e - 1))
                tt(xr[e % 2][:, :, :], xnT[:, :, :], scB[:, e - 1, :].unsqueeze(1).to_broadcast([128, DC, T]),
                   ALU.mult).then_inc(xr_ready, 1)

            def weight_mean(i):
                dve.wait_ge(ld_f[i], 16)
                nc.vector.tensor_reduce(wcol[:, i:i + 1], fw[:, :], AX.X, ALU.add, apply_absolute_value=True)\
                  .then_inc(w_abs, 1)
                dve.wait_ge(w_mean, i + 1)
                step(ts(wmean[:, i:i + 1], wsum[:, i:i + 1], 1.0 / (F1 * D), Q_EPS, ALU.mult, ALU.max))
                nc.vector.reciprocal(winv[:, i:i + 1], wmean[:, i:i + 1]).then_inc(w_quant, 2)

            scaled_x(1)
            scaled_x(2)
            for k in range(ITEMS):
                e = k // (2 * FM)
                if k % (2 * FM) == 4 and 2 <= e < NE:
                    scaled_x(e + 1)
                if k in (3, 27, 51):
                    weight_mean(k // 24)
                dve.wait_ge(silu_done, k + 1)
                if k >= 3:
                    dve.wait_ge(down_done, k - 2)
                tt(hT[k % 3][:, :], sg[k % 2][:, :], ps[:, 6 + k % 2, 0:HT], ALU.mult).then_inc(h_ready, 1)
            for n in range(2):
                dve.wait_ge(down_done, ITEMS - 1 + n)
                nc.vector.tensor_copy(yT[:, 1, HT * n:HT * n + HT], ps[:, 2 + n, 0:HT]).then_inc(y_kept_v, 1)
            for b in range(B):
                dve.wait_ge(y_turned, b + 1)
                tt(x_sb[:, b, :], x_sb[:, b, :], ps[0:S, 4 + b % 4, 0:D], ALU.add).then_inc(x2_ready, 1)
                dve.wait_ge(x2_ready, b + 1)
                last = nc.vector.bn_stats(stats[:, b, :], x_sb[:, b, :])
            step(last)
            for b in range(B):
                last = nc.vector.bn_aggr(mv[:, b, :], stats[:, b, :])
            step(last)
            ts(veps[:, :], mv[:, :, 1], LN_EPS, None, ALU.add).then_inc(var3_ready, 1)
            dve.wait_ge(rstd3_ready, 1)

            def norm_x3(b):
                if b:
                    dve.wait_ge(x3_turned, b)
                ts(xn3[:, :], x_sb[:, b, :], mv[:, b, 0:1], rstd[:, b:b + 1], ALU.subtract, ALU.mult).then_inc(xn3_ready, 1)

            def rope(b, g):
                k = NG * b + g
                dve.wait_ge(qbig_done, k + 1)
                if k >= 2:
                    dve.wait_ge(q_done, k - 1)
                o = xyz[k % 2]
                for j in range(2):
                    tt(o[:, j, :, :], ps[:, 4, 0:HT].rearrange("p (i q) -> p i q", i=HG),
                       ropeq[:, j, :].unsqueeze(1).to_broadcast([128, HG, S]), ALU.mult)
                for j in range(2):
                    for a in range(2):
                        last = tt(o[CD * j:CD * j + CD, 2, a:HG:2, :],
                                  ps[CD * a:CD * a + CD, 5, 0:HT // 2].rearrange("p (i q) -> p i q", i=HG // 2),
                                  ropeq[CD * a:CD * a + CD, 2 + j, :].unsqueeze(1).to_broadcast([CD, HG // 2, S]), ALU.mult)
                last.then_inc(rope_done, 1)

            def low_q(b, g):
                k = NG * b + g
                cols = slice(HT * g, HT * g + HT)
                dve.wait_ge(q_hi, k + 1)
                tt(ql[b % 2][0:CD, cols], ps[0:CD, 6, 0:HT], qh[b % 2][0:CD, cols].bitcast(F32), ALU.subtract).then_inc(q_lo, 1)

            def reduce_max(b, i):
                dve.wait_ge(m_done, MT * b + i + 1)
                w = m_rows(i)
                if i == 0 and b >= 2:
                    dve.wait_ge(m_turned, b - 1)
                nc.vector.tensor_reduce(nmx[b % 2][0:w, i:i + 1], ps[0:w, max_bank(b, i):max_bank(b, i) + 3, 0:MN], AX.XY, ALU.max, negate=True)\
                  .then_inc(m_reduced, 1)

            def invert_sums(q):
                dve.wait_ge(sums_turned, q + 1)
                if q >= 2:
                    dve.wait_ge(sum_spread, q - 1)
                nc.vector.reciprocal(inv[q % 2][:, :], ps[0:S, 7, 0:HG]).then_inc(sums_inverted, 1)

            def divide(q):
                dve.wait_ge(sum_spread, q + 1)
                dve.wait_ge(c_kept, q + 1)
                if q >= NG and q % NG == 0:
                    dve.wait_ge(o_done, q // NG)
                a = q % NG // 2
                p, cols = slice(CD * a, CD * a + CD), slice(HT * (q % 2), HT * (q % 2) + HT)
                tt(ct[p, cols], ctu[p, cols], ps[p, 7, 0:HT], ALU.mult).then_inc(c_ready, 1)

            def residual(b):
                dve.wait_ge(o_done, b + 1)
                tt(x_sb[:, b, :], x_sb[:, b, :], ps[0:S, 6, 0:D], ALU.add).then_inc(x3_ready, 1)
                dve.wait_ge(x3_ready, b + 1)
                step(nc.vector.bn_stats(stats4[:, :], x_sb[:, b, :]))
                step(nc.vector.bn_aggr(mv4[:, :], stats4[:, :]))
                ts(veps4[:, :], mv4[:, 1:2], LN_EPS, None, ALU.add).then_inc(var4_ready, 1)

            def quantise_x(b):
                dve.wait_ge(rstd4_ready, b + 1)
                if b:
                    dve.wait_ge(xq_turned, b)
                    dve.wait_ge(silu1_done, b)
                step(ts(xn4[:, :], x_sb[:, b, :], mv4[:, 0:1], rstd4[:, 0:1], ALU.subtract, ALU.mult))
                step(nc.vector.tensor_reduce(qsc[:, 4:5], xn4[:, :], AX.X, ALU.max, apply_absolute_value=True))
                step(ts(qsc[:, 4:5], qsc[:, 4:5], Q_EPS, None, ALU.max))
                step(nc.vector.reciprocal(qsc[:, 5:6], qsc[:, 4:5]))
                step(ts(qsc[:, 5:6], qsc[:, 5:6], Q_MAX, None, ALU.mult))
                step(ts(xn4[:, :], xn4[:, :], qsc[:, 5:6], ROUND, ALU.mult, ALU.add))
                ts(qsc[:, 2:3], qsc[:, 4:5], 1.0 / Q_MAX, wmean[0:S, 0:1], ALU.mult, ALU.mult)
                ts(qsc[:, 3:4], qsc[:, 4:5], 1.0 / Q_MAX, wmean[0:S, 1:2], ALU.mult, ALU.mult)
                ts(xq[:, :], xn4[:, :], ROUND, Q_MAX, ALU.subtract, ALU.min).then_inc(xq_ready, 1)

            def hidden(b, half):
                dve.wait_ge(silu1_done, b + 1)
                dve.wait_ge(u_done, 2 * b + half + 1)
                cols = slice(512 * half, 512 * half + 512)
                stt(h1[:, cols], ps[0:S, 4, :], qsc[:, 3:4], sg1[:, cols], ALU.mult, ALU.mult).then_inc(h1_part, 1)

            def hidden_norm(b):
                dve.wait_ge(h1_square, b + 1)
                ts(vh[:, :], ssq[:, 0:1], 1.0 / F1, RMS_EPS, ALU.mult, ALU.add).then_inc(varh_ready, 1)

            def quantise_h(b, part):
                if part == 0:
                    dve.wait_ge(rstdh_ready, b + 1)
                    step(stt(h1[:, :], h1[:, :], rstdh[:, 0:1], lnw_b[:, :], ALU.mult, ALU.mult))
                elif part == 1:
                    step(nc.vector.tensor_reduce(qsc[:, 6:7], h1[:, :], AX.X, ALU.max, apply_absolute_value=True))
                    step(ts(qsc[:, 6:7], qsc[:, 6:7], Q_EPS, None, ALU.max))
                    step(nc.vector.reciprocal(qsc[:, 7:8], qsc[:, 6:7]))
                    step(ts(qsc[:, 7:8], qsc[:, 7:8], Q_MAX, None, ALU.mult))
                    step(ts(qsc[:, 0:1], qsc[:, 6:7], 1.0 / Q_MAX, wmean[0:S, 2:3], ALU.mult, ALU.mult))
                elif part == 2:
                    step(ts(h1[:, :], h1[:, :], qsc[:, 7:8], ROUND, ALU.mult, ALU.add))
                else:
                    if b:
                        dve.wait_ge(hq_turned, b)
                    ts(hq[:, :], h1[:, :], ROUND, Q_MAX, ALU.subtract, ALU.min).then_inc(hq_ready, 1)

            def result(b):
                dve.wait_ge(down1_done, b + 1)
                if b >= 2:
                    dve.wait_ge(y_stored[b % 2], 16 * (b // 2))
                stt(y[b % 2][:, :], ps[0:S, 5, 0:D], qsc[:, 0:1], x_sb[:, b, :], ALU.mult, ALU.add).then_inc(y_ready, 1)

            norm_x3(0)
            dve.wait_ge(ld_const, 16)
            dve.wait_ge(ld_lnw, 16)
            rope(0, 0)
            rope(0, 1)
            low_q(0, 0)
            dve.wait_ge(tails_set, 2)
            rope(0, 2)
            reduce_max(0, 0)
            low_q(0, 1)
            reduce_max(0, 1)
            rope(0, 3)
            reduce_max(0, 2)
            low_q(0, 2)
            reduce_max(0, 3)
            low_q(0, 3)
            for i in range(EARLY, MT):
                reduce_max(0, i)
            norm_x3(1)
            for b in range(B):
                for s in range(SLOTS):
                    if (b or s >= KT) and s % KT == TURN_AT:
                        invert_sums(NG * b + s // KT - 1)
                    if (b or s >= KT) and s % KT == SPREAD_AT:
                        divide(NG * b + s // KT - 1)
                    if b + 1 < B:
                        if s in BIG_SLOT:
                            rope(b + 1, BIG_SLOT.index(s))
                        if s in LAT_SLOT:
                            low_q(b + 1, LAT_SLOT.index(s))
                    if b:
                        if s == OUT_SLOT:
                            residual(b - 1)
                        if s == LAT_SLOT[-1]:
                            quantise_x(b - 1)
                        if s in GU_SLOT:
                            hidden(b - 1, GU_SLOT.index(s))
                        if s == SQ_SLOT:
                            hidden_norm(b - 1)
                        if s in QH_SLOT:
                            quantise_h(b - 1, QH_SLOT.index(s))
                        if s == DOWN_SLOT:
                            result(b - 1)
                    if b + 1 < B and s in M_SLOT:
                        reduce_max(b + 1, M_SLOT.index(s))
                    if s == MX_SLOT and b + 2 < B:
                        norm_x3(b + 2)
            invert_sums(NG * B - 1)
            divide(NG * B - 1)
            residual(B - 1)
            quantise_x(B - 1)
            hidden(B - 1, 0)
            hidden(B - 1, 1)
            hidden_norm(B - 1)
            for part in range(4):
                quantise_h(B - 1, part)
            result(B - 1)


def rope_tables():
    import numpy as np

    def table(length, dim):
        inv = (np.float32(1.0) / np.power(np.float32(10000.0), np.arange(0, dim, 2, dtype=np.float32) / np.float32(dim))).astype(np.float32)
        f = np.arange(length, dtype=np.float32)[:, None] * inv[None, :]
        return np.repeat(np.sin(f), 2, axis=-1), np.repeat(np.cos(f), 2, axis=-1)

    half = QB // 2
    sin_q, cos_q = table(S, QB)
    turned = np.concatenate([sin_q[:, half:], -sin_q[:, :half]], axis=1)
    rope_q = np.zeros((128, 4, S), np.float32)
    rope_q[:, 0] = cos_q[:, 0:128].T
    rope_q[:, 1] = turned[:, 0:128].T
    rope_q[:, 2] = np.tile(cos_q[:, 128:QB].T, (2, 1))
    rope_q[:, 3] = np.tile(turned[:, 128:QB].T, (2, 1))
    sin_k, cos_k = table(LC, CD)
    sin_k = np.concatenate([-sin_k[:, :CD // 2], sin_k[:, CD // 2:]], axis=1)
    return rope_q, np.ascontiguousarray(cos_k), np.ascontiguousarray(sin_k)


_INS = ['x', 'ctx_512', 'L0_xattn_Wq', 'L0_xattn_Wkv_expand', 'L0_xattn_Wout', 'L0_ffn_router_w',
        'L0_ffn_gate_up_proj', 'L0_ffn_down_proj', 'L0_ffn_shared_gate_w', 'L0_ffn_shared_up_w',
        'L0_ffn_shared_down_w', 'L1_xattn_Wq', 'L1_xattn_w_kc_q', 'L1_xattn_w_kc_kv', 'L1_xattn_W_qr',
        'L1_xattn_W_kr', 'L1_xattn_Wo', 'L1_ffn_w_gate', 'L1_ffn_w_up', 'L1_ffn_w_down', 'L1_ffn_ln_weight']


def kernel(**inputs):
    import numpy as _np
    import concourse.bacc as _bacc
    from concourse import mybir as _mybir
    from concourse.bass_utils import run_bass_kernel_spmd as _run

    nc = _bacc.Bacc("TRN2", target_bir_lowering=False, num_devices=1)
    arrays, args = {}, []
    tables = dict(zip(("rope_q", "rope_kc", "rope_ks"), rope_tables()))
    for name in _INS + list(tables):
        a = _np.ascontiguousarray(tables[name] if name in tables else inputs[name])
        arrays[f"in_{name}_dram"] = a
        args.append(nc.dram_tensor(f"in_{name}_dram", a.shape, _mybir.dt.from_np(a.dtype), kind="ExternalInput").ap())
    args.append(nc.dram_tensor("out_0_dram", (B, S, D), F32, kind="ExternalOutput").ap())
    build(nc, *args)
    r = _run(nc, [arrays], core_ids=[0])
    return r.results[0]["out_0_dram"]
```

```python
from contextlib import ExitStack

import concourse.bass as bass
from concourse import mybir

F32 = mybir.dt.float32
F32R = mybir.dt.float32r
BF16 = mybir.dt.bfloat16
ALU = mybir.AluOpType
ACT = mybir.ActivationFunctionType
AX = mybir.AxisListType

B, S, D = 8, 100, 256
T = B * S
HT = T // 2
DC = D // 128
LC, CD = 1444, 64
NH, HD = 16, 16
HS = 32
HG = 4
NG = NH // HG
NE, FI = 8, 512
FM = FI // 128
QK, QB, RD = 128, 192, 64
KT = 12
KP = -(-LC // KT)
KL = LC - (KP - 1) * KT
GH = NH // 2
GQ = GH * S
MT = -(-NH * S // 128)
MN = 482
MSTART = (0, 481, 962)
F1 = 1024
FC = F1 // 128
SLOTS = NG * KT
LAG = 3
KEEP_AT, TURN_AT, SPREAD_AT = 3, 4, 5
X_SLOT = 0
KEY_SLOT = (8, 9, 11)
BIG_SLOT = (1, 4, 7, 10)
LAT_SLOT = (4, 7, 10, 12)
M_SLOT = (14, 18, 22, 24, 26, 28, 30, 32, 34, 36, 37, 39, 40)
MX_SLOT = 42
OUT_SLOT = 8
XQ_SLOT, GU_SLOT = 17, (19, 21)
SQ_SLOT, QH_SLOT = 22, (25, 28, 31, 34)
HQ_SLOT, DOWN_SLOT = 38, 41
X4_SLOT, H_NORM_SLOT = 10, 24
ROTATE_SLOT = (4, 5, 7, 8, 10, 11)
LN_EPS, RMS_EPS, Q_EPS, Q_MAX = 1e-5, 1e-6, 1e-5, 127.0
ROUND = 12582912.0
MASKED = -1e30
LO_ROW = 32

ITEMS = (NE + 1) * FM * 2
EBUF = 2
CHUNKS = (NE + 1) * FM
TERNARY_AFTER = (5, 7)
SUM_ITEM = (14, 36, 53)
DOWN_LAG = 2
PT_BUF, PS_BUF = 3, 4
KV_BUF = 3


def key_rows(t):
    return KP if t < KL else KP - 1


def key_start(t):
    return t * KP if t <= KL else KL * KP + (t - KL) * (KP - 1)


def m_rows(i):
    return min(128, NH * S - 128 * i)


EARLY = 4


def max_bank(b, i):
    return 4 if b or (i > EARLY and i % 2) else 0


def groups_for(i):
    return (min(128 * (i + 1), NH * S) - 1) // HT + 1


def build(nc, x, ctx_in, wq0, wkv0, wout0, router, gate_up, down, sh_gate, sh_up, sh_down,
          wq1, kcq, kckv, wqr, wkr, wo1, fg, fu, fd, lnw, rope_q, rope_kc, rope_ks, out):
    with ExitStack() as ctx:
        def sem(name):
            return ctx.enter_context(nc.semaphore(name))

        total = 212544
        slab_at = -(-nc.sbuf_base // 64) * 64
        ctx.enter_context(nc.sbuf_tensor("slab", [128, total // 4 + 16], F32))
        cursor = [0]

        def size_of(shape, dt):
            n = 2 if dt == BF16 else 4
            for d in shape[1:]:
                n *= d
            return -(-n // 32) * 32

        def place(name, shape, dt=F32):
            at = cursor[0]
            cursor[0] += size_of(shape, dt)
            assert cursor[0] <= total, (name, cursor[0])
            return nc.alloc_sbuf_tensor_at(name, shape, dt, offset=slab_at + at)

        x_sb = place("x_sb", [S, B, D])
        ident = place("ident", [128, 128])
        ident_bf = place("ident_bf", [128, 128], BF16)
        sel = place("sel", [128, NE], F32R)
        mhalf = place("mhalf", [128, B])
        wqb = place("wqb", [128, DC, NH, 128])
        wqt = place("wqt", [128, DC, NH, QB - 128])
        amat = place("amat", [128, NH, 3, CD])
        bmat = place("bmat", [128, GH, D])
        ropeq = place("ropeq", [128, 4, S])
        wgT = place("wgT", [128, DC, F1], BF16)
        wuT = place("wuT", [128, DC, F1], BF16)
        wdT = place("wdT", [128, FC, D], BF16)
        wmean = place("wmean", [128, 3])
        wcol = place("wcol", [128, 3])
        wsum = place("wsum", [128, 3])
        winv = place("winv", [128, 3])
        stats = place("stats", [S, B, 6])
        mv = place("mv", [S, B, 2])
        veps = place("veps", [S, B])
        rstd = place("rstd", [S, B])
        top = place("top", [S, B])
        gatev = place("gatev", [S, B])
        pick = place("pick", [S, B])
        eq = place("eq", [S, B, NE])
        cand = place("cand", [S, B, NE])
        score = place("score", [S, B, NE])
        order = place("order", [S, NE])
        mx0 = [place(f"mx0_{i}", [S, NH]) for i in range(2)]
        rec0 = place("rec0", [S, NH])
        ones = place("ones", [128, CD])
        stats4 = place("stats4", [S, 6])
        mv4 = place("mv4", [S, 2])
        veps4 = place("veps4", [S, 1])
        rstd4 = place("rstd4", [S, 1])
        qsc = place("qsc", [S, 8])
        ssq = place("ssq", [S, 2])
        vh = place("vh", [S, 1])
        rstdh = place("rstdh", [S, 1])
        after_fixed = cursor[0]

        wkr_n = place("wkr_n", [CD, NH, RD])
        wqr_n = place("wqr_n", [QB // 2, 2 * NH, RD])
        lxyz = [place(f"lxyz{i}", [RD, 2, 3, 128]) for i in range(2)]
        wkrT = place("wkrT", [RD, NH, CD])
        kckv_n = place("kckv_n", [QK, NH, CD])
        wo_n = place("wo_n", [128, DC, NH * QK])
        woT = [place(f"woT{i}", [QK, 2, D]) for i in range(2)]
        end_1 = cursor[0]
        cursor[0] = after_fixed
        wq1_n = place("wq1_n", [QK, NH, D])
        kcq_n = place("kcq_n", [QK, NH, QB])
        after_qb = cursor[0]
        fw = place("fw", [128, 2 * F1])
        after_fw = cursor[0]
        fq = [place(f"fq{i}", [128, 2 * F1], BF16) for i in range(3)]
        end_2 = cursor[0]
        cursor[0] = after_fixed
        kv = [place(f"kv{i}", [KP, KT, 2 * CD + 1], F32R) for i in range(2)]
        craw = [place(f"craw{i}", [KP, KT, CD]) for i in range(2)]
        ropekc = place("ropekc", [KP, KT, CD])
        ropeks = place("ropeks", [KP, KT, CD])
        kcos = place("kcos", [KP, 2, CD])
        ksin = place("ksin", [KP, 2, CD])
        kraw = place("kraw", [KP, 2, CD])
        y = [place(f"y{i}", [S, D]) for i in range(2)]
        assert cursor[0] <= after_qb
        cursor[0] = after_qb
        kv += [place(f"kv{i}", [KP, KT, 2 * CD + 1], F32R) for i in range(2, KV_BUF)]
        ctu = place("ctu", [128, GQ])
        ct = place("ct", [128, GQ])
        lnw_b = place("lnw_b", [S, F1])
        sums = [place(f"sums{i}", [CD + 1, HT]) for i in range(2)]
        end_3 = cursor[0]
        after_stage = max(end_1, end_2, end_3)

        cursor[0] = after_stage
        xnT = place("xnT", [128, DC, T])
        wqT = place("wqT", [128, DC, NG, 128])
        wkT = place("wkT", [CD, NG, 128])
        wvT = place("wvT", [CD, D])
        ctx0T = place("ctx0T", [CD, T])
        ctx0 = place("ctx0", [S, B, CD])
        cursor[0] = max(cursor[0], after_stage + 3 * size_of([128, DC, T], F32))
        woutT = place("woutT", [128, DC, D])
        routerT = place("routerT", [128, DC, NE])
        xn = place("xn", [S, B, D])
        qT = place("qT", [128, NG, T])
        kT = place("kT", [128, NG, T])
        vaug = place("vaug", [S, B, NH, HS])
        sm = [place(f"sm{i}", [S, NH, S]) for i in range(2)]
        turned_once = cursor[0]
        wq_n = place("wq_n", [128, DC, D])
        wout_n = place("wout_n", [128, DC, D])
        router_n = place("router_n", [NE, D])
        cursor[0] = turned_once
        pT = place("pT", [S, NH, S])
        mask = place("mask", [S, S])
        wkv_n = place("wkv_n", [128, 4, CD])
        cursor[0] = after_fw
        oT = place("oT", [128, DC, S])
        ao = place("ao", [S, D])
        vT = place("vT", [128, HT])
        cursor[0] = after_stage + size_of([128, DC, T], F32)
        xh = place("xh", [128, DC, T], F32R)
        xl = place("xl", [128, DC, T], F32R)
        scB = place("scB", [128, NE, T])
        egu = [place(f"egu{i}", [128, DC, 2, FM, 128]) for i in range(EBUF)]
        edn = [place(f"edn{i}", [128, FM, D]) for i in range(EBUF)]
        wgh = [place(f"wgh{i}", [128, DC, 2, 128], F32R) for i in range(2)]
        wgl = [place(f"wgl{i}", [128, DC, 2, 128], F32R) for i in range(2)]
        wdh = [place(f"wdh{i}", [128, D], F32R) for i in range(2)]
        wdl = [place(f"wdl{i}", [128, D], F32R) for i in range(2)]
        hf = place("hf", [128, HT])
        scT_at = cursor[0]
        hh = [place(f"hh{i}", [128, HT], F32R) for i in range(3)]
        hl = [place(f"hl{i}", [128, HT], F32R) for i in range(3)]
        cursor[0] = scT_at
        scT = place("scT", [128, T], F32R)
        cursor[0] = after_stage
        gs = [place(f"gs{i}", [128, HT]) for i in range(2)]
        sg = [place(f"sg{i}", [128, HT]) for i in range(2)]
        cursor[0] = after_stage + 3 * size_of([128, DC, T], F32)
        yT = place("yT", [128, DC, T])
        cursor[0] = after_stage
        khl = [place(f"khl{i}", [128, LC], F32R) for i in range(2)]
        kh1 = [place(f"kh1{i}", [CD + 1, LC], F32R) for i in range(2)]
        qh = [place(f"qh{i}", [128, NH * S], F32R) for i in range(2)]
        ql = [place(f"ql{i}", [CD + 1, NH * S], F32R) for i in range(2)]
        xyz = [place(f"xyz{i}", [128, 3, HG, S]) for i in range(2)]
        pt = [place(f"pt{i}", [KP, HT]) for i in range(PT_BUF)]
        ph = [place(f"ph{i}", [KP, HT], F32R) for i in range(PS_BUF)]
        pl = [place(f"pl{i}", [KP, HT], F32R) for i in range(PS_BUF)]
        xn3 = place("xn3", [S, D])
        x3T = place("x3T", [128, DC, S])
        nm3 = place("nm3", [128, MT, 3])
        nmx = [place(f"nmx{i}", [128, MT]) for i in range(2)]
        nmr = [place(f"nmr{i}", [MT, 128], F32R) for i in range(2)]
        xn4 = place("xn4", [S, D])
        xq = place("xq", [S, D], BF16)
        xqT = place("xqT", [128, DC, S], BF16)
        sg1 = place("sg1", [S, F1])
        h1 = place("h1", [S, F1])
        hq = place("hq", [S, F1], BF16)
        hqT = place("hqT", [128, FC, S], BF16)
        inv = [place(f"inv{i}", [S, HG]) for i in range(2)]

        ps = ctx.enter_context(nc.psum_tensor("ps", [128, 8, 512], F32))

        ld_x, ld_ctx0, ld_w0, ld_router = sem("ld_x"), sem("ld_ctx0"), sem("ld_w0"), sem("ld_router")
        ld_st1, ld_st2, ld_wo, ld_const = sem("ld_st1"), sem("ld_st2"), sem("ld_wo"), sem("ld_const")
        ld_f = [sem(f"ld_f{i}") for i in range(3)]
        ld_e = [sem(f"ld_e{i}") for i in range(EBUF)]
        ld_craw = [sem(f"ld_craw{i}") for i in range(2)]
        tails_set = sem("tails_set")
        ld_rk, ld_lnw = sem("ld_rk"), sem("ld_lnw")
        set_up, pool_step = sem("set_up"), sem("pool_step")
        dve_step = sem("dve_step")
        var_ready, rstd_ready, xn_ready = sem("var_ready"), sem("rstd_ready"), sem("xn_ready")
        w_turned, w_kept = sem("w_turned"), sem("w_kept")
        proj_done, proj_kept_a, proj_kept_v = sem("proj_done"), sem("proj_kept_a"), sem("proj_kept_v")
        st_turned, st_kept, st_product, st_product_kept = (
            sem("st_turned"), sem("st_kept"), sem("st_product"), sem("st_product_kept"))
        qb_product, qb_kept_a, qb_kept_v = sem("qb_product"), sem("qb_kept_a"), sem("qb_kept_v")
        w_abs, w_mean, w_scaled, w_quant = sem("w_abs"), sem("w_mean"), sem("w_scaled"), sem("w_quant")
        fq_turned, fq_kept = sem("fq_turned"), sem("fq_kept")
        s0_done, s0_masked, s0_max, s0_shifted, s0_exp = (
            sem("s0_done"), sem("s0_masked"), sem("s0_max"), sem("s0_shifted"), sem("s0_exp"))
        vaug_set, vT_kept, v_turned = sem("vaug_set"), sem("vT_kept"), sem("v_turned")
        p0_turned, p0_kept_a, p0_kept_v = sem("p0_turned"), sem("p0_kept_a"), sem("p0_kept_v")
        pv0_done, ao_ready, o0_turned, o0_kept, out0_done, x1_ready = (
            sem("pv0_done"), sem("ao_ready"), sem("o0_turned"), sem("o0_kept"), sem("out0_done"), sem("x1_ready"))
        var2_ready, rstd2_ready, xn2_ready, xn2_turned, xn2_kept = (
            sem("var2_ready"), sem("rstd2_ready"), sem("xn2_ready"), sem("xn2_turned"), sem("xn2_kept"))
        logits_done, top_ready, gate_ready, score_ready = (
            sem("logits_done"), sem("top_ready"), sem("gate_ready"), sem("score_ready"))
        sc_clear, sel_ready = sem("sc_clear"), sem("sel_ready")
        sc_turned, sc_kept, sc_spread, sc_spread_kept_a, sc_spread_kept_v = (
            sem("sc_turned"), sem("sc_kept"), sem("sc_spread"), sem("sc_spread_kept_a"), sem("sc_spread_kept_v"))
        xl_ready, wg_hi, wg_lo, wd_hi, wd_lo = (
            sem("xl_ready"), sem("wg_hi"), sem("wg_lo"), sem("wd_hi"), sem("wd_lo"))
        gu_done, gs_ready, silu_done, hf_ready, hh_ready, hl_ready, down_done = (
            sem("gu_done"), sem("gs_ready"), sem("silu_done"), sem("hf_ready"), sem("hh_ready"), sem("hl_ready"), sem("down_done"))
        y_kept_a, y_kept_v, y_turned, x2_ready = sem("y_kept_a"), sem("y_kept_v"), sem("y_turned"), sem("x2_ready")
        var3_ready, rstd3_ready, xn3_ready, x3_turned, x3_kept = (
            sem("var3_ready"), sem("rstd3_ready"), sem("xn3_ready"), sem("x3_turned"), sem("x3_kept"))
        kv_ready, k_turned, k_kept = (
            sem("kv_ready"), sem("k_turned"), sem("k_kept"))
        qbig_done, rope_done, q_done, q_hi, q_lo = (
            sem("qbig_done"), sem("rope_done"), sem("q_done"), sem("q_hi"), sem("q_lo"))
        m_done, m_reduced, max_ready, m_turned, m_kept = sem("m_done"), sem("m_reduced"), sem("max_ready"), sem("m_turned"), sem("m_kept")
        max_row = [sem(f"max_row{i}") for i in range(2)]
        s_done, ph_ready, pl_ready, pv_done = (
            sem("s_done"), sem("ph_ready"), sem("pl_ready"), sem("pv_done"))
        sums_kept, sums_turned, sums_inverted, c_kept, sum_spread, c_ready, o_done, x3_ready = (
            sem("sums_kept"), sem("sums_turned"), sem("sums_inverted"), sem("c_kept"), sem("sum_spread"), sem("c_ready"), sem("o_done"), sem("x3_ready"))
        var4_ready, rstd4_ready, xq_ready, xq_turned, xq_kept = (
            sem("var4_ready"), sem("rstd4_ready"), sem("xq_ready"), sem("xq_turned"), sem("xq_kept"))
        g_done, u_done, silu1_done, h1_part, h1_square = (
            sem("g_done"), sem("u_done"), sem("silu1_done"), sem("h1_part"), sem("h1_square"))
        varh_ready, rstdh_ready, hq_ready, hq_turned, hq_kept = (
            sem("varh_ready"), sem("rstdh_ready"), sem("hq_ready"), sem("hq_turned"), sem("hq_kept"))
        down1_done, y_ready = sem("down1_done"), sem("y_ready")
        y_stored = [sem(f"y_stored{i}") for i in range(2)]

        SET_UP = 6 + NE
        LG_AT = 400
        ST1 = 16
        block = ctx.enter_context(nc.Block())

        def load_expert(sp, e):
            g, d, s = egu[e % EBUF][:, :, :, :, :].rearrange("p c a m q -> p c a (m q)"), edn[e % EBUF], ld_e[e % EBUF]
            if e == 0:
                sp.dma_start(g[:, :, 0, :], sh_gate.rearrange("(c p) n -> p c n", p=128)).then_inc(s, 16)
                sp.dma_start(g[:, :, 1, :], sh_up.rearrange("(c p) n -> p c n", p=128)).then_inc(s, 16)
                sp.dma_start(d[:, :, :], sh_down.rearrange("(m p) n -> p m n", p=128)).then_inc(s, 16)
            else:
                sp.dma_start(egu[e % EBUF][:, :, :, :, :].rearrange("p c a m q -> p c (a m q)"),
                             gate_up[e - 1].rearrange("(c p) n -> p c n", p=128)).then_inc(s, 16)
                sp.dma_start(d[:, :, :], down[e - 1].rearrange("(m p) n -> p m n", p=128)).then_inc(s, 16)

        def load_ternary(sp, i):
            if i:
                sp.wait_ge(w_scaled, i)
            dst = fw[:, :].rearrange("p (r n) -> p r n", r=2 if i == 2 else FC)
            sp.dma_start(dst, (fg, fu, fd)[i].rearrange("(r p) n -> p r n", p=128)).then_inc(ld_f[i], 16)

        def expert_loaded(e):
            return 32 * (e // EBUF + 1) + (16 if e % EBUF == 0 else 0)

        def split_slot(k):
            i = k // 2 + (k % 2 == 0)
            return i if 2 <= i < CHUNKS else None

        def load_keys(sp, b):
            if b >= 2:
                sp.wait_ge(kv_ready, KT // 2 * (b - 1))
            c = craw[b % 2]
            sp.dma_start(c[0:KP - 1, :, :], ctx_in[b, 0:(KP - 1) * KT, :].rearrange("(p t) d -> p t d", t=KT)).then_inc(ld_craw[b % 2], 16)
            sp.dma_start(c[KP - 1:KP, 0:KL, :], ctx_in[b, (KP - 1) * KT:LC, :].rearrange("(p t) d -> p t d", t=KL)).then_inc(ld_craw[b % 2], 16)

        def store_y(sp, b):
            sp.wait_ge(y_ready, b + 1)
            sp.dma_start(out[b], y[b % 2][:, :]).then_inc(y_stored[b % 2], 16)

        @block.sync
        def _(sp):
            sp.dma_start(x_sb[:, :, :], x.rearrange("b s d -> s b d")).then_inc(ld_x, 16)
            sp.dma_start(wq_n[:, :, :], wq0.rearrange("(r p) d -> p r d", p=128)).then_inc(ld_w0, 16)
            sp.dma_start(wkv_n[:, :, :], wkv0.rearrange("(r p) d -> p r d", p=128)).then_inc(ld_w0, 16)
            sp.dma_start(wout_n[:, :, :], wout0.rearrange("(r p) d -> p r d", p=128)).then_inc(ld_w0, 16)
            sp.dma_start(ctx0[:, :, :], ctx_in[:, 0:S, :].rearrange("b s d -> s b d")).then_inc(ld_ctx0, 16)
            sp.dma_start(router_n[:, :], router).then_inc(ld_router, 16)
            sp.dma_start(wkr_n[:, :, :], wkr.rearrange("h d r -> d h r")).then_inc(ld_st1, 16)
            sp.dma_start(wqr_n[:, :, :], wqr.rearrange("h (a q) r -> q (h a) r", a=2)).then_inc(ld_st1, 16)
            sp.dma_start(kckv_n[:, :, :], kckv.rearrange("h k d -> k h d")).then_inc(ld_wo, 16)
            sp.dma_start(wo_n[:, :, :], wo1.rearrange("(r p) k -> p r k", p=128)).then_inc(ld_wo, 16)
            sp.dma_start(ropeq[:, :, :], rope_q).then_inc(ld_const, 16)
            sp.wait_ge(st_product, ST1)
            sp.wait_ge(st_kept, ST1)
            sp.dma_start(wq1_n[:, :, :], wq1.rearrange("(h k) d -> k h d", k=QK)).then_inc(ld_st2, 16)
            sp.dma_start(kcq_n[:, :, :], kcq.rearrange("h k q -> k h q")).then_inc(ld_st2, 16)
            load_ternary(sp, 0)
            sp.wait_ge(out0_done, B)
            sp.wait_ge(o0_kept, B)
            sp.wait_ge(x1_ready, B)
            sp.wait_ge(xn2_turned, B)
            for e in range(EBUF):
                load_expert(sp, e)
            sp.wait_ge(qb_product, NH)
            for dst, src in ((ropekc, rope_kc), (ropeks, rope_ks)):
                sp.dma_start(dst[0:KP - 1, :, :], src[0:(KP - 1) * KT, :].rearrange("(p t) d -> p t d", t=KT)).then_inc(ld_rk, 16)
                sp.dma_start(dst[KP - 1:KP, 0:KL, :], src[(KP - 1) * KT:LC, :].rearrange("(p t) d -> p t d", t=KL)).then_inc(ld_rk, 16)
            load_keys(sp, 0)
            load_keys(sp, 1)
            for e in range(EBUF, NE + 1):
                sp.wait_ge(wg_lo, FM * (e - EBUF + 1))
                sp.wait_ge(wd_lo, FM * (e - EBUF + 1))
                load_expert(sp, e)
                if e in TERNARY_AFTER:
                    load_ternary(sp, 1 + TERNARY_AFTER.index(e))
            sp.wait_ge(fq_turned, 6)
            sp.dma_start(lnw_b[:, :], lnw.rearrange("(a n) -> a n", a=1).to_broadcast([S, F1])).then_inc(ld_lnw, 16)
            for b in range(B):
                sp.wait_ge(m_kept, b + 1)
                if b >= 2:
                    sp.wait_ge(s_done, SLOTS * (b - 1))
                row = ql[b % 2][CD:CD + 1, :].bitcast(F32)
                for i0, n in ((0, MT - 1), (MT - 1, 1)):
                    w = m_rows(i0)
                    sp.dma_start(row[:, 128 * i0:128 * i0 + n * w].rearrange("a (i q) -> a i q", q=w),
                                 nmr[b % 2][i0:i0 + n, 0:w].bitcast(F32)).then_inc(max_row[b % 2], 16)
                if b + 2 < B:
                    load_keys(sp, b + 2)
                if b >= 2:
                    store_y(sp, b - 2)
            store_y(sp, B - 2)
            store_y(sp, B - 1)
            for i in range(2):
                sp.wait_ge(y_stored[i], 16 * B // 2)

        def rotate_keys(pool, step, b, j):
            c, k = craw[b % 2], kv[b % KV_BUF]
            h = CD // 2
            r, t = slice(0, key_rows(2 * j)), slice(2 * j, 2 * j + 2)
            if j == 0:
                pool.wait_ge(ld_craw[b % 2], 32 * (b // 2 + 1))
                if b >= KV_BUF:
                    pool.wait_ge(pv_done, SLOTS * (b - KV_BUF + 1))
            nc.gpsimd.tensor_tensor(kcos[r, :, :], c[r, t, :], ropekc[r, t, :], ALU.mult)
            nc.gpsimd.tensor_tensor(ksin[r, :, 0:h], c[r, t, h:CD], ropeks[r, t, 0:h], ALU.mult)
            step(nc.gpsimd.tensor_tensor(ksin[r, :, h:CD], c[r, t, 0:h], ropeks[r, t, h:CD], ALU.mult))
            step(nc.gpsimd.tensor_tensor(kraw[r, :, :], kcos[r, :, :], ksin[r, :, :], ALU.add))
            step(nc.gpsimd.tensor_copy(k[r, t, CD:2 * CD], kraw[r, :, :]))
            nc.gpsimd.tensor_tensor(k[r, t, 0:CD], kraw[r, :, :], k[r, t, CD:2 * CD].bitcast(F32), ALU.subtract)\
                .then_inc(kv_ready, 1)
            pool.wait_ge(kv_ready, KT // 2 * b + j + 1)

        def norm_x4(pool, power, b):
            pool.wait_ge(var4_ready, b + 1)
            power(rstd4[:, :], veps4[:, :], S).then_inc(rstd4_ready, 1)

        def norm_h(pool, power, b):
            pool.wait_ge(varh_ready, b + 1)
            power(rstdh[:, :], vh[:, :], S).then_inc(rstdh_ready, 1)

        @block.gpsimd
        def _(pool):
            steps = [0]

            def step(ins):
                steps[0] += 1
                ins.then_inc(pool_step, 1)
                pool.wait_ge(pool_step, steps[0])

            def power(dst, src, rows):
                return nc.gpsimd.tensor_tensor(dst, src, mhalf[0:rows, 0:src.shape[1]], ALU.pow)

            step(nc.gpsimd.memset(ident[:, :], 0.0))
            step(nc.gpsimd.affine_select(out=ident[:, :], in_=ident[:, :], compare_op=ALU.not_equal, fill=1.0,
                                         base=0, pattern=[[-1, 128]], channel_multiplier=1))
            nc.gpsimd.tensor_copy(ident_bf[:, :], ident[:, :]).then_inc(set_up, 1)
            nc.gpsimd.memset(mhalf[:, :], -0.5).then_inc(set_up, 1)
            nc.gpsimd.memset(ones[:, :], 1.0).then_inc(set_up, 1)
            nc.gpsimd.memset(wqT[:, :, :, :], 0.0).then_inc(set_up, 1)
            nc.gpsimd.memset(wkT[:, :, :], 0.0).then_inc(set_up, 1)
            for e in range(NE):
                nc.gpsimd.memset(order[:, e:e + 1], float(NE - e)).then_inc(set_up, 1)
            step(nc.gpsimd.memset(mask[:, :], 0.0))
            nc.gpsimd.affine_select(out=mask[:, :], in_=mask[:, :], compare_op=ALU.is_ge, fill=MASKED,
                                    base=0, pattern=[[-1, S]], channel_multiplier=1).then_inc(set_up, 1)
            pool.wait_ge(set_up, SET_UP)
            pool.wait_ge(var_ready, 1)
            power(rstd[:, :], veps[:, :], S).then_inc(rstd_ready, 1)
            pool.wait_ge(rstd_ready, 1)
            nc.gpsimd.memset(vaug[:, :, :, HD + 1:HS], 0.0).then_inc(vaug_set, 1)
            nc.gpsimd.memset(vaug[:, :, :, HD:HD + 1], 1.0).then_inc(vaug_set, 1)
            for i in range(B + 2):
                if i < B:
                    pool.wait_ge(s0_max, i + 1)
                    nc.gpsimd.tensor_tensor(sm[i % 2][:, :, :], sm[i % 2][:, :, :],
                                            mx0[i % 2][:, :].unsqueeze(2).to_broadcast([S, NH, S]),
                                            ALU.subtract).then_inc(s0_shifted, 1)
                if i >= 2:
                    b = i - 2
                    pool.wait_ge(var2_ready, b + 1)
                    power(rstd[:, b:b + 1], veps[:, b:b + 1], S).then_inc(rstd2_ready, 1)
            pool.wait_ge(xn2_kept, B)
            pool.wait_ge(out0_done, B)
            nc.gpsimd.memset(scT[:, :].bitcast(F32), 0.0).then_inc(sc_clear, 1)
            pool.wait_ge(sc_clear, 1)
            pool.wait_ge(qb_product, NH)
            for i in range(2):
                step(nc.gpsimd.memset(kv[i][:, :, 2 * CD:2 * CD + 1].bitcast(F32), 1.0))
            pool.wait_ge(ld_rk, 64)
            for b in range(2):
                for j in range(KT // 2):
                    rotate_keys(pool, step, b, j)
            for i in range(3):
                pool.wait_ge(w_abs, i + 1)
                nc.gpsimd.partition_all_reduce(wsum[:, i:i + 1], wcol[:, i:i + 1], 128,
                                               bass.bass_isa.ReduceOp.add).then_inc(w_mean, 1)
                pool.wait_ge(w_quant, 2 * i + 1)
                step(nc.gpsimd.tensor_scalar(fw[:, :], fw[:, :], winv[:, i:i + 1], 1.0, ALU.mult, ALU.min))
                step(nc.gpsimd.tensor_scalar(fw[:, :], fw[:, :], -1.0, ROUND, ALU.max, ALU.add))
                nc.gpsimd.tensor_scalar(fq[i][:, :], fw[:, :], ROUND, None, ALU.subtract).then_inc(w_scaled, 1)
                pool.wait_ge(w_scaled, i + 1)
                pool.wait_ge(w_quant, 2 * i + 2)
            pool.wait_ge(var3_ready, 1)
            power(rstd[:, :], veps[:, :], S).then_inc(rstd3_ready, 1)
            pool.wait_ge(fq_turned, 6)
            for i in range(2, KV_BUF):
                step(nc.gpsimd.memset(kv[i][:, :, 2 * CD:2 * CD + 1].bitcast(F32), 1.0))
            for i in range(2):
                step(nc.gpsimd.memset(nm3[:, :, :], 0.0))
                nc.gpsimd.memset(kh1[i][CD:CD + 1, :].bitcast(F32), 1.0).then_inc(tails_set, 1)
                pool.wait_ge(tails_set, i + 1)
            for b in range(B):
                for s in range(SLOTS):
                    k = SLOTS * b + s
                    pool.wait_ge(ph_ready, k + 1)
                    if k >= PS_BUF:
                        pool.wait_ge(pv_done, k - PS_BUF + 1)
                    r = slice(0, key_rows(k % KT))
                    nc.gpsimd.tensor_tensor(pl[k % PS_BUF][r, :], pt[k % PT_BUF][r, :], ph[k % PS_BUF][r, :].bitcast(F32),
                                            ALU.subtract).then_inc(pl_ready, 1)
                    if b and s == X4_SLOT:
                        pool.wait_ge(pl_ready, k + 1)
                        norm_x4(pool, power, b - 1)
                    if b and s == H_NORM_SLOT:
                        pool.wait_ge(pl_ready, k + 1)
                        norm_h(pool, power, b - 1)
                    if b + 2 < B and s in ROTATE_SLOT:
                        rotate_keys(pool, step, b + 2, ROTATE_SLOT.index(s))
            pool.wait_ge(pl_ready, SLOTS * B)
            norm_x4(pool, power, B - 1)
            norm_h(pool, power, B - 1)

        @block.tensor
        def _(pe):
            mm, turn = nc.tensor.matmul, nc.tensor.transpose

            def job_bank(n):
                if n >= 4:
                    pe.wait_ge(w_kept, n - 3)
                return ps[:, 4 + n % 4, :]

            pe.wait_ge(set_up, SET_UP)
            pe.wait_ge(ld_w0, 48)
            for n, src in ((0, wq_n), (2, wout_n)):
                if n == 2:
                    o = job_bank(1)
                    for r in range(4):
                        last = turn(o[0:CD, 128 * r:128 * r + 128], wkv_n[:, r, :], ident[:, :])
                    last.then_inc(w_turned, 1)
                o = job_bank(n)
                for c in range(DC):
                    for r in range(DC):
                        last = turn(o[:, (DC * c + r) * 128:(DC * c + r + 1) * 128],
                                    src[:, r, 128 * c:128 * c + 128], ident[:, :])
                last.then_inc(w_turned, 1)
            pe.wait_ge(ld_ctx0, 16)
            for n in (3, 4):
                o = job_bank(n)
                for j in range(4):
                    last = turn(o[0:CD, S * j:S * j + S], ctx0[:, 4 * (n - 3) + j, :], ident[0:S, 0:S])
                last.then_inc(w_turned, 1)
            pe.wait_ge(ld_router, 16)
            o = job_bank(5)
            for c in range(DC):
                last = turn(o[:, NE * c:NE * c + NE], router_n[:, 128 * c:128 * c + 128], ident[0:NE, 0:NE])
            last.then_inc(w_turned, 1)
            for j in range(4):
                pe.wait_ge(xn_ready, 2 * j + 2)
                o = job_bank(6 + j)
                for c in range(DC):
                    for i in range(2):
                        last = turn(o[:, (2 * c + i) * S:(2 * c + i + 1) * S],
                                    xn[:, 2 * j + i, 128 * c:128 * c + 128], ident[0:S, 0:S])
                last.then_inc(w_turned, 1)

            job = 0

            def proj_bank():
                if job >= 4:
                    pe.wait_ge(proj_kept_v if job % 2 else proj_kept_a, (job - 4) // 2 + 1)
                return ps[:, job % 4, :]

            for n in range(2):
                pe.wait_ge(w_kept, 8 + 2 * n)
                for g in range(NG):
                    o = proj_bank()
                    for c in range(DC):
                        last = mm(o[:, 0:HT], wqT[:, c, g, :], xnT[:, c, HT * n:HT * n + HT], start=c == 0, stop=c == DC - 1)
                    last.then_inc(proj_done, 1)
                    job += 1
                    o = proj_bank()
                    mm(o[:, 0:HT], wkT[:, g, :], ctx0T[:, HT * n:HT * n + HT], start=True, stop=True).then_inc(proj_done, 1)
                    job += 1
            for b in range(B):
                o = proj_bank()
                mm(o[0:S, 0:D], ctx0T[:, S * b:S * b + S], wvT[:, :], start=True, stop=True).then_inc(proj_done, 1)
                job += 1

            pe.wait_ge(ld_st1, 32)
            pe.wait_ge(w_kept, 10)
            for j in range(2):
                for i in range(8):
                    last = turn(ps[0:RD, 4 + j, CD * i:CD * i + CD], wkr_n[:, 8 * j + i, :], ident[0:CD, 0:CD])
                last.then_inc(st_turned, 1)

            def stage_turn(i):
                pe.wait_ge(st_kept, i + 1 if i < 2 else i - 1 + 2)
                o = ps[:, 4 + i % 2, :]
                if i < 8:
                    for j in range(4):
                        last = turn(o[0:RD, 96 * j:96 * j + 96], wqr_n[:, 4 * i + j, :], ident[0:96, 0:96])
                else:
                    if i == 8:
                        pe.wait_ge(ld_wo, 32)
                    for a in range(2):
                        h = i - 8 + GH * a
                        for r in range(DC):
                            last = turn(o[:, (DC * a + r) * 128:(DC * a + r + 1) * 128],
                                        wo_n[:, r, QK * h:QK * h + QK], ident[:, :])
                last.then_inc(st_turned, 1)

            def stage_product(i):
                pe.wait_ge(st_kept, i + 3)
                if i >= 2:
                    pe.wait_ge(st_product_kept, i - 1)
                o = ps[:, 6 + i % 2, :]
                if i < 8:
                    for a in range(2):
                        for k in range(3):
                            last = mm(o[:, (3 * a + k) * CD:(3 * a + k + 1) * CD], lxyz[i % 2][:, a, k, :],
                                      wkrT[:, 2 * i + a, :], start=True, stop=True)
                else:
                    for a in range(2):
                        h = i - 8 + GH * a
                        last = mm(o[CD * a:CD * a + CD, 0:D], kckv_n[:, h, :], woT[i % 2][:, a, :], start=True, stop=True)
                last.then_inc(st_product, 1)

            stage_turn(0)
            for i in range(ST1):
                if i + 1 < ST1:
                    stage_turn(i + 1)
                stage_product(i)

            def logits(b):
                for c in range(DC):
                    last = mm(ps[0:S, 6, LG_AT + NE * b:LG_AT + NE * b + NE], xnT[:, c, S * b:S * b + S], routerT[:, c, :],
                              start=c == 0, stop=c == DC - 1)
                return last

            def qb_head(h):
                if h == 0:
                    pe.wait_ge(ld_st2, 32)
                for c in range(DC):
                    last = mm(ps[:, h % 4, QB * c:QB * c + QB], wq1_n[:, h, 128 * c:128 * c + 128], kcq_n[:, h, :],
                              start=True, stop=True)
                last.then_inc(qb_product, 1)

            pe.wait_ge(vaug_set, 2)
            pe.wait_ge(proj_kept_a, 12)
            pe.wait_ge(proj_kept_v, 12)
            pe.wait_ge(st_product_kept, ST1)
            for step in range(B + 3):
                if step < B:
                    b = step
                    if b:
                        pe.wait_ge(s0_masked, b)
                    if b >= 2:
                        pe.wait_ge(qb_kept_a, b - 1)
                        pe.wait_ge(qb_kept_v, b - 1)
                    tok = slice(S * b, S * b + S)
                    for g in range(NG):
                        for i in range(HG):
                            p = slice(HS * i, HS * i + HS)
                            last = mm(ps[0:S, i, S * g:S * g + S], qT[p, g, tok], kT[p, g, tok], start=True, stop=True)
                    last.then_inc(s0_done, 1)
                if 1 <= step <= B:
                    b = step - 1
                    pe.wait_ge(s0_exp, b + 1)
                    for half in range(2):
                        if half == 1:
                            pe.wait_ge(p0_kept_a, b + 1)
                        elif b:
                            pe.wait_ge(p0_kept_v, b)
                            pe.wait_ge(ao_ready, b)
                            if step >= 4:
                                pe.wait_ge(xn2_kept, step - 3)
                        for j in range(8):
                            last = turn(ps[0:S, 4 + j // 4, S * (j % 4):S * (j % 4) + S],
                                        sm[b % 2][:, 8 * half + j, :], ident[0:S, 0:S])
                        last.then_inc(p0_turned, 1)
                    if b:
                        pe.wait_ge(vT_kept, b)
                    if b >= 3:
                        logits(b - 3)
                    pe.wait_ge(s0_masked, min(step + 1, B))
                    qb_head(2 * b)
                    qb_head(2 * b + 1)
                    pe.wait_ge(p0_kept_v, b + 1)
                    for i in range(HG):
                        for g in range(NG):
                            h = HG * g + i
                            last = mm(ps[HS * i:HS * i + HS, 6, S * g:S * g + S], vaug[:, b, h, :],
                                      pT[:, NG * i + g, :], start=True, stop=True)
                    last.then_inc(pv0_done, 1)
                if 2 <= step <= B + 1:
                    b = step - 2
                    pe.wait_ge(ao_ready, b + 1)
                    for c in range(DC):
                        last = turn(ps[:, 4, S * c:S * c + S], ao[:, 128 * c:128 * c + 128], ident[0:S, 0:S])
                    last.then_inc(o0_turned, 1)
                if step >= 3:
                    b = step - 3
                    pe.wait_ge(xn2_ready, b + 1)
                    if b:
                        pe.wait_ge(xn2_kept, b)
                    for c in range(DC):
                        last = turn(ps[:, 5, S * c:S * c + S], xn[:, b, 128 * c:128 * c + 128], ident[0:S, 0:S])
                    last.then_inc(xn2_turned, 1)
                if 2 <= step <= B + 1:
                    b = step - 2
                    pe.wait_ge(o0_kept, b + 1)
                    if b:
                        pe.wait_ge(x1_ready, b)
                    for c in range(DC):
                        last = mm(ps[0:S, 7, 0:D], oT[:, c, :], woutT[:, c, :], start=c == 0, stop=c == DC - 1)
                    last.then_inc(out0_done, 1)
                if 1 <= step <= B:
                    b = step - 1
                    pe.wait_ge(vT_kept, b + 1)
                    for g in range(NG):
                        last = turn(ps[0:S, 4, 128 * g:128 * g + 128], vT[:, S * g:S * g + S], ident[:, :])
                    last.then_inc(v_turned, 1)

            pe.wait_ge(xn2_kept, B)
            pe.wait_ge(vT_kept, B)
            for b in range(B - 3, B):
                last = logits(b)
            last.then_inc(logits_done, 1)
            pe.wait_ge(score_ready, 1)
            for b in range(B):
                last = turn(ps[0:NE, 4 + b // 4, S * (b % 4):S * (b % 4) + S], score[:, b, :], ident[0:S, 0:S])
            last.then_inc(sc_turned, 1)
            pe.wait_ge(sel_ready, 1)
            pe.wait_ge(sc_kept, 1)
            for e in range(NE):
                if e >= 2:
                    pe.wait_ge(sc_spread_kept_v if e % 2 else sc_spread_kept_a, e // 2)
                for n in range(2):
                    last = mm(ps[:, 4 + 2 * (e % 2) + n, 0:HT], sel[:, e:e + 1].to_broadcast([128, 128]),
                              scT[:, HT * n:HT * n + HT], start=True, stop=True)
                last.then_inc(sc_spread, 1)
            pe.wait_ge(sc_spread_kept_a, NE // 2)
            pe.wait_ge(sc_spread_kept_v, NE // 2)
            pe.wait_ge(qb_kept_a, NH // 2)
            pe.wait_ge(qb_kept_v, NH // 2)

            pe.wait_ge(xl_ready, B)
            for k in range(ITEMS + DOWN_LAG):
                if k < ITEMS:
                    i, n = k // 2, k % 2
                    pe.wait_ge(wg_lo, i + 1)
                    if k >= 2:
                        pe.wait_ge(hf_ready, k - 1)
                    cols = slice(HT * n, HT * n + HT)
                    for a in range(2):
                        for c in range(DC):
                            hi, lo = wgh[i % 2][:, c, a, :], wgl[i % 2][:, c, a, :]
                            for p, (w, v) in enumerate(((hi, xh), (lo, xh), (hi, xl))):
                                last = mm(ps[:, 4 + 2 * a + n, 0:HT], w, v[:, c, cols],
                                          start=c == 0 and p == 0, stop=c == DC - 1 and p == 2)
                    last.then_inc(gu_done, 1)
                if k >= DOWN_LAG:
                    j = k - DOWN_LAG
                    i, n = j // 2, j % 2
                    pe.wait_ge(wd_lo, i + 1)
                    pe.wait_ge(hl_ready, j + 1)
                    for c in range(DC):
                        hi, lo = wdh[i % 2][:, 128 * c:128 * c + 128], wdl[i % 2][:, 128 * c:128 * c + 128]
                        for p, (w, v) in enumerate(((hi, hh), (lo, hh), (hi, hl))):
                            last = mm(ps[:, 2 * c + n, 0:HT], w, v[j % 3][:, :],
                                      start=j < 2 and p == 0, stop=j >= ITEMS - 2 and p == 2)
                    last.then_inc(down_done, 1)
            pe.wait_ge(y_kept_a, 2)
            pe.wait_ge(y_kept_v, 2)
            for b in range(B):
                if b >= 4:
                    pe.wait_ge(x2_ready, b - 3)
                for c in range(DC):
                    last = turn(ps[0:S, 4 + b % 4, 128 * c:128 * c + 128], yT[:, c, S * b:S * b + S], ident[:, :])
                last.then_inc(y_turned, 1)
            for n in range(6):
                i, half = n // 2, n % 2
                pe.wait_ge(w_scaled, i + 1)
                if n >= 4:
                    pe.wait_ge(fq_kept, n - 3)
                o = ps[:, n % 4, :].bitcast(BF16)
                src = fq[i][:, :].rearrange("p (r n) -> p r n", r=2 if i == 2 else FC)
                for j in range(8):
                    if i < 2:
                        part = src[:, j, 128 * half:128 * half + 128]
                    else:
                        part = src[:, j % 2, 128 * (4 * half + j // 2):128 * (4 * half + j // 2) + 128]
                    last = turn(o[:, 128 * j:128 * j + 128], part, ident_bf[:, :])
                last.then_inc(fq_turned, 1)
            pe.wait_ge(fq_kept, 6)

            def turn_x3(b):
                pe.wait_ge(xn3_ready, b + 1)
                for c in range(DC):
                    last = turn(ps[:, 4, S * c:S * c + S], xn3[:, 128 * c:128 * c + 128], ident[0:S, 0:S])
                last.then_inc(x3_turned, 1)

            def q_big(b, g):
                if g == 0:
                    pe.wait_ge(x3_kept, b + 1)
                if NG * b + g:
                    pe.wait_ge(rope_done, NG * b + g)
                for i in range(HG):
                    h = HG * g + i
                    for c in range(DC):
                        mm(ps[:, 4, S * i:S * i + S], wqb[:, c, h, 0:128], x3T[:, c, :], start=c == 0, stop=c == DC - 1)
                for i in range(HG // 2):
                    h = HG * g + 2 * i
                    for c in range(DC):
                        last = mm(ps[:, 5, S * i:S * i + S], wqt[:, c, h:h + 2, :].rearrange("p h q -> p (h q)"),
                                  x3T[:, c, :], start=c == 0, stop=c == DC - 1)
                last.then_inc(qbig_done, 1)

            def q_latent(b, g):
                k = NG * b + g
                pe.wait_ge(rope_done, k + 1)
                if k:
                    pe.wait_ge(q_lo, k)
                if g == 2 and b >= 2:
                    pe.wait_ge(x3_ready, b - 1)
                for i in range(HG):
                    h = HG * g + i
                    for j in range(3):
                        last = mm(ps[0:CD, 6, S * i:S * i + S], amat[:, h, j, :],
                                  xyz[k % 2][:, j, i, :], start=j == 0, stop=j == 2)
                last.then_inc(q_done, 1)

            def turn_keys(b, j):
                pe.wait_ge(kv_ready, KT // 2 * b + 2 * j + 2)
                if 3 * b + j:
                    pe.wait_ge(k_kept, 3 * b + j)
                if j == 0 and b >= 2:
                    pe.wait_ge(c_ready, NG * (b - 1))
                for t in range(4 * j, 4 * j + 4):
                    at = key_start(t) - key_start(4 * j)
                    last = turn(ps[:, 7, at:at + key_rows(t)], kv[b % KV_BUF][0:key_rows(t), t, 0:2 * CD].bitcast(F32),
                                ident[0:key_rows(t), 0:key_rows(t)])
                last.then_inc(k_turned, 1)

            def max_tile(b, i):
                k = MT * b + i
                if i == 0:
                    pe.wait_ge(k_kept, 3 * (b + 1))
                if i == 0 or b == 0:
                    pe.wait_ge(q_lo, NG * b + (groups_for(i) if b == 0 and i < EARLY else NG))
                w = m_rows(i)
                before = k - 2 if b == 0 and i > EARLY else k - 1
                for n in range(3):
                    if before >= 0:
                        pe.wait_ge(m_reduced, 3 * before + n + 1)
                    mm(ps[0:w, max_bank(b, i) + n, 0:MN], qh[b % 2][:, 128 * i:128 * i + w],
                              khl[b % 2][:, MSTART[n]:MSTART[n] + MN], start=True, stop=True).then_inc(m_done, 1)

            def turn_max(b):
                pe.wait_ge(tails_set, 2)
                pe.wait_ge(max_ready, b + 1)
                turn(ps[0:MT, 6, 0:128], nmx[b % 2][:, :], ident[:, :]).then_inc(m_turned, 1)

            def scores(k):
                b, c, t = k // SLOTS, k // KT % NG, k % KT
                if k % SLOTS == 0:
                    pe.wait_ge(max_row[b % 2], 32 * (b // 2 + 1))
                if k >= 2:
                    pe.wait_ge(ph_ready, k - 1)
                keys = slice(key_start(t), key_start(t) + key_rows(t))
                for lhs, rhs, first in ((khl[b % 2], qh[b % 2], True), (kh1[b % 2], ql[b % 2], False)):
                    last = mm(ps[0:key_rows(t), k % 2, 0:HT], lhs[:, keys], rhs[:, HT * c:HT * c + HT],
                              start=first, stop=not first)
                last.then_inc(s_done, 1)

            def values(k):
                b, t, q = k // SLOTS, k % KT, k // KT
                pe.wait_ge(ph_ready, k + 1)
                if t == 0 and q >= 2:
                    pe.wait_ge(c_kept, q - 1)
                r, bank = slice(0, key_rows(t)), ps[:, 2 + q % 2, 0:HT]
                w, hi, lo = kv[b % KV_BUF], ph[k % PS_BUF], pl[k % PS_BUF]
                mm(bank[0:CD + 1, :], w[r, t, CD:2 * CD + 1], hi[r, :], start=t == 0, stop=False)
                mm(bank[0:CD, :], w[r, t, 0:CD], hi[r, :], start=False, stop=False)
                pe.wait_ge(pl_ready, k + 1)
                mm(bank[0:CD + 1, :], w[r, t, CD:2 * CD + 1], lo[r, :], start=False, stop=t == KT - 1).then_inc(pv_done, 1)

            def turn_sums(q):
                pe.wait_ge(sums_kept, q + 1)
                if q:
                    pe.wait_ge(c_ready, q)
                if q % NG == 0 and q // NG + 1 < B:
                    pe.wait_ge(k_kept, 3 * (q // NG + 2))
                for i in range(HG):
                    last = mm(ps[0:S, 7, i:i + 1], sums[q % 2][CD:CD + 1, S * i:S * i + S], ones[CD:CD + 1, 0:1],
                              start=True, stop=True)
                last.then_inc(sums_turned, 1)

            def spread_sums(q):
                a = q % NG // 2
                pe.wait_ge(sums_inverted, q + 1)
                for i in range(HG):
                    last = mm(ps[CD * a:CD * a + CD, 7, S * i:S * i + S], inv[q % 2][:, i:i + 1].to_broadcast([S, CD]),
                              ident[0:S, 0:S], start=True, stop=True)
                last.then_inc(sum_spread, 1)

            def attention_out(b):
                pe.wait_ge(c_ready, NG * (b + 1))
                if b + 2 < B:
                    pe.wait_ge(q_lo, NG * (b + 2) + 2)
                for h in range(GH):
                    last = mm(ps[0:S, 6, 0:D], ct[:, S * h:S * h + S], bmat[:, h, :], start=h == 0, stop=h == GH - 1)
                last.then_inc(o_done, 1)

            def maxima_read(b, s):
                if b + 2 < B:
                    pe.wait_ge(m_reduced, 3 * (MT * (b + 2) + sum(x < s for x in M_SLOT)))

            def turn_xq(b):
                pe.wait_ge(xq_ready, b + 1)
                maxima_read(b, XQ_SLOT)
                o = ps[:, 4, :].bitcast(BF16)
                for c in range(DC):
                    last = turn(o[:, S * c:S * c + S], xq[:, 128 * c:128 * c + 128], ident_bf[0:S, 0:S])
                last.then_inc(xq_turned, 1)

            def gate_and_up(b, half):
                maxima_read(b, GU_SLOT[half])
                if half:
                    pe.wait_ge(h1_part, 2 * b + 1)
                else:
                    pe.wait_ge(xq_kept, b + 1)
                    pe.wait_ge(x3_ready, b + 1)
                    for n in range(2):
                        for c in range(DC):
                            last = mm(ps[0:S, 5 + n, :], xqT[:, c, :], wgT[:, c, 512 * n:512 * n + 512],
                                      start=c == 0, stop=c == DC - 1)
                    last.then_inc(g_done, 1)
                for c in range(DC):
                    last = mm(ps[0:S, 4, :], xqT[:, c, :], wuT[:, c, 512 * half:512 * half + 512],
                              start=c == 0, stop=c == DC - 1)
                last.then_inc(u_done, 1)

            def turn_hq(b):
                pe.wait_ge(hq_ready, b + 1)
                maxima_read(b, HQ_SLOT)
                o = ps[:, 4, :].bitcast(BF16)
                for f in range(FC):
                    last = turn(o[:, S * f:S * f + S], hq[:, 128 * f:128 * f + 128], ident_bf[0:S, 0:S])
                last.then_inc(hq_turned, 1)

            def ffn_down(b):
                pe.wait_ge(hq_kept, b + 1)
                maxima_read(b, DOWN_SLOT)
                for f in range(FC):
                    last = mm(ps[0:S, 5, 0:D], hqT[:, f, :], wdT[:, f, :], start=f == 0, stop=f == FC - 1)
                last.then_inc(down1_done, 1)

            def feed_forward_read(b, s):
                if s > XQ_SLOT:
                    pe.wait_ge(xq_kept, b + 1)
                if s > GU_SLOT[1]:
                    pe.wait_ge(h1_part, 2 * b + 2)
                if s > HQ_SLOT:
                    pe.wait_ge(hq_kept, b + 1)
                if s > DOWN_SLOT:
                    pe.wait_ge(y_ready, b + 1)

            pe.wait_ge(x2_ready, B)
            turn_keys(0, 0)
            turn_x3(0)
            q_big(0, 0)
            turn_keys(0, 1)
            q_big(0, 1)
            q_latent(0, 0)
            turn_keys(0, 2)
            pe.wait_ge(tails_set, 2)
            q_big(0, 2)
            max_tile(0, 0)
            q_latent(0, 1)
            max_tile(0, 1)
            q_big(0, 3)
            max_tile(0, 2)
            q_latent(0, 2)
            max_tile(0, 3)
            q_latent(0, 3)
            for i in range(EARLY, MT):
                max_tile(0, i)
            turn_max(0)
            for b in range(B):
                pe.wait_ge(m_kept, b + 1)
                if b >= 2:
                    pe.wait_ge(y_ready, b - 1)
                for s in range(SLOTS):
                    k = SLOTS * b + s
                    scores(k)
                    if k >= LAG:
                        values(k - LAG)
                    if (b or s >= KT) and s % KT == TURN_AT:
                        turn_sums(NG * b + s // KT - 1)
                    if (b or s >= KT) and s % KT == SPREAD_AT:
                        spread_sums(NG * b + s // KT - 1)
                    if b + 1 < B:
                        if s == X_SLOT:
                            turn_x3(b + 1)
                        if s in BIG_SLOT:
                            q_big(b + 1, BIG_SLOT.index(s))
                        if s in LAT_SLOT:
                            q_latent(b + 1, LAT_SLOT.index(s))
                    if b + 1 < B and s in KEY_SLOT:
                        turn_keys(b + 1, KEY_SLOT.index(s))
                    if b:
                        if s == OUT_SLOT:
                            attention_out(b - 1)
                        if s == XQ_SLOT:
                            turn_xq(b - 1)
                        if s in GU_SLOT:
                            gate_and_up(b - 1, GU_SLOT.index(s))
                        if s == HQ_SLOT:
                            turn_hq(b - 1)
                        if s == DOWN_SLOT:
                            ffn_down(b - 1)
                    if b + 1 < B:
                        if s in M_SLOT:
                            if b:
                                feed_forward_read(b - 1, s)
                            max_tile(b + 1, M_SLOT.index(s))
                        if s == MX_SLOT:
                            turn_max(b + 1)
            for k in range(SLOTS * B - LAG, SLOTS * B):
                values(k)
            turn_sums(NG * B - 1)
            spread_sums(NG * B - 1)
            attention_out(B - 1)
            turn_xq(B - 1)
            gate_and_up(B - 1, 0)
            gate_and_up(B - 1, 1)
            pe.wait_ge(h1_part, 2 * B)
            turn_hq(B - 1)
            ffn_down(B - 1)

        @block.scalar
        def _(act):
            def keep(dst, src, **more):
                return nc.scalar.activation(dst, src, ACT.Copy, **more)

            act.wait_ge(set_up, SET_UP)
            for n in range(10):
                act.wait_ge(w_turned, n + 1)
                o = ps[:, 4 + n % 4, :]
                if n == 0:
                    last = keep(wqT[:, :, :, :].rearrange("p c g (i s) -> p (c g i) s", s=HS)[:, :, 0:HD],
                                o.rearrange("p (j d) -> p j d", d=HD))
                elif n == 1:
                    keep(wkT[:, :, :].rearrange("p g (i s) -> p (g i) s", s=HS)[:, :, 0:HD],
                         o[0:CD, 0:D].rearrange("p (j d) -> p j d", d=HD))
                    last = keep(wvT[:, :], o[0:CD, D:2 * D])
                elif n == 2:
                    last = keep(woutT[:, :, :].rearrange("p c n -> p (c n)"), o)
                elif n in (3, 4):
                    last = keep(ctx0T[:, HT * (n - 3):HT * (n - 2)], o[0:CD, 0:HT])
                elif n == 5:
                    last = keep(routerT[:, :, :].rearrange("p c e -> p (c e)"), o[:, 0:DC * NE])
                else:
                    j = n - 6
                    last = keep(xnT[:, :, 2 * S * j:2 * S * (j + 1)], o[:, 0:2 * DC * S].rearrange("p (c q) -> p c q", c=DC))
                last.then_inc(w_kept, 1)
            for job in range(0, 24, 2):
                act.wait_ge(proj_done, job + 1)
                o = ps[:, job % 4, :]
                if job < 16:
                    last = keep(qT[:, job // 2 % NG, HT * (job // 8):HT * (job // 8 + 1)], o[:, 0:HT])
                else:
                    last = keep(vaug[:, job - 16, :, 0:HD], o[0:S, 0:D].rearrange("p (h d) -> p h d", d=HD))
                last.then_inc(proj_kept_a, 1)
            for j in range(2):
                act.wait_ge(st_turned, j + 1)
                keep(wkrT[:, 8 * j:8 * j + 8, :].rearrange("p h d -> p (h d)"), ps[0:RD, 4 + j, :]).then_inc(st_kept, 1)
            for i in range(ST1):
                act.wait_ge(st_turned, i + 3)
                if i >= 2:
                    act.wait_ge(st_product, i - 1)
                o = ps[:, 4 + i % 2, :]
                if i < 8:
                    t = o[0:RD, 0:2 * QB].rearrange("p (a q) -> p a q", a=2)
                    l, h = lxyz[i % 2], QB // 2
                    keep(l[:, :, 0, :], t[:, :, 0:128])
                    keep(l[:, :, 1, 0:h], t[:, :, h:QB])
                    keep(l[:, :, 1, h:128], t[:, :, 0:128 - h])
                    keep(l[:, :, 2, 0:RD], t[:, :, 128:QB])
                    last = keep(l[:, :, 2, RD:128], t[:, :, 128 - h:QB - h])
                else:
                    last = keep(woT[i % 2][:, :, :].rearrange("p a n -> p (a n)"), o)
                last.then_inc(st_kept, 1)
            for step in range(B + 3):
                if 1 <= step <= B:
                    b = step - 1
                    act.wait_ge(p0_turned, 2 * b + 1)
                    if b:
                        act.wait_ge(pv0_done, b)
                    keep(pT[:, 0:8, :].rearrange("p (a j) q -> p a (j q)", a=2), ps[0:S, 4:6, 0:HT]).then_inc(p0_kept_a, 1)
                if step < B:
                    act.wait_ge(s0_shifted, step + 1)
                    nc.scalar.activation(sm[step % 2][:, :, :], sm[step % 2][:, :, :], ACT.Exp, scale=HD ** -0.5)\
                      .then_inc(s0_exp, 1)
                if 1 <= step <= B:
                    h = 2 * (step - 1)
                    act.wait_ge(qb_product, h + 1)
                    o = ps[:, h % 4, 0:DC * QB].rearrange("p (c q) -> p c q", c=DC)
                    keep(wqb[:, :, h, :], o[:, :, 0:128])
                    keep(wqt[:, :, h, :], o[:, :, 128:QB]).then_inc(qb_kept_a, 1)
                if 1 <= step <= B:
                    act.wait_ge(pv0_done, step)
                    if step >= 2:
                        act.wait_ge(v_turned, step - 1)
                    keep(vT[:, :], ps[:, 6, 0:HT]).then_inc(vT_kept, 1)
                if 2 <= step <= B + 1:
                    act.wait_ge(o0_turned, step - 1)
                    keep(oT[:, :, :].rearrange("p c q -> p (c q)"), ps[:, 4, 0:DC * S]).then_inc(o0_kept, 1)
                if step >= 3:
                    b = step - 3
                    act.wait_ge(xn2_turned, b + 1)
                    o = ps[:, 5, 0:DC * S].rearrange("p (c q) -> p c q", c=DC)
                    keep(xnT[:, :, S * b:S * b + S], o)
                    keep(xh[:, :, S * b:S * b + S], o).then_inc(xn2_kept, 1)
            act.wait_ge(top_ready, 1)
            nc.scalar.activation(gatev[:, :], top[:, :], ACT.Sigmoid).then_inc(gate_ready, 1)
            def split_gate_up(i):
                e, m = i // FM, i % FM
                act.wait_ge(ld_e[e % EBUF], expert_loaded(e))
                if i >= 2:
                    act.wait_ge(gu_done, 2 * i - 2)
                keep(wgh[i % 2][:, :, :, :], egu[e % EBUF][:, :, :, m, :]).then_inc(wg_hi, 1)

            def split_down(i):
                e, m = i // FM, i % FM
                if i >= 2:
                    act.wait_ge(down_done, 2 * i - 2)
                keep(wdh[i % 2][:, :], edn[e % EBUF][:, m, :]).then_inc(wd_hi, 1)

            for e in range(0, NE, 2):
                act.wait_ge(sc_spread, e + 1)
                keep(scB[:, e, :].rearrange("p (n q) -> p n q", n=2), ps[:, 4:6, 0:HT]).then_inc(sc_spread_kept_a, 1)
            for i in range(2):
                split_gate_up(i)
                split_down(i)
            for k in range(ITEMS):
                i = split_slot(k)
                if i is not None:
                    (split_down if k % 2 else split_gate_up)(i)
                if k < 2 * FM:
                    act.wait_ge(gu_done, k + 1)
                    src = ps[:, 4 + k % 2, 0:HT]
                else:
                    act.wait_ge(gs_ready, k + 1 - 2 * FM)
                    src = gs[k % 2][:, :]
                nc.scalar.activation(sg[k % 2][:, :], src, ACT.Silu).then_inc(silu_done, 1)
                act.wait_ge(hf_ready, k + 1)
                if k >= 3:
                    act.wait_ge(down_done, k - 2)
                keep(hh[k % 3][:, :], hf[:, :]).then_inc(hh_ready, 1)
            for n in range(2):
                act.wait_ge(down_done, ITEMS - 1 + n)
                keep(yT[:, 0, HT * n:HT * n + HT], ps[:, n, 0:HT]).then_inc(y_kept_a, 1)
            for n in range(6):
                i, half = n // 2, n % 2
                act.wait_ge(fq_turned, n + 1)
                o = ps[:, n % 4, :].bitcast(BF16)
                if i < 2:
                    last = keep((wgT, wuT)[i][:, half, :], o)
                else:
                    last = keep(wdT[:, 4 * half:4 * half + 4, :].rearrange("p f n -> p (f n)"), o)
                last.then_inc(fq_kept, 1)

            def keep_x3(b):
                act.wait_ge(x3_turned, b + 1)
                keep(x3T[:, :, :].rearrange("p c q -> p (c q)"), ps[:, 4, 0:DC * S]).then_inc(x3_kept, 1)

            def keep_q(b, g):
                k = NG * b + g
                act.wait_ge(q_done, k + 1)
                if g == 0 and b >= 2:
                    act.wait_ge(s_done, SLOTS * (b - 1))
                for p in (0, CD):
                    last = nc.scalar.activation(qh[b % 2][p:p + CD, HT * g:HT * g + HT], ps[0:CD, 6, 0:HT], ACT.Copy)
                last.then_inc(q_hi, 1)

            def keep_keys(b, j):
                act.wait_ge(k_turned, 3 * b + j + 1)
                if j == 0 and b >= 2:
                    act.wait_ge(s_done, SLOTS * (b - 1))
                k0 = key_start(4 * j)
                n = key_start(4 * j + 4) - k0
                keep(khl[b % 2][:, k0:k0 + n], ps[:, 7, 0:n])
                keep(kh1[b % 2][0:CD, k0:k0 + n], ps[CD:128, 7, 0:n]).then_inc(k_kept, 1)

            def keep_max(b):
                act.wait_ge(m_turned, b + 1)
                if b >= 2:
                    act.wait_ge(max_row[b % 2], 32 * (b // 2))
                nc.scalar.activation(nmr[b % 2][:, :], ps[0:MT, 6, 0:128], ACT.Copy).then_inc(m_kept, 1)

            def keep_context(q):
                act.wait_ge(pv_done, KT * (q + 1))
                if q >= 2:
                    act.wait_ge(sums_turned, q - 1)
                if q >= NG:
                    act.wait_ge(c_ready, q - NG + 1)
                keep(sums[q % 2][CD:CD + 1, :], ps[CD:CD + 1, 2 + q % 2, 0:HT]).then_inc(sums_kept, 1)
                a = q % NG // 2
                keep(ctu[CD * a:CD * a + CD, HT * (q % 2):HT * (q % 2) + HT], ps[0:CD, 2 + q % 2, 0:HT]).then_inc(c_kept, 1)

            def keep_xq(b):
                act.wait_ge(xq_turned, b + 1)
                o = ps[:, 4, :].bitcast(BF16)
                keep(xqT[:, :, :].rearrange("p c q -> p (c q)"), o[:, 0:DC * S]).then_inc(xq_kept, 1)

            def silu_gate(b):
                act.wait_ge(g_done, b + 1)
                if b:
                    act.wait_ge(hq_ready, b)
                nc.scalar.activation(sg1[:, :].rearrange("p (n q) -> p n q", n=2), ps[0:S, 5:7, :], ACT.Silu,
                                     scale=qsc[:, 2:3]).then_inc(silu1_done, 1)

            def square_h(b):
                act.wait_ge(h1_part, 2 * b + 2)
                nc.scalar.activation(sg1[:, :], h1[:, :], ACT.Square, accum_out=ssq[:, 0:1]).then_inc(h1_square, 1)

            def turn_hq(b):
                act.wait_ge(hq_turned, b + 1)
                o = ps[:, 4, :].bitcast(BF16)
                keep(hqT[:, :, :].rearrange("p f q -> p (f q)"), o[:, 0:FC * S]).then_inc(hq_kept, 1)

            keep_keys(0, 0)
            keep_x3(0)
            keep_keys(0, 1)
            keep_q(0, 0)
            keep_keys(0, 2)
            for g in range(1, NG):
                keep_q(0, g)
            keep_max(0)
            for b in range(B):
                for s in range(SLOTS):
                    k = SLOTS * b + s
                    act.wait_ge(s_done, k + 1)
                    if k >= PT_BUF:
                        act.wait_ge(pl_ready, k - PT_BUF + 1)
                    if k >= PS_BUF:
                        act.wait_ge(pv_done, k - PS_BUF + 1)
                    rows = key_rows(k % KT)
                    nc.scalar.activation(pt[k % PT_BUF][0:rows, :], ps[0:rows, k % 2, 0:HT], ACT.Exp)
                    nc.scalar.activation(ph[k % PS_BUF][0:rows, :], ps[0:rows, k % 2, 0:HT], ACT.Exp).then_inc(ph_ready, 1)
                    if b + 1 < B:
                        if s == X_SLOT:
                            keep_x3(b + 1)
                        if s in KEY_SLOT:
                            keep_keys(b + 1, KEY_SLOT.index(s))
                        if s in LAT_SLOT:
                            keep_q(b + 1, LAT_SLOT.index(s))
                    if (b or s >= KT) and s % KT == KEEP_AT:
                        keep_context(NG * b + s // KT - 1)
                    if b:
                        if s == XQ_SLOT:
                            keep_xq(b - 1)
                        if s == GU_SLOT[0]:
                            silu_gate(b - 1)
                        if s == SQ_SLOT:
                            square_h(b - 1)
                        if s == HQ_SLOT:
                            turn_hq(b - 1)
                    if b + 1 < B and s == MX_SLOT:
                        keep_max(b + 1)
            keep_context(NG * B - 1)
            keep_xq(B - 1)
            silu_gate(B - 1)
            square_h(B - 1)
            turn_hq(B - 1)

        @block.vector
        def _(dve):
            steps = [0]
            tt, ts, stt = nc.vector.tensor_tensor, nc.vector.tensor_scalar, nc.vector.scalar_tensor_tensor

            def step(ins):
                steps[0] += 1
                ins.then_inc(dve_step, 1)
                dve.wait_ge(dve_step, steps[0])

            dve.wait_ge(ld_x, 16)
            for b in range(B):
                last = nc.vector.bn_stats(stats[:, b, :], x_sb[:, b, :])
            step(last)
            for b in range(B):
                last = nc.vector.bn_aggr(mv[:, b, :], stats[:, b, :])
            step(last)
            dve.wait_ge(set_up, SET_UP)
            ts(veps[:, :], mv[:, :, 1], LN_EPS, None, ALU.add).then_inc(var_ready, 1)
            dve.wait_ge(rstd_ready, 1)
            for b in range(B):
                ts(xn[:, b, :], x_sb[:, b, :], mv[:, b, 0:1], rstd[:, b:b + 1], ALU.subtract, ALU.mult).then_inc(xn_ready, 1)
            for job in range(1, 24, 2):
                dve.wait_ge(proj_done, job + 1)
                o = ps[:, job % 4, :]
                if job < 16:
                    last = nc.vector.tensor_copy(kT[:, job // 2 % NG, HT * (job // 8):HT * (job // 8 + 1)], o[:, 0:HT])
                else:
                    last = nc.vector.tensor_copy(vaug[:, job - 16, :, 0:HD], o[0:S, 0:D].rearrange("p (h d) -> p h d", d=HD))
                last.then_inc(proj_kept_v, 1)
            for i in range(ST1):
                dve.wait_ge(st_product, i + 1)
                o = ps[:, 6 + i % 2, :]
                if i < 8:
                    last = nc.vector.tensor_copy(amat[:, 2 * i:2 * i + 2, :, :].rearrange("p a j d -> p (a j d)"), o[:, 0:6 * CD])
                else:
                    last = nc.vector.tensor_copy(bmat[:, i - 8, :], o[:, 0:D])
                last.then_inc(st_product_kept, 1)

            dve.wait_ge(set_up, SET_UP)
            tt(sel[:, :], ident[:, 0:NE], ident[:, LO_ROW:LO_ROW + NE], ALU.add).then_inc(sel_ready, 1)

            for s in range(B + 3):
                if s < B:
                    dve.wait_ge(s0_done, s + 1)
                    if s >= 2:
                        dve.wait_ge(p0_turned, 2 * (s - 1))
                    m = sm[s % 2]
                    tt(m[:, :, :].rearrange("p (i g) k -> p i g k", i=HG),
                       ps[0:S, 0:HG, 0:HT].rearrange("p i (g k) -> p i g k", g=NG),
                       mask[:, :].unsqueeze(1).unsqueeze(1).to_broadcast([S, HG, NG, S]), ALU.add).then_inc(s0_masked, 1)
                    dve.wait_ge(s0_masked, s + 1)
                    nc.vector.tensor_reduce(mx0[s % 2][:, :], m[:, :, :], AX.X, ALU.max).then_inc(s0_max, 1)
                if 1 <= s <= B:
                    b = s - 1
                    dve.wait_ge(p0_turned, 2 * b + 2)
                    if b:
                        dve.wait_ge(pv0_done, b)
                    nc.vector.tensor_copy(pT[:, 8:16, :].rearrange("p (a j) q -> p a (j q)", a=2), ps[0:S, 4:6, 0:HT])\
                      .then_inc(p0_kept_v, 1)
                    h = 2 * b + 1
                    dve.wait_ge(qb_product, h + 1)
                    o = ps[:, h % 4, 0:DC * QB].rearrange("p (c q) -> p c q", c=DC)
                    nc.vector.tensor_copy(wqb[:, :, h, :], o[:, :, 0:128])
                    nc.vector.tensor_copy(wqt[:, :, h, :], o[:, :, 128:QB]).then_inc(qb_kept_v, 1)
                if 2 <= s <= B + 1:
                    b = s - 2
                    dve.wait_ge(out0_done, b + 1)
                    tt(x_sb[:, b, :], x_sb[:, b, :], ps[0:S, 7, 0:D], ALU.add).then_inc(x1_ready, 1)
                    dve.wait_ge(x1_ready, b + 1)
                    step(nc.vector.bn_stats(stats[:, b, :], x_sb[:, b, :]))
                    step(nc.vector.bn_aggr(mv[:, b, :], stats[:, b, :]))
                    ts(veps[:, b:b + 1], mv[:, b, 1:2], LN_EPS, None, ALU.add).then_inc(var2_ready, 1)
                    dve.wait_ge(rstd2_ready, b + 1)
                    ts(xn[:, b, :], x_sb[:, b, :], mv[:, b, 0:1], rstd[:, b:b + 1], ALU.subtract, ALU.mult).then_inc(xn2_ready, 1)
                if s >= 3:
                    b = s - 3
                    dve.wait_ge(xn2_kept, b + 1)
                    own = slice(S * b, S * b + S)
                    tt(xl[:, :, own], xnT[:, :, own], xh[:, :, own].bitcast(F32), ALU.subtract).then_inc(xl_ready, 1)
                if 1 <= s <= B:
                    b = s - 1
                    dve.wait_ge(v_turned, b + 1)
                    if b:
                        dve.wait_ge(o0_turned, b)
                    o = ps[0:S, 4, :].rearrange("p (h d) -> p h d", d=HS)
                    step(nc.vector.reciprocal(rec0[:, :], o[:, :, HD]))
                    tt(ao[:, :].rearrange("p (h d) -> p h d", d=HD), o[:, :, 0:HD],
                       rec0[:, :].unsqueeze(2).to_broadcast([S, NH, HD]), ALU.mult).then_inc(ao_ready, 1)

            dve.wait_ge(logits_done, 1)
            lg = ps[0:S, 6, LG_AT:LG_AT + B * NE].rearrange("p (b e) -> p b e", e=NE)

            def over(v):
                return v.unsqueeze(2).to_broadcast([S, B, NE])

            nc.vector.tensor_reduce(top[:, :], lg, AX.X, ALU.max).then_inc(top_ready, 1)
            dve.wait_ge(top_ready, 1)
            step(tt(eq[:, :, :], lg, over(top[:, :]), ALU.is_equal))
            step(tt(cand[:, :, :], eq[:, :, :], order[:, :].unsqueeze(1).to_broadcast([S, B, NE]), ALU.mult))
            step(nc.vector.tensor_reduce(pick[:, :], cand[:, :, :], AX.X, ALU.max))
            step(tt(eq[:, :, :], cand[:, :, :], over(pick[:, :]), ALU.is_equal))
            dve.wait_ge(gate_ready, 1)
            tt(score[:, :, :], eq[:, :, :], over(gatev[:, :]), ALU.mult).then_inc(score_ready, 1)
            dve.wait_ge(sc_clear, 1)
            dve.wait_ge(sc_turned, 1)
            turned = ps[0:NE, 4:6, 0:HT]
            hi, lo = scT[0:NE, :], scT[LO_ROW:LO_ROW + NE, :]
            step(nc.vector.tensor_copy(hi.rearrange("p (n q) -> p n q", n=2), turned))
            tt(lo.rearrange("p (n q) -> p n q", n=2), turned, hi.bitcast(F32).rearrange("p (n q) -> p n q", n=2),
               ALU.subtract).then_inc(sc_kept, 1)

            def split_gate_up(i):
                e, m = i // FM, i % FM
                dve.wait_ge(wg_hi, i + 1)
                tt(wgl[i % 2][:, :, :, :], egu[e % EBUF][:, :, :, m, :], wgh[i % 2][:, :, :, :].bitcast(F32),
                   ALU.subtract).then_inc(wg_lo, 1)

            def split_down(i):
                e, m = i // FM, i % FM
                dve.wait_ge(wd_hi, i + 1)
                tt(wdl[i % 2][:, :], edn[e % EBUF][:, m, :], wdh[i % 2][:, :].bitcast(F32), ALU.subtract).then_inc(wd_lo, 1)

            def weight_sum(i):
                dve.wait_ge(ld_f[i], 16)
                nc.vector.tensor_reduce(wcol[:, i:i + 1], fw[:, :], AX.X, ALU.add, apply_absolute_value=True)\
                  .then_inc(w_abs, 1)

            def weight_mean(i):
                dve.wait_ge(w_mean, i + 1)
                step(ts(wmean[:, i:i + 1], wsum[:, i:i + 1], 1.0 / (F1 * D), Q_EPS, ALU.mult, ALU.max))
                nc.vector.reciprocal(winv[:, i:i + 1], wmean[:, i:i + 1]).then_inc(w_quant, 2)

            for e in range(1, NE, 2):
                dve.wait_ge(sc_spread, e + 1)
                nc.vector.tensor_copy(scB[:, e, :].rearrange("p (n q) -> p n q", n=2), ps[:, 6:8, 0:HT])\
                  .then_inc(sc_spread_kept_v, 1)
            for i in range(2):
                split_gate_up(i)
                split_down(i)
            for k in range(ITEMS):
                e, n = k // (2 * FM), k % 2
                if k in SUM_ITEM:
                    weight_sum(SUM_ITEM.index(k))
                if k - 2 in SUM_ITEM:
                    weight_mean(SUM_ITEM.index(k - 2))
                if e == 0:
                    up = ps[:, 6 + n, 0:HT]
                else:
                    sc, up = scB[:, e - 1, HT * n:HT * n + HT], hf[:, :]
                    dve.wait_ge(gu_done, k + 1)
                    tt(gs[n][:, :], ps[:, 4 + n, 0:HT], sc, ALU.mult).then_inc(gs_ready, 1)
                    dve.wait_ge(hl_ready, k)
                    step(tt(hf[:, :], ps[:, 6 + n, 0:HT], sc, ALU.mult))
                dve.wait_ge(silu_done, k + 1)
                if k and e == 0:
                    dve.wait_ge(hl_ready, k)
                tt(hf[:, :], sg[n][:, :], up, ALU.mult).then_inc(hf_ready, 1)
                i = split_slot(k)
                if i is not None:
                    (split_down if k % 2 else split_gate_up)(i)
                dve.wait_ge(hh_ready, k + 1)
                tt(hl[k % 3][:, :], hf[:, :], hh[k % 3][:, :].bitcast(F32), ALU.subtract).then_inc(hl_ready, 1)
            for n in range(2):
                dve.wait_ge(down_done, ITEMS - 1 + n)
                nc.vector.tensor_copy(yT[:, 1, HT * n:HT * n + HT], ps[:, 2 + n, 0:HT]).then_inc(y_kept_v, 1)
            for b in range(B):
                dve.wait_ge(y_turned, b + 1)
                tt(x_sb[:, b, :], x_sb[:, b, :], ps[0:S, 4 + b % 4, 0:D], ALU.add).then_inc(x2_ready, 1)
                dve.wait_ge(x2_ready, b + 1)
                last = nc.vector.bn_stats(stats[:, b, :], x_sb[:, b, :])
            step(last)
            for b in range(B):
                last = nc.vector.bn_aggr(mv[:, b, :], stats[:, b, :])
            step(last)
            ts(veps[:, :], mv[:, :, 1], LN_EPS, None, ALU.add).then_inc(var3_ready, 1)
            dve.wait_ge(rstd3_ready, 1)

            def norm_x3(b):
                if b:
                    dve.wait_ge(x3_turned, b)
                ts(xn3[:, :], x_sb[:, b, :], mv[:, b, 0:1], rstd[:, b:b + 1], ALU.subtract, ALU.mult).then_inc(xn3_ready, 1)

            def rope(b, g):
                k = NG * b + g
                dve.wait_ge(qbig_done, k + 1)
                if k >= 2:
                    dve.wait_ge(q_done, k - 1)
                o = xyz[k % 2]
                for j in range(2):
                    tt(o[:, j, :, :], ps[:, 4, 0:HT].rearrange("p (i q) -> p i q", i=HG),
                       ropeq[:, j, :].unsqueeze(1).to_broadcast([128, HG, S]), ALU.mult)
                for j in range(2):
                    for a in range(2):
                        last = tt(o[CD * j:CD * j + CD, 2, a:HG:2, :],
                                  ps[CD * a:CD * a + CD, 5, 0:HT // 2].rearrange("p (i q) -> p i q", i=HG // 2),
                                  ropeq[CD * a:CD * a + CD, 2 + j, :].unsqueeze(1).to_broadcast([CD, HG // 2, S]), ALU.mult)
                last.then_inc(rope_done, 1)

            def low_q(b, g):
                k = NG * b + g
                cols = slice(HT * g, HT * g + HT)
                dve.wait_ge(q_hi, k + 1)
                tt(ql[b % 2][0:CD, cols], ps[0:CD, 6, 0:HT], qh[b % 2][0:CD, cols].bitcast(F32), ALU.subtract).then_inc(q_lo, 1)

            def reduce_max(b, i):
                w = m_rows(i)
                if i == 0 and b:
                    dve.wait_ge(max_ready, b)
                for n in range(3):
                    dve.wait_ge(m_done, 3 * (MT * b + i) + n + 1)
                    nc.vector.tensor_reduce(nm3[0:w, i, n:n + 1], ps[0:w, max_bank(b, i) + n, 0:MN], AX.X, ALU.max)\
                      .then_inc(m_reduced, 1)

            def join_max(b):
                dve.wait_ge(m_reduced, 3 * MT * (b + 1))
                if b >= 2:
                    dve.wait_ge(m_turned, b - 1)
                nc.vector.tensor_reduce(nmx[b % 2][:, :], nm3[:, :, :], AX.X, ALU.max, negate=True).then_inc(max_ready, 1)

            def invert_sums(q):
                dve.wait_ge(sums_turned, q + 1)
                if q >= 2:
                    dve.wait_ge(sum_spread, q - 1)
                nc.vector.reciprocal(inv[q % 2][:, :], ps[0:S, 7, 0:HG]).then_inc(sums_inverted, 1)

            def divide(q):
                dve.wait_ge(sum_spread, q + 1)
                dve.wait_ge(c_kept, q + 1)
                if q >= NG and q % NG == 0:
                    dve.wait_ge(o_done, q // NG)
                a = q % NG // 2
                p, cols = slice(CD * a, CD * a + CD), slice(HT * (q % 2), HT * (q % 2) + HT)
                tt(ct[p, cols], ctu[p, cols], ps[p, 7, 0:HT], ALU.mult).then_inc(c_ready, 1)

            def residual(b):
                dve.wait_ge(o_done, b + 1)
                tt(x_sb[:, b, :], x_sb[:, b, :], ps[0:S, 6, 0:D], ALU.add).then_inc(x3_ready, 1)
                dve.wait_ge(x3_ready, b + 1)
                step(nc.vector.bn_stats(stats4[:, :], x_sb[:, b, :]))
                step(nc.vector.bn_aggr(mv4[:, :], stats4[:, :]))
                ts(veps4[:, :], mv4[:, 1:2], LN_EPS, None, ALU.add).then_inc(var4_ready, 1)

            def quantise_x(b):
                dve.wait_ge(rstd4_ready, b + 1)
                if b:
                    dve.wait_ge(xq_turned, b)
                    dve.wait_ge(silu1_done, b)
                step(ts(xn4[:, :], x_sb[:, b, :], mv4[:, 0:1], rstd4[:, 0:1], ALU.subtract, ALU.mult))
                step(nc.vector.tensor_reduce(qsc[:, 4:5], xn4[:, :], AX.X, ALU.max, apply_absolute_value=True))
                step(ts(qsc[:, 4:5], qsc[:, 4:5], Q_EPS, None, ALU.max))
                step(nc.vector.reciprocal(qsc[:, 5:6], qsc[:, 4:5]))
                step(ts(qsc[:, 5:6], qsc[:, 5:6], Q_MAX, None, ALU.mult))
                step(ts(xn4[:, :], xn4[:, :], qsc[:, 5:6], ROUND, ALU.mult, ALU.add))
                ts(qsc[:, 2:3], qsc[:, 4:5], 1.0 / Q_MAX, wmean[0:S, 0:1], ALU.mult, ALU.mult)
                ts(qsc[:, 3:4], qsc[:, 4:5], 1.0 / Q_MAX, wmean[0:S, 1:2], ALU.mult, ALU.mult)
                ts(xq[:, :], xn4[:, :], ROUND, Q_MAX, ALU.subtract, ALU.min).then_inc(xq_ready, 1)

            def hidden(b, half):
                dve.wait_ge(silu1_done, b + 1)
                dve.wait_ge(u_done, 2 * b + half + 1)
                cols = slice(512 * half, 512 * half + 512)
                stt(h1[:, cols], ps[0:S, 4, :], qsc[:, 3:4], sg1[:, cols], ALU.mult, ALU.mult).then_inc(h1_part, 1)

            def hidden_norm(b):
                dve.wait_ge(h1_square, b + 1)
                ts(vh[:, :], ssq[:, 0:1], 1.0 / F1, RMS_EPS, ALU.mult, ALU.add).then_inc(varh_ready, 1)

            def quantise_h(b, part):
                if part == 0:
                    dve.wait_ge(rstdh_ready, b + 1)
                    step(stt(h1[:, :], h1[:, :], rstdh[:, 0:1], lnw_b[:, :], ALU.mult, ALU.mult))
                elif part == 1:
                    step(nc.vector.tensor_reduce(qsc[:, 6:7], h1[:, :], AX.X, ALU.max, apply_absolute_value=True))
                    step(ts(qsc[:, 6:7], qsc[:, 6:7], Q_EPS, None, ALU.max))
                    step(nc.vector.reciprocal(qsc[:, 7:8], qsc[:, 6:7]))
                    step(ts(qsc[:, 7:8], qsc[:, 7:8], Q_MAX, None, ALU.mult))
                    step(ts(qsc[:, 0:1], qsc[:, 6:7], 1.0 / Q_MAX, wmean[0:S, 2:3], ALU.mult, ALU.mult))
                elif part == 2:
                    step(ts(h1[:, :], h1[:, :], qsc[:, 7:8], ROUND, ALU.mult, ALU.add))
                else:
                    if b:
                        dve.wait_ge(hq_turned, b)
                    ts(hq[:, :], h1[:, :], ROUND, Q_MAX, ALU.subtract, ALU.min).then_inc(hq_ready, 1)

            def result(b):
                dve.wait_ge(down1_done, b + 1)
                if b >= 2:
                    dve.wait_ge(y_stored[b % 2], 16 * (b // 2))
                stt(y[b % 2][:, :], ps[0:S, 5, 0:D], qsc[:, 0:1], x_sb[:, b, :], ALU.mult, ALU.add).then_inc(y_ready, 1)

            norm_x3(0)
            dve.wait_ge(ld_const, 16)
            dve.wait_ge(ld_lnw, 16)
            rope(0, 0)
            rope(0, 1)
            low_q(0, 0)
            dve.wait_ge(tails_set, 2)
            rope(0, 2)
            reduce_max(0, 0)
            low_q(0, 1)
            reduce_max(0, 1)
            rope(0, 3)
            reduce_max(0, 2)
            low_q(0, 2)
            reduce_max(0, 3)
            low_q(0, 3)
            for i in range(EARLY, MT):
                reduce_max(0, i)
            join_max(0)
            norm_x3(1)
            for b in range(B):
                for s in range(SLOTS):
                    if (b or s >= KT) and s % KT == TURN_AT:
                        invert_sums(NG * b + s // KT - 1)
                    if (b or s >= KT) and s % KT == SPREAD_AT:
                        divide(NG * b + s // KT - 1)
                    if b + 1 < B:
                        if s in BIG_SLOT:
                            rope(b + 1, BIG_SLOT.index(s))
                        if s in LAT_SLOT:
                            low_q(b + 1, LAT_SLOT.index(s))
                    if b:
                        if s == OUT_SLOT:
                            residual(b - 1)
                        if s == LAT_SLOT[-1]:
                            quantise_x(b - 1)
                        if s in GU_SLOT:
                            hidden(b - 1, GU_SLOT.index(s))
                        if s == SQ_SLOT:
                            hidden_norm(b - 1)
                        if s in QH_SLOT:
                            quantise_h(b - 1, QH_SLOT.index(s))
                        if s == DOWN_SLOT:
                            result(b - 1)
                    if b + 1 < B and s in M_SLOT:
                        reduce_max(b + 1, M_SLOT.index(s))
                        if s == M_SLOT[-1]:
                            join_max(b + 1)
                    if s == MX_SLOT and b + 2 < B:
                        norm_x3(b + 2)
            invert_sums(NG * B - 1)
            divide(NG * B - 1)
            residual(B - 1)
            quantise_x(B - 1)
            hidden(B - 1, 0)
            hidden(B - 1, 1)
            hidden_norm(B - 1)
            for part in range(4):
                quantise_h(B - 1, part)
            result(B - 1)


def rope_tables():
    import numpy as np

    def table(length, dim):
        inv = (np.float32(1.0) / np.power(np.float32(10000.0), np.arange(0, dim, 2, dtype=np.float32) / np.float32(dim))).astype(np.float32)
        f = np.arange(length, dtype=np.float32)[:, None] * inv[None, :]
        return np.repeat(np.sin(f), 2, axis=-1), np.repeat(np.cos(f), 2, axis=-1)

    half = QB // 2
    sin_q, cos_q = table(S, QB)
    turned = np.concatenate([sin_q[:, half:], -sin_q[:, :half]], axis=1)
    rope_q = np.zeros((128, 4, S), np.float32)
    rope_q[:, 0] = cos_q[:, 0:128].T
    rope_q[:, 1] = turned[:, 0:128].T
    rope_q[:, 2] = np.tile(cos_q[:, 128:QB].T, (2, 1))
    rope_q[:, 3] = np.tile(turned[:, 128:QB].T, (2, 1))
    sin_k, cos_k = table(LC, CD)
    sin_k = np.concatenate([-sin_k[:, :CD // 2], sin_k[:, CD // 2:]], axis=1)
    return rope_q, np.ascontiguousarray(cos_k), np.ascontiguousarray(sin_k)


_INS = ['x', 'ctx_512', 'L0_xattn_Wq', 'L0_xattn_Wkv_expand', 'L0_xattn_Wout', 'L0_ffn_router_w',
        'L0_ffn_gate_up_proj', 'L0_ffn_down_proj', 'L0_ffn_shared_gate_w', 'L0_ffn_shared_up_w',
        'L0_ffn_shared_down_w', 'L1_xattn_Wq', 'L1_xattn_w_kc_q', 'L1_xattn_w_kc_kv', 'L1_xattn_W_qr',
        'L1_xattn_W_kr', 'L1_xattn_Wo', 'L1_ffn_w_gate', 'L1_ffn_w_up', 'L1_ffn_w_down', 'L1_ffn_ln_weight']


def kernel(**inputs):
    import numpy as _np
    import concourse.bacc as _bacc
    from concourse import mybir as _mybir
    from concourse.bass_utils import run_bass_kernel_spmd as _run

    nc = _bacc.Bacc("TRN2", target_bir_lowering=False, num_devices=1)
    arrays, args = {}, []
    tables = dict(zip(("rope_q", "rope_kc", "rope_ks"), rope_tables()))
    for name in _INS + list(tables):
        a = _np.ascontiguousarray(tables[name] if name in tables else inputs[name])
        arrays[f"in_{name}_dram"] = a
        args.append(nc.dram_tensor(f"in_{name}_dram", a.shape, _mybir.dt.from_np(a.dtype), kind="ExternalInput").ap())
    args.append(nc.dram_tensor("out_0_dram", (B, S, D), F32, kind="ExternalOutput").ap())
    build(nc, *args)
    r = _run(nc, [arrays], core_ids=[0])
    return r.results[0]["out_0_dram"]
```
